# Optimizing a Trainium2 kernel written in Bass

```python
import numpy as np
import jax
import jax.numpy as jnp

def _softmax(x, axis=-1):
    return jax.nn.softmax(x, axis=axis)

def _gelu(x):
    return jax.nn.gelu(x, approximate=True)

def _silu(x):
    return jax.nn.silu(x)

def _sigmoid(x):
    return jax.nn.sigmoid(x)

def _layernorm(x, axis=-1, eps=1e-05):
    m = jnp.mean(x, axis=axis, keepdims=True)
    v = jnp.var(x, axis=axis, keepdims=True)
    return (x - m) / jnp.sqrt(v + eps)

def _scatter_add(tgt, idx, src, axis=0):
    return tgt.at[idx].add(src)

def _segment_sum(src, seg, n):
    return jax.ops.segment_sum(src, seg, n)
kernel_name = 'mk_gps_d2_gnn_r32_b9105f'

def setup_inputs(seed: int=0):
    np.random.seed(seed)
    _w = jnp.asarray

    def _rec_inputs():
        import jax
        import jax.numpy as jnp
        _gk = jax.random.key(seed)
        x = -0.0002117 + 1 * jax.random.normal(jax.random.fold_in(_gk, 1), (3125, 256), jnp.float32)
        src = jax.random.randint(jax.random.fold_in(_gk, 2), (50000,), 0, 3125, jnp.int32)
        dst = jnp.minimum((3125 * jax.random.uniform(jax.random.fold_in(_gk, 3), (50000,)) ** 2.0).astype(jnp.int32), 99999)
        _o = jnp.argsort(dst, stable=True)
        src = src[_o]
        dst = dst[_o]
        return (x, src, dst)
    x, src, dst = _rec_inputs()

    def _L0_gnn_setup():
        import jax, jax.numpy as jnp
        import numpy as np
        N = 3125
        E = 50000
        IN_FEATS = 256
        OUT_FEATS = 256
        MAXK = 32

        def _maxk(x, k):
            _, idx = jax.lax.top_k(x, k)
            rows = jnp.arange(x.shape[0])[:, None]
            mask = jnp.zeros_like(x).at[rows, idx].set(1.0)
            return x * mask
        key = jax.random.key(seed)
        k1, k2, k3, k4, k5 = jax.random.split(key, 5)
        feat = jax.random.normal(k1, (N, IN_FEATS), dtype=jnp.float32)
        W_self = jax.random.normal(k2, (IN_FEATS, OUT_FEATS), dtype=jnp.float32) * (1.0 / np.sqrt(IN_FEATS))
        W_neigh = jax.random.normal(k3, (IN_FEATS, OUT_FEATS), dtype=jnp.float32) * (1.0 / np.sqrt(IN_FEATS))
        src = jax.random.randint(k4, (E,), 0, N, dtype=jnp.int64)
        dst = jax.random.randint(k5, (E,), 0, N, dtype=jnp.int64)
        return {'feat': feat, 'W_self': W_self, 'W_neigh': W_neigh, 'src': src, 'dst': dst}
    _L0_gnn_all = _L0_gnn_setup()
    _L0_gnn_in = {k: v for k, v in _L0_gnn_all.items() if k in ('W_self', 'W_neigh')}
    del _L0_gnn_all

    def _L0_mix_setup():
        import jax, jax.numpy as jnp
        import numpy as np
        N, F, C, H = (32, 128, 256, 8)
        D = C // H
        EPS_ATTN = 1e-06
        EPS_LN = 1e-05

        def layer_norm(x, g, b):
            mu = jnp.mean(x, axis=-1, keepdims=True)
            var = jnp.var(x, axis=-1, keepdims=True)
            return (x - mu) * jax.lax.rsqrt(var + EPS_LN) * g + b
        key = jax.random.key(seed)
        ks = jax.random.split(key, 8)
        s = 1.0 / np.sqrt(C)
        return {'x': jax.random.normal(ks[0], (N, F, C), jnp.float32), 'Wqkv': jax.random.uniform(ks[1], (3 * C, C), jnp.float32, -s, s), 'ln1_g': jnp.ones((C,), jnp.float32), 'ln1_b': jnp.zeros((C,), jnp.float32), 'W1': jax.random.uniform(ks[2], (C, C), jnp.float32, -s, s), 'b1': jax.random.uniform(ks[3], (C,), jnp.float32, -s, s), 'W2': jax.random.uniform(ks[4], (C, C), jnp.float32, -s, s), 'b2': jax.random.uniform(ks[5], (C,), jnp.float32, -s, s), 'ln2_g': jnp.ones((C,), jnp.float32), 'ln2_b': jnp.zeros((C,), jnp.float32)}
    _L0_mix_all = _L0_mix_setup()
    _L0_mix_in = {k: v for k, v in _L0_mix_all.items() if k in ('Wqkv', 'ln1_g', 'ln1_b', 'W1', 'b1', 'W2', 'b2', 'ln2_g', 'ln2_b')}
    del _L0_mix_all

    def _L0_ffn_setup():
        import jax, jax.numpy as jnp
        import numpy as np
        B, K, D = (512, 16, 256)
        E = 32
        H = int(D * 0.25)
        key = jax.random.key(seed)
        ks = jax.random.split(key, 7)
        d_rs = D ** (-0.5)
        h_rs = H ** (-0.5)
        x = jax.random.normal(ks[0], (B, K, D), dtype=jnp.float32)
        router_w = jax.random.uniform(ks[1], (E, D), jnp.float32, -d_rs, d_rs)
        router_b = jax.random.uniform(ks[2], (E,), jnp.float32, -d_rs, d_rs)
        W1 = jax.random.uniform(ks[3], (E, D, H), jnp.float32, -h_rs, h_rs)
        b1 = jax.random.uniform(ks[4], (E, H), jnp.float32, -h_rs, h_rs)
        W2 = jax.random.uniform(ks[5], (E, H, D), jnp.float32, -d_rs, d_rs)
        b2 = jax.random.uniform(ks[6], (E, D), jnp.float32, -d_rs, d_rs)
        return {'x': x, 'router_w': router_w, 'router_b': router_b, 'W1': W1, 'b1': b1, 'W2': W2, 'b2': b2}
    _L0_ffn_all = _L0_ffn_setup()
    _L0_ffn_in = {k: v for k, v in _L0_ffn_all.items() if k in ('router_w', 'router_b', 'W1', 'b1', 'W2', 'b2')}
    del _L0_ffn_all

    def _L1_gnn_setup():
        import jax, jax.numpy as jnp
        import numpy as np
        N_NODES = 50000
        N_EDGES = 25000
        D_IN = 256
        D_OUT = 256
        key = jax.random.key(seed)
        k1, k2, k3, k4 = jax.random.split(key, 4)
        x = jax.random.normal(k1, (N_NODES, D_IN), dtype=jnp.float32)
        edge_index = jax.random.randint(k2, (2, N_EDGES), 0, N_NODES, dtype=jnp.int64)
        W = jax.random.normal(k3, (D_OUT, D_IN), dtype=jnp.float32) * (1.0 / np.sqrt(D_IN))
        b = jax.random.normal(k4, (D_OUT,), dtype=jnp.float32) * 0.01
        return {'x': x, 'edge_index': edge_index, 'W': W, 'b': b}
    _L1_gnn_all = _L1_gnn_setup()
    _L1_gnn_in = {k: v for k, v in _L1_gnn_all.items() if k in ('W', 'b')}
    del _L1_gnn_all

    def _L1_mix_setup():
        import jax, jax.numpy as jnp
        import numpy as np
        NUM_HEADS = 8
        key = jax.random.key(seed)
        ks = jax.random.split(key, 5)
        B, N, C = (8, 512, 256)
        x = jax.random.normal(ks[0], (B, N, C), dtype=jnp.float32)
        Wq = jax.random.normal(ks[1], (C, C), dtype=jnp.float32) * 0.02
        Wkv = jax.random.normal(ks[2], (2 * C, C), dtype=jnp.float32) * 0.02
        Wproj = jax.random.normal(ks[3], (C, C), dtype=jnp.float32) * 0.02
        bproj = jnp.zeros((C,), dtype=jnp.float32)
        return {'x': x, 'Wq': Wq, 'Wkv': Wkv, 'Wproj': Wproj, 'bproj': bproj}
    _L1_mix_all = _L1_mix_setup()
    _L1_mix_in = {k: v for k, v in _L1_mix_all.items() if k in ('Wq', 'Wkv', 'Wproj', 'bproj')}
    del _L1_mix_all

    def _L1_ffn_setup():
        import math
        import jax, jax.numpy as jnp
        import numpy as np
        CAPACITY_FACTOR = 1.25
        key = jax.random.key(seed)
        ks = jax.random.split(key, 5)
        B, L, D, F, E = (8, 256, 256, 1024, 8)
        h = jax.random.normal(ks[0], (B, L, D), dtype=jnp.float32)
        gate_w = jax.random.normal(ks[1], (D, E), dtype=jnp.float32) * 0.02
        gate_b = jnp.zeros((E,), dtype=jnp.float32)
        w1 = jax.random.normal(ks[2], (E, D, F), dtype=jnp.float32) * (1.0 / math.sqrt(D))
        b1 = jnp.zeros((E, F), dtype=jnp.float32)
        w2 = jax.random.normal(ks[3], (E, F, D), dtype=jnp.float32) * (1.0 / math.sqrt(F))
        b2 = jnp.zeros((E, D), dtype=jnp.float32)
        return {'h': h, 'gate_w': gate_w, 'gate_b': gate_b, 'w1': w1, 'b1': b1, 'w2': w2, 'b2': b2}
    _L1_ffn_all = _L1_ffn_setup()
    _L1_ffn_in = {k: v for k, v in _L1_ffn_all.items() if k in ('gate_w', 'gate_b', 'w1', 'b1', 'w2', 'b2')}
    del _L1_ffn_all
    return {'x': x, 'src': src, 'dst': dst, 'L0_gnn_W_self': _L0_gnn_in['W_self'], 'L0_gnn_W_neigh': _L0_gnn_in['W_neigh'], 'L0_mix_Wqkv': _L0_mix_in['Wqkv'], 'L0_mix_ln1_g': _L0_mix_in['ln1_g'], 'L0_mix_ln1_b': _L0_mix_in['ln1_b'], 'L0_mix_W1': _L0_mix_in['W1'], 'L0_mix_b1': _L0_mix_in['b1'], 'L0_mix_W2': _L0_mix_in['W2'], 'L0_mix_b2': _L0_mix_in['b2'], 'L0_mix_ln2_g': _L0_mix_in['ln2_g'], 'L0_mix_ln2_b': _L0_mix_in['ln2_b'], 'L0_ffn_router_w': _L0_ffn_in['router_w'], 'L0_ffn_router_b': _L0_ffn_in['router_b'], 'L0_ffn_W1': _L0_ffn_in['W1'], 'L0_ffn_b1': _L0_ffn_in['b1'], 'L0_ffn_W2': _L0_ffn_in['W2'], 'L0_ffn_b2': _L0_ffn_in['b2'], 'L1_gnn_W': _L1_gnn_in['W'], 'L1_gnn_b': _L1_gnn_in['b'], 'L1_mix_Wq': _L1_mix_in['Wq'], 'L1_mix_Wkv': _L1_mix_in['Wkv'], 'L1_mix_Wproj': _L1_mix_in['Wproj'], 'L1_mix_bproj': _L1_mix_in['bproj'], 'L1_ffn_gate_w': _L1_ffn_in['gate_w'], 'L1_ffn_gate_b': _L1_ffn_in['gate_b'], 'L1_ffn_w1': _L1_ffn_in['w1'], 'L1_ffn_b1': _L1_ffn_in['b1'], 'L1_ffn_w2': _L1_ffn_in['w2'], 'L1_ffn_b2': _L1_ffn_in['b2']}

def reference(x, src, dst, L0_gnn_W_self, L0_gnn_W_neigh, L0_mix_Wqkv, L0_mix_ln1_g, L0_mix_ln1_b, L0_mix_W1, L0_mix_b1, L0_mix_W2, L0_mix_b2, L0_mix_ln2_g, L0_mix_ln2_b, L0_ffn_router_w, L0_ffn_router_b, L0_ffn_W1, L0_ffn_b1, L0_ffn_W2, L0_ffn_b2, L1_gnn_W, L1_gnn_b, L1_mix_Wq, L1_mix_Wkv, L1_mix_Wproj, L1_mix_bproj, L1_ffn_gate_w, L1_ffn_gate_b, L1_ffn_w1, L1_ffn_b1, L1_ffn_w2, L1_ffn_b2):
    import jax
    import jax.numpy as jnp

    def _L0_gnn_ref(feat, W_self, W_neigh, src, dst):
        import jax, jax.numpy as jnp
        import numpy as np
        N = 3125
        E = 50000
        IN_FEATS = 256
        OUT_FEATS = 256
        MAXK = 32

        def _maxk(x, k):
            _, idx = jax.lax.top_k(x, k)
            rows = jnp.arange(x.shape[0])[:, None]
            mask = jnp.zeros_like(x).at[rows, idx].set(1.0)
            return x * mask
        n = feat.shape[0]
        h_self = feat @ W_self
        h_neigh = feat @ W_neigh
        h_sparse = _maxk(h_neigh, MAXK)
        msg = h_sparse[src]
        summed = jax.ops.segment_sum(msg, dst, num_segments=n)
        deg = jax.ops.segment_sum(jnp.ones((src.shape[0],), dtype=feat.dtype), dst, num_segments=n)
        neigh = summed / jnp.maximum(deg, 1.0)[:, None]
        return h_self + neigh

    def _L0_mix_ref(x, Wqkv, ln1_g, ln1_b, W1, b1, W2, b2, ln2_g, ln2_b):
        import jax, jax.numpy as jnp
        import numpy as np
        N, F, C, H = (32, 128, 256, 8)
        D = C // H
        EPS_ATTN = 1e-06
        EPS_LN = 1e-05

        def layer_norm(x, g, b):
            mu = jnp.mean(x, axis=-1, keepdims=True)
            var = jnp.var(x, axis=-1, keepdims=True)
            return (x - mu) * jax.lax.rsqrt(var + EPS_LN) * g + b
        n, f, c = x.shape
        qkv = jnp.einsum('nfc,oc->nfo', x, Wqkv)
        q, k, v = jnp.split(qkv, 3, axis=-1)
        q = q.reshape(n, f, H, D)
        k = k.reshape(n, f, H, D)
        v = v.reshape(n, f, H, D)
        q = jax.nn.elu(q) + 1.0
        k = jax.nn.elu(k) + 1.0
        kv = jnp.einsum('nshd,nshm->nhmd', k, v)
        ksum = jnp.sum(k, axis=1)
        z = 1.0 / (jnp.einsum('nlhd,nhd->nlh', q, ksum) + EPS_ATTN)
        t = jnp.einsum('nlhd,nhmd,nlh->nlhm', q, kv, z)
        t = t.reshape(n, f, c)
        x1 = layer_norm(t + x, ln1_g, ln1_b)
        h = jax.nn.gelu(jnp.einsum('nfc,oc->nfo', x1, W1) + b1, approximate=False)
        y = jnp.einsum('nfc,oc->nfo', h, W2) + b2
        return layer_norm(y + x1, ln2_g, ln2_b)

    def _L0_ffn_ref(x, router_w, router_b, W1, b1, W2, b2):
        import jax, jax.numpy as jnp
        import numpy as np
        B, K, D = (512, 16, 256)
        E = 32
        H = int(D * 0.25)
        xf = x.reshape(-1, D)
        logits = xf @ router_w.T + router_b
        idx = jnp.argmax(logits, axis=-1)
        w1t = jnp.take(W1, idx, axis=0)
        h = jnp.einsum('nd,ndh->nh', xf, w1t) + jnp.take(b1, idx, axis=0)
        h = jax.nn.relu(h)
        w2t = jnp.take(W2, idx, axis=0)
        out = jnp.einsum('nh,nhd->nd', h, w2t) + jnp.take(b2, idx, axis=0)
        out = jax.nn.relu(out)
        return out.reshape(x.shape)

    def _L1_gnn_ref(x, edge_index, W, b):
        import jax, jax.numpy as jnp
        import numpy as np
        N_NODES = 50000
        N_EDGES = 25000
        D_IN = 256
        D_OUT = 256
        N = x.shape[0]
        loop = jnp.arange(N, dtype=edge_index.dtype)
        row = jnp.concatenate([edge_index[0], loop])
        col = jnp.concatenate([edge_index[1], loop])
        ew = jnp.ones(row.shape[0], dtype=x.dtype)
        deg = jax.ops.segment_sum(ew, col, num_segments=N)
        dinv = jnp.where(deg > 0, jax.lax.rsqrt(deg), jnp.zeros_like(deg))
        norm = dinv[row] * dinv[col]
        msg = x[row] * norm[:, None]
        agg = jax.ops.segment_sum(msg, col, num_segments=N)
        return agg @ W.T + b

    def _L1_mix_ref(x, Wq, Wkv, Wproj, bproj):
        import jax, jax.numpy as jnp
        import numpy as np
        NUM_HEADS = 8
        B, N, C = x.shape
        h = NUM_HEADS
        d = C // h
        q = jnp.einsum('bnc,oc->bno', x, Wq).reshape(B, N, h, d).transpose(0, 2, 1, 3)
        kv = jnp.einsum('bnc,oc->bno', x, Wkv).reshape(B, N, 2, h, d)
        k = kv[:, :, 0].transpose(0, 2, 1, 3)
        v = kv[:, :, 1].transpose(0, 2, 1, 3)
        q = jax.nn.elu(q) + 1.0
        k = jax.nn.elu(k) + 1.0
        k_sum = k.sum(axis=2)
        D_inv = 1.0 / jnp.maximum(jnp.einsum('bhnd,bhd->bhn', q, k_sum), 1e-06)
        context = jnp.einsum('bhnd,bhne->bhde', k, v)
        attn = jnp.einsum('bhnd,bhde->bhne', q, context) * D_inv[..., None]
        out = attn.transpose(0, 2, 1, 3).reshape(B, N, C)
        out = jnp.einsum('bnc,oc->bno', out, Wproj) + bproj
        return out

    def _L1_ffn_ref(h, gate_w, gate_b, w1, b1, w2, b2):
        import math
        import jax, jax.numpy as jnp
        import numpy as np
        CAPACITY_FACTOR = 1.25
        B, L, D = h.shape
        E = gate_w.shape[1]
        T = B * L
        C = max(1, math.ceil(CAPACITY_FACTOR * T / E))
        x = h.reshape(T, D)
        logits = x @ gate_w + gate_b
        probs = jax.nn.softmax(logits, axis=-1)
        idx = jnp.argmax(probs, axis=-1)
        prb = jnp.take_along_axis(probs, idx[:, None], axis=1)[:, 0]
        one_hot = jax.nn.one_hot(idx, E, dtype=jnp.float32)
        pos = (jnp.cumsum(one_hot, axis=0) * one_hot).sum(-1).astype(jnp.int32) - 1
        kept = pos < C
        pos_safe = jnp.where(kept, pos, C)
        buf = jnp.zeros((E, C, D), dtype=h.dtype).at[idx, pos_safe].set(x, mode='drop')
        hmid = jax.nn.relu(jnp.einsum('ecd,edf->ecf', buf, w1) + b1[:, None, :])
        ybuf = jnp.einsum('ecf,efd->ecd', hmid, w2) + b2[:, None, :]
        pos_g = jnp.minimum(pos, C - 1)
        y_tok = ybuf[idx, pos_g] * (prb * kept)[:, None]
        y = y_tok.reshape(B, L, D)
        y = jnp.nan_to_num(y, nan=0.0, posinf=10000.0, neginf=-10000.0)
        return y
    edge_index = jnp.stack([src, dst])
    xn = _layernorm(x, axis=-1)
    x = x + _L0_gnn_ref(xn, L0_gnn_W_self, L0_gnn_W_neigh, src, dst) + _L0_mix_ref(xn[None], L0_mix_Wqkv, L0_mix_ln1_g, L0_mix_ln1_b, L0_mix_W1, L0_mix_b1, L0_mix_W2, L0_mix_b2, L0_mix_ln2_g, L0_mix_ln2_b)[0]
    x = x + _L0_ffn_ref(_layernorm(x, axis=-1)[None], L0_ffn_router_w, L0_ffn_router_b, L0_ffn_W1, L0_ffn_b1, L0_ffn_W2, L0_ffn_b2)[0]
    xn = _layernorm(x, axis=-1)
    x = x + _L1_gnn_ref(xn, edge_index, L1_gnn_W, L1_gnn_b) + _L1_mix_ref(xn[None], L1_mix_Wq, L1_mix_Wkv, L1_mix_Wproj, L1_mix_bproj)[0]
    x = x + _L1_ffn_ref(_layernorm(x, axis=-1)[None], L1_ffn_gate_w, L1_ffn_gate_b, L1_ffn_w1, L1_ffn_b1, L1_ffn_w2, L1_ffn_b2)[0]
    return x

_drawn_inputs = setup_inputs


def setup_inputs(seed=0):
    import zlib

    import numpy as np

    out = dict(_drawn_inputs(seed))
    spreads = {'L0_mix_ln1_g': (1.0, 0.2),
     'L0_mix_ln1_b': (0.0, 0.1),
     'L0_mix_ln2_g': (1.0, 0.2),
     'L0_mix_ln2_b': (0.0, 0.1),
     'L1_mix_bproj': (0.0, 0.1),
     'L1_ffn_gate_b': (0.0, 0.1),
     'L1_ffn_b1': (0.0, 0.8),
     'L1_ffn_b2': (0.0, 0.8)}
    factors = {'L0_mix_Wqkv': 6.934,
     'L0_mix_b1': 5.978,
     'L0_mix_b2': 2.742,
     'L0_ffn_router_b': 2.813,
     'L0_ffn_b1': 8.0,
     'L0_ffn_b2': 4.682,
     'L1_gnn_b': 8.0,
     'L1_mix_Wq': 8.0,
     'L1_mix_Wkv': 8.0,
     'L1_mix_Wproj': 8.0}
    for name, (base, spread) in spreads.items():
        noise = np.random.default_rng([zlib.crc32(name.encode()), seed]).standard_normal(out[name].shape)
        drawn = base * np.exp(spread * noise) if base else spread * noise
        out[name] = jnp.asarray(drawn.astype(out[name].dtype))
    for name, factor in factors.items():
        out[name] = (out[name] * factor).astype(out[name].dtype)
    return out
```

```python
import numpy as np
import concourse.bass as bass
from concourse import mybir
from contextlib import ExitStack

F32 = mybir.dt.float32
I32 = mybir.dt.int32
U32 = mybir.dt.uint32
ALU = mybir.AluOpType
ACT = mybir.ActivationFunctionType
AX = mybir.AxisListType

P = 128
N = 3125
D = 256
KD = D // P
NT = -(-N // P)
TAIL = N - (NT - 1) * P
CT = 5
NC = NT // CT
CN = CT * P
HN = CN // 2
NP = NT * P
E = 50000
GT = 4
GE = GT * P
NG = -(-E // GE)
ET = NG * GT
R = 8
LAG = 2
SEG = -(-NG // NC)
MAXN = NG * NT + 2
H = 8
HD = D // H
HH = P // HD
E0, F0 = 32, 64
NB0 = N // P + E0
E1, F1 = 8, 1024
CAP = -(-5 * N // (4 * E1))
ST = -(-CAP // P)
STAIL = CAP - (ST - 1) * P
MT = F1 // P
XB1 = 4096
FAR = 1.0e6
SENT = -3.0e38
FMAX = 3.4028234e38
AP_ = D + 1


class Chain:

    def __init__(self, eng, sem, idle):
        self.eng, self.sem, self.idle = eng, sem, idle
        self.base, self.k, self.i, self.per = 0, 0, None, 0

    def loop(self, i, per):
        self.base += self.k
        self.i, self.per, self.k = i, per, 0

    def end(self, trips):
        assert self.k == self.per, (self.k, self.per)
        self.base += self.per * trips
        self.i, self.k = None, 0

    def link(self, ins):
        ins.then_inc(self.sem, 1)
        self.k += 1

    def join(self):
        if self.i is None:
            self.eng.wait_ge(self.sem, self.base + self.k)
        else:
            self.eng.wait_ge(self.sem, self.i * self.per + (self.base + self.k))
            self.eng.sem_inc(self.idle, 1)


def build(nc, a, out):
    ctx = ExitStack()
    with ctx:
        def sb(n, s, d=F32):
            return ctx.enter_context(nc.sbuf_tensor(n, s, d))

        def dr(n, s, d=F32):
            return nc.dram_tensor(n, s, d, kind="Internal").ap()

        xnT_d = dr("xnT_d", [P, KD, NP])
        table = [dr("table0", [NP, D]), dr("table1", [NP, D])]
        slots = [dr("slots0", [NB0 * P, D]), dr("slots1", [XB1, D])]
        yslots = [dr("yslots0", [NB0 * P, D]), dr("yslots1", [E1 * CAP, D])]

        X = sb("X", [P, NT, D])
        acc = sb("acc", [P, (NT + 1) * AP_])
        ring = sb("ring", [P, R * GT * AP_])
        iota = sb("iota", [P, (NT + 1) * P])
        TE = sb("TE", [P, 2 * CT * D])
        step = TE[0:NG, 0:MAXN]
        src = sb("src", [P, ET], I32)
        dst = sb("dst", [P, ET])
        stage = sb("stage", [P, R, GT], I32)
        g_row = sb("g_row", [1, MAXN], I32)
        w_row = sb("w_row", [1, MAXN + 1], I32)
        bi_row = sb("bi_row", [1, NG], I32)
        seg_row = sb("seg_row", [1, NC + 1], I32)
        dg = TE[0:NG, 0:GE].bitcast(I32)
        dn = TE[0:NG, GE:2 * GE].bitcast(I32)
        tri = sb("tri", [P, P])
        tris = sb("tris", [P, P])
        ident = sb("ident", [P, P])
        ones = sb("ones", [P, P])
        valid = sb("valid", [P, NT])
        eps = sb("eps", [P, 1])
        sm = sb("sm", [NG, 12])
        smi = sb("smi", [NG, 3], I32)
        lo0 = sb("lo0", [1, 1])
        oh = sb("oh", [P, GT, P])
        st = sb("st", [P, NT, 6])
        mv = sb("mv", [P, NT, 2])
        rs = sb("rs", [P, NT])
        nm = sb("nm", [P, NT])
        sd = sb("sd", [P, NT])
        deg = sb("deg", [P, NT])
        rdeg = sb("rdeg", [P, NT])
        dinv = sb("dinv", [P, NT])
        wn = sb("wn", [P, KD, D])
        ws = sb("ws", [P, KD, D])
        wqkv = sb("wqkv", [P, KD, 3 * D])
        wm1 = sb("wm1", [P, KD, D])
        wm2 = sb("wm2", [P, KD, D])
        lng = sb("lng", [P, 4, D])
        b1c = sb("b1c", [P, KD])
        brow = sb("brow", [1, 3, D])
        XN = sb("XN", [P, CT, D])
        xT = sb("xT", [P, KD, CN])
        Kb = sb("Kb", [P, CT, D])
        Vb = sb("Vb", [P, CT, 2, P + 1])
        tmp = TE[:, 0:CT * D].rearrange("p (j f) -> p j f", f=D)
        ex = TE[:, CT * D:].rearrange("p (j f) -> p j f", f=D)
        Hs = sb("Hs", [P, CT, D])
        Wk = sb("Wk", [P, CT, D])
        m8 = sb("m8", [P, CT, 8])
        KV = sb("KV", [P, 2, P + 1])
        KVb = sb("KVb", [P, 2, P + HH])
        KS = sb("KS", [P, 2, P])
        CTx = sb("CTx", [P, 2, P])
        Mx = sb("Mx", [P, 2, D])
        den = sb("den", [P, CT, 2, HH])
        rw = sb("rw", [P, KD, E0])
        gw = sb("gw", [P, KD, E1])
        rrow = sb("rrow", [1, E0 + E1])
        ps = ctx.enter_context(nc.psum_tensor("ps", [P, 8 * 512], F32))
        B = 512

        def bank(i, w=512, n=1):
            return ps[:, i * B:i * B + w * n]

        QT = Kb[:].rearrange("p j f -> p (j f)")
        X1 = Hs
        Z = Wk
        HT = Vb[:].rearrange("p j a f -> p (j a f)")[:, 0:KD * CN].rearrange("p (k n) -> p k n", k=KD)
        AG = XN
        XALL = acc[:, 0:NT * D].rearrange("p (t f) -> p t f", f=D)
        a3 = acc[:].rearrange("p (w f) -> p w f", f=AP_)
        ring4 = ring[:].rearrange("p (r j f) -> p r j f", r=R, f=AP_)
        o = [0]

        def take(n, v=None):
            r = ring[:, o[0]:o[0] + n]
            o[0] += n
            return r
        LG = take(NT * E0)
        OH = take(NT * E0)
        TT = take(NT * E0)
        IN = take(NT * E0)
        MSK = take(NT * E0)
        PR = take(NT * E0)
        mx = take(NT * 8)
        mi = take(NT * 8).bitcast(U32)
        mif = take(NT)
        rank = take(NT)
        pos = take(NT)
        kept = take(NT)
        wgt = take(NT)
        t25 = take(NT)
        se = take(NT)
        cntE = take(E0)
        nbE = take(E0)
        nbEi = take(E0).bitcast(I32)
        CE = take(E0)
        baseE = take(E0)
        ebc = take(NB0 * E0)
        ebf = take(NB0)
        sidx = sb("sidx", [P, NT], I32)
        gidx = sb("gidx", [P, NT], I32)
        ebi = sb("ebi", [1, NB0], I32)
        Q0 = 4
        o[0] = 0
        xb0 = XN[:, 0:Q0, :]
        xbT0 = xT[:].rearrange("p k n -> p (k n)")[:, 0:Q0 * D].rearrange("p (s k n) -> p s k n", s=Q0, k=KD)
        w10 = tmp[:].rearrange("p j f -> p (j f)")[:, 0:Q0 * KD * F0].rearrange("p (s k f) -> p s k f", s=Q0, k=KD)
        w20 = ex[:, 0:Q0, :]
        b10 = sb("b10", [F0, Q0])
        h0 = Hs[:].rearrange("p j f -> p (j f)")[:, 0:Q0 * P].rearrange("p (s n) -> p s n", s=Q0)
        y0 = Wk[:, 0:Q0, :]
        w11 = ring[:, 0:2 * KD * F1].rearrange("p (s k f) -> p s k f", s=2, k=KD)
        w21 = ring[:, 2 * KD * F1:4 * KD * F1].rearrange("p (s m f) -> p s m f", s=2, m=MT)
        h1 = acc[:, 0:MT * CAP].rearrange("p (m n) -> p m n", m=MT)
        xb1 = XN[:, 0:ST, :]
        xb1T = xT[:, :, 0:ST * P]
        y1 = Wk[:, 0:ST, :]
        b11 = sb("b11", [P, E1 * MT])
        b21 = sb("b21", [1, 2, D])
        rt = sb("rt", [P, 8, NT])

        S = {}
        names = """loaded xload consts made prepped ranked listed bounds idle_p idle_a idle_v idle_t idle_s
            dve_chain act_chain pool_chain landed oh_half half_used added agg_done stat stat_sd stat_done
            a_xn a_tr a_xT a_nb a_kvp a_hs a_e a_v a_k a_kv a_kvacc a_done a_sp a_xnT a_tab kv_ready ct_ps ct_sb m_ps m_ready
            b_xs b_q b_e b_u b_qt b_t b_z b_sd1 b_rs1 b_n1 b_x1 b_x1t b_x1T b_h b_g b_y b_z2 b_sd2 b_rs2 b_n2 b_done b_den b_qs
            layer_done c_ag c_tr c_aT c_y c_done deg_ready deg_sd
            r_xn r_tr r_xT r_lg r_lgs r_done r_xall oh_ready mass mass_used routed expd negm zeroed scattered gathered
            e_x e_w e_tr e_xT e_h e_hs e_y e_ys e_out e_done
            f_x f_w1 f_w2 f_b2 f_tr f_xT f_h f_hs f_y f_ys f_out f_hfree outp wload stagep""".split()
        for n in names:
            S[n] = ctx.enter_context(nc.semaphore(n))
        slot_in = [ctx.enter_context(nc.semaphore(f"slot_in{i}")) for i in range(R)]
        NLOAD = 0

        block = ctx.enter_context(nc.Block())

        def v5(L, c):
            return c + (NC * L + 1)

        loads = [(src[:], a["srcT"]), (oh[:].rearrange("p j n -> p (j n)")[:, 0:ET].bitcast(I32), a["dstT"]), (dg, a["dgrp"]), (dn, a["dnext"]),
                 (wn[:], a["wn"]), (ws[:], a["ws"]), (wqkv[:], a["wqkv0"]), (wm1[:], a["wm1"]), (wm2[:], a["wm2"]),
                 (lng[:], a["lng"]), (b1c[:], a["b1c"]), (brow[:, 0, :], a["mb2"]), (rw[:], a["rw"]), (gw[:], a["gw"]),
                 (rrow[:], a["rrow"]), (valid[:], a["valid"]), (b11[:], a["b11"]), (brow[:, 1:3, :], a["b1rows"])]

        @block.sync
        def _(sp):
            def held(sem, val):
                sp.wait_ge(S[sem], val)
                sp.sem_inc(S["idle_s"], 1)

            for d, s in loads:
                sp.dma_start(d, s).then_inc(S["loaded"], 16)
            sp.wait_ge(S["consts"], 9)
            for c in range(NC):
                last = c == NC - 1
                n = CT - 1 if last else CT
                sp.dma_start(X[:, c * CT:c * CT + n, :], a["x"][c * CN:c * CN + n * P, :].rearrange("(j p) f -> p j f", p=P)).then_inc(S["xload"], 16)
            sp.dma_start(X[0:TAIL, NT - 1, :], a["x"][(NT - 1) * P:N, :]).then_inc(S["xload"], 16)
            for L in range(2):
                rows = slots[L].shape[0]
                per = 1024
                z = slots[L].rearrange("(p r) f -> p (r f)", p=P)
                w = z.shape[1]
                for q in range(0, w, 2048):
                    sp.dma_start(z[:, q:q + 2048], acc[:, 0:2048]).then_inc(S["zeroed"], 16)

            for L in range(2):
                with sp.Fori(0, NC) as c:
                    held("a_xT", v5(L, c))
                    sp.dma_start(xnT_d[:, :, bass.ds(c * CN, CN)], xT[:]).then_inc(S["a_xnT"], 16)
                    held("a_sp", v5(L, c))
                    sp.dma_start(table[L][bass.ds(c * CN, CN), :].rearrange("(j p) f -> p j f", p=P), (Hs if L == 0 else Wk)[:]).then_inc(S["a_tab"], 16)
                if L == 1:
                    pass
                sp.wait_ge(S["a_xnT"], 16 * NC * (L + 1) + 16)
                sp.wait_ge(S["kv_ready"], L + 1)
                with sp.Fori(0, NC) as c:
                    held("b_done", c + (NC * L + 1))
                    sp.dma_start(xT[:], xnT_d[:, :, bass.ds(c * CN, CN)]).then_inc(S["b_xs"], 16)
                if L == 0:
                    sp.wait_ge(S["layer_done"], 1)
                    sp.dma_start(wn[:], a["wg1"]).then_inc(S["wload"], 16)
                    sp.dma_start(wqkv[:], a["wqkv1"]).then_inc(S["wload"], 16)
                    sp.dma_start(wm1[:], a["wproj"]).then_inc(S["wload"], 16)
                    sp.wait_ge(S["scattered"], 16 * NT)
                    with sp.Fori(0, NB0 // Q0) as i:
                        held("e_done", i + 1)
                        for s in range(Q0):
                            b = i * Q0 + s
                            e = sp.value_load(ebi[0:1, bass.ds(b, 1)], min_val=0, max_val=E0 - 1)
                            sp.dma_start(xb0[:, s, :], slots[0][bass.ds(b * P, P), :]).then_inc(S["e_x"], 16)
                            sp.dma_start(w10[:, s], a["e1"][bass.ds(e, 1), :, :].rearrange("e (k p) f -> p (e k) f", p=P)).then_inc(S["e_x"], 16)
                            sp.dma_start(b10[:, s:s + 1], a["eb1"][bass.ds(e, 1), :].rearrange("e f -> f e")).then_inc(S["e_x"], 16)
                            sp.dma_start(w20[0:F0 + 1, s, :], a["e2"][bass.ds(e, 1), :, :].rearrange("e k f -> k (e f)")).then_inc(S["e_x"], 16)
                        held("e_ys", i + 1)
                        sp.dma_start(yslots[0][bass.ds(i * Q0 * P, Q0 * P), :].rearrange("(s p) f -> p s f", p=P), y0).then_inc(S["e_out"], 16)
                else:
                    sp.wait_ge(S["scattered"], 32 * NT)
                    with sp.Fori(0, E1 // 2) as i:
                        for s in range(2):
                            e = i * 2 + s
                            held("f_ys", e + 1)
                            sp.dma_start(xb1[:, 0:ST - 1, :], slots[1][bass.ds(e * CAP, (ST - 1) * P), :].rearrange("(t p) f -> p t f", p=P)).then_inc(S["f_x"], 16)
                            sp.dma_start(xb1[0:STAIL, ST - 1, :], slots[1][bass.ds(e * CAP + (ST - 1) * P, STAIL), :]).then_inc(S["f_x"], 16)
                            sp.dma_start(w11[:, s], a["w1"][bass.ds(e, 1), :, :].rearrange("e (k p) f -> p (e k) f", p=P)).then_inc(S["f_x"], 16)
                            sp.dma_start(w21[:, s], a["w2"][bass.ds(e, 1), :, :].rearrange("e (m p) f -> p (e m) f", p=P)).then_inc(S["f_x"], 16)
                            sp.dma_start(b21[:, s, :], a["b2"][bass.ds(e, 1), :]).then_inc(S["f_x"], 16)
                            held("f_ys", e + 2)
                            sp.dma_start(yslots[1][bass.ds(e * CAP, (ST - 1) * P), :].rearrange("(t p) f -> p t f", p=P), y1[:, 0:ST - 1, :]).then_inc(S["f_out"], 16)
                            sp.dma_start(yslots[1][bass.ds(e * CAP + (ST - 1) * P, STAIL), :], y1[0:STAIL, ST - 1, :]).then_inc(S["f_out"], 16)
            for c in range(NC):
                n = CT - 1 if c == NC - 1 else CT
                sp.wait_ge(S["layer_done"], 3 + c)
                sp.dma_start(out[c * CN:c * CN + n * P, :].rearrange("(j p) f -> p j f", p=P), X[:, c * CT:c * CT + n, :]).then_inc(S["outp"], 16)
            sp.dma_start(out[(NT - 1) * P:N, :], X[0:TAIL, NT - 1, :]).then_inc(S["outp"], 16)
            sp.wait_ge(S["outp"], 16 * (NC + 1))

        @block.gpsimd
        def _(gp):
            gp.iota(iota[:], pattern=[[1, (NT + 1) * P]], base=0, channel_multiplier=0, allow_small_or_imprecise_dtypes=True).then_inc(S["consts"], 1)
            gp.memset(tri[:], 1.0).then_inc(S["consts"], 1)
            gp.memset(tris[:], 1.0).then_inc(S["consts"], 1)
            gp.memset(ident[:], 0.0).then_inc(S["consts"], 1)
            gp.memset(ones[:], 1.0).then_inc(S["consts"], 1)
            gp.memset(eps[:], 1e-5).then_inc(S["consts"], 1)
            gp.memset(X[:, NT - 1, :], 0.0).then_inc(S["consts"], 1)
            gp.memset(acc[:], 0.0).then_inc(S["consts"], 1)
            gp.memset(ring4[:, :, :, D:AP_], 1.0).then_inc(S["consts"], 1)
            gp.wait_ge(S["consts"], 9)
            gp.affine_select(out=tri[:], in_=tri[:], compare_op=ALU.is_ge, fill=0.0, base=0, pattern=[[1, P]], channel_multiplier=-1).then_inc(S["made"], 1)
            gp.affine_select(out=tris[:], in_=tris[:], compare_op=ALU.is_gt, fill=0.0, base=0, pattern=[[1, P]], channel_multiplier=-1).then_inc(S["made"], 1)
            gp.affine_select(out=ident[:], in_=ident[:], compare_op=ALU.not_equal, fill=1.0, base=0, pattern=[[-1, P]], channel_multiplier=1).then_inc(S["made"], 1)
            gp.wait_ge(S["loaded"], 16 * len(loads))
            gp.wait_ge(S["listed"], -(-MAXN // 512) + 1)

            for L in range(2):
                gp.wait_ge(S["a_tab"], 16 * NC * (L + 1) + 16)

                def fetch(g, b):
                    gp.tensor_copy(stage[:, b, :], src[:, bass.ds(g * GT, GT)]).then_inc(S["stagep"], 1)
                    gp.wait_ge(S["stagep"], g + (1 + NG * L))
                    gp.sem_inc(S["idle_p"], 1)
                    for j in range(GT):
                        gp.indirect_dma_start(ring4[:, b, j, 0:D], None, table[L], bass.IndirectOffsetOnAxis(ap=stage[:, b, j:j + 1], axis=0)).then_inc(slot_in[b], 16)

                def arrived(b, turn):
                    before = L * (NG // R + (1 if b < NG % R else 0))
                    gp.wait_ge(slot_in[b], (turn + (before + 1)) * (16 * GT))
                    gp.sem_inc(S["landed"], 1)

                def freed(gprev, base):
                    n = gp.value_load(bi_row[0:1, gprev], min_val=1, max_val=MAXN)
                    gp.wait_ge(S["half_used"], n * 2 + base)
                    gp.sem_inc(S["idle_p"], 1)

                if L == 1:
                    ntot = gp.value_load(bi_row[0:1, NG - 1:NG], min_val=1, max_val=MAXN)
                    off = gp.snap(ntot * 2 + 2)
                else:
                    off = 2
                for g in range(R):
                    fetch(g, g)
                    if g >= LAG:
                        arrived(g - LAG, 0)
                with gp.Fori(1, NG // R) as r:
                    for b in range(R):
                        freed(bass.ds((r - 1) * R + b, 1), off)
                        fetch(r * R + b, b)
                        arrived((b - LAG) % R, r if b >= LAG else r - 1)
                for g in range(NG // R * R, NG):
                    freed(bass.ds(g - R, 1), off)
                    fetch(g, g % R)
                    arrived((g - LAG) % R, (g - LAG) // R)
                for g in range(NG - LAG, NG):
                    arrived(g % R, g // R)
                gp.wait_ge(S["routed"], L + 1)
                gp.wait_ge(S["r_xall"], 1 + NC * (L + 1))
                gp.wait_ge(S["zeroed"], 16 * 11)
                for t in range(NT):
                    gp.indirect_dma_start(slots[L], bass.IndirectOffsetOnAxis(ap=sidx[:, t:t + 1], axis=0), XALL[:, t, :], None,
                                          bounds_check=slots[L].shape[0] - 1, oob_is_err=False).then_inc(S["scattered"], 16)
                if L == 0:
                    gp.wait_ge(S["e_out"], 16 * (NB0 // Q0) + 16)
                else:
                    gp.wait_ge(S["f_out"], 32 * E1 + 16)
                for t in range(NT):
                    gp.indirect_dma_start(XALL[:, t, :], None, yslots[L], bass.IndirectOffsetOnAxis(ap=gidx[:, t:t + 1], axis=0)).then_inc(S["gathered"], 16)

        @block.scalar
        def _(ac):
            ch = Chain(ac, S["act_chain"], S["idle_a"])
            for n, k in (("a_done", 1), ("a_kvacc", 1), ("b_done", 1), ("e_done", 1), ("f_ys", 1), ("r_done", 1), ("half_used", 2),
                         ("added", 1), ("a_xnT", 16), ("a_tab", 16), ("f_hs", 4), ("e_out", 16), ("f_out", 16), ("c_done", 1), ("a_sp", 0), ("r_xall", 1)):
                if k:
                    ac.sem_inc(S[n], k)
            ac.wait_ge(S["consts"], 9)
            ac.wait_ge(S["loaded"], 16 * len(loads))

            def held(sem, val):
                ac.wait_ge(S[sem], val)
                ac.sem_inc(S["idle_a"], 1)

            def landed(L):
                pass

            def root(k):
                ac.wait_ge(S["stat"], k)
                ac.activation(sd[:], mv[:, :, 1], ACT.Sqrt, bias=eps[:]).then_inc(S["stat_sd"], 1)

            def copyT(sem_in, sem_out, val):
                held(sem_in, val)
                for k in range(KD):
                    i = ac.activation(xT[:, k, :], ps[:, k * 1024:k * 1024 + CN], ACT.Copy)
                    if k == KD - 1:
                        i.then_inc(S[sem_out], 1)

            for L in range(2):
                if L == 1:
                    ac.wait_ge(S["deg_ready"], 1)
                    ac.activation(dinv[:], deg[:], ACT.Sqrt, bias=ones[:, 0:1]).then_inc(S["deg_sd"], 1)
                root(2 * L + 1)
                ac.wait_ge(S["made"], 3)
                with ac.Fori(0, NC) as c:
                    ch.loop(c, 1)
                    held("a_xnT", (c + NC * L + 1) * 16)
                    copyT("a_tr", "a_xT", v5(L, c))
                    if L == 0:
                        held("a_tab", (c + 1) * 16)
                        held("a_nb", c + 1)
                        ac.activation(Hs[:].rearrange("p j f -> p (j f)"), ps[:, 5 * B:5 * B + CT * D], ACT.Copy).then_inc(S["a_hs"], 1)
                    held("a_kvp", v5(L, c))
                    k_ps = ps[:, 0:CT * B].rearrange("p (j f) -> p j f", f=B)
                    ch.link(ac.activation(tmp[:], k_ps[:, :, 0:D], ACT.Relu, scale=-1.0))
                    ch.join()
                    ac.activation(ex[:], tmp[:], ACT.Exp, scale=-1.0).then_inc(S["a_e"], 1)
                    for j in range(CT):
                        i = ac.activation(Vb[:, j, :, 0:P], k_ps[:, j, D:2 * D].rearrange("p (a f) -> p a f", a=2), ACT.Copy, scale=valid[:, bass.ds(c * CT + j, 1)])
                    i.then_inc(S["a_v"], 1)
                ch.end(NC)
                if L == 1:
                    ac.wait_ge(S["ct_ps"], 1)
                    ac.activation(CTx[:].rearrange("p a f -> p (a f)"), bank(0, D), ACT.Copy).then_inc(S["ct_sb"], 1)
                    ac.wait_ge(S["m_ps"], 1)
                    ac.activation(Mx[:].rearrange("p a f -> p (a f)"), bank(1, 512), ACT.Copy).then_inc(S["m_ready"], 1)
                with ac.Fori(0, NC) as c:
                    ch.loop(c, 1)
                    q_ps = ps[:, 0:4 * B].rearrange("p (q n) -> p q n", n=B)[:, :, 0:HN]
                    t4 = tmp[:].rearrange("p j f -> p (j f)").rearrange("p (q n) -> p q n", q=4)
                    e4 = ex[:].rearrange("p j f -> p (j f)").rearrange("p (q n) -> p q n", q=4)
                    held("b_q", v5(L, c))
                    ch.link(ac.activation(t4, q_ps, ACT.Relu, scale=-1.0))
                    ch.join()
                    ac.activation(e4, t4, ACT.Exp, scale=-1.0).then_inc(S["b_e"], 1)
                    if L == 0:
                        for j in range(CT):
                            i = ac.activation(XN[:, j, :], X[:, bass.ds(c * CT + j, 1), :].rearrange("p a f -> p (a f)"), ACT.Identity,
                                              scale=rs[:, bass.ds(c * CT + j, 1)], bias=nm[:, bass.ds(c * CT + j, 1)])
                        i.then_inc(S["b_u"], 1)

                        def norm(z, w, r):
                            held(z, c + 1)
                            ac.activation(rt[:, 1, 0:CT], rt[:, 0, 0:2 * CT].rearrange("p (j s) -> p j s", s=2)[:, :, 1], ACT.Sqrt, bias=eps[:]).then_inc(S[w], 1)
                            held(r, c + 1)

                        norm("b_z", "b_sd1", "b_rs1")
                        for j in range(CT):
                            i = ac.activation(tmp[:, j, :], Z[:, j, :], ACT.Identity, scale=rt[:, 2, j:j + 1], bias=rt[:, 3, j:j + 1])
                        i.then_inc(S["b_n1"], 1)
                        held("b_x1t", c + 1)
                        for k in range(KD):
                            i = ac.activation(QT[:, k * CN:(k + 1) * CN], ps[:, k * 1024:k * 1024 + CN], ACT.Copy)
                        i.then_inc(S["b_x1T"], 1)
                        held("b_h", c + 1)
                        for m in range(KD):
                            i = ac.activation(HT[:, m, :].rearrange("p (q n) -> p q n", q=2), q_ps[:, 2 * m:2 * m + 2, :], ACT.Gelu, bias=b1c[:, m:m + 1])
                        i.then_inc(S["b_g"], 1)
                        norm("b_z2", "b_sd2", "b_rs2")
                        for j in range(CT):
                            i = ac.activation(tmp[:, j, :], Z[:, j, :], ACT.Identity, scale=rt[:, 2, j:j + 1], bias=rt[:, 3, j:j + 1])
                        i.then_inc(S["b_n2"], 1)
                ch.end(NC)
                if L == 1:
                    ac.wait_ge(S["agg_done"], 2)
                    with ac.Fori(0, NC) as c:
                        held("c_done", c + 1)
                        for j in range(CT):
                            i = ac.activation(AG[:, j, :], acc[:, bass.ds((c * CT + j) * AP_, D)], ACT.Copy, scale=dinv[:, bass.ds(c * CT + j, 1)])
                        i.then_inc(S["c_ag"], 1)
                        held("c_tr", c + 1)
                        for k in range(KD):
                            i = ac.activation(xT[:, k, :], ps[:, k * 1024:k * 1024 + CN], ACT.Copy)
                        i.then_inc(S["c_aT"], 1)
                root(2 * L + 2)
                with ac.Fori(0, NC) as c:
                    held("r_xn", v5(L, c))
                    ac.activation(acc[:, bass.ds(c * CT * D, CT * D)], XN[:].rearrange("p j f -> p (j f)"), ACT.Copy).then_inc(S["r_xall"], 1)
                    copyT("r_tr", "r_xT", v5(L, c))
                if L == 1:
                    ac.wait_ge(S["negm"], 1)
                    ac.activation(LG[:, 0:NT * E1], LG[:, 0:NT * E1], ACT.Exp).then_inc(S["expd"], 1)
                if L == 0:
                    with ac.Fori(0, NB0 // Q0) as i4:
                        held("e_tr", i4 + 1)
                        ac.activation(xbT0.rearrange("p s k n -> p (s k n)"), ps[:, 0:Q0 * D], ACT.Copy).then_inc(S["e_xT"], 1)
                        held("e_h", i4 + 1)
                        for s in range(Q0):
                            i = ac.activation(h0[0:F0, s, :], ps[0:F0, 2 * B + s * P:2 * B + (s + 1) * P], ACT.Relu, bias=b10[:, s:s + 1])
                        i.then_inc(S["e_hs"], 1)
                else:
                    with ac.Fori(0, E1 // 2) as i2:
                        for s in range(2):
                            e = i2 * 2 + s
                            held("f_tr", e + 1)
                            ac.activation(xb1T[:, :, 0:CAP], ps[:, 0:2 * B].rearrange("p (k n) -> p k n", k=2)[:, :, 0:CAP], ACT.Copy).then_inc(S["f_xT"], 1)
                            for m in range(MT):
                                held("f_h", e * MT + (m + 1))
                                ac.activation(h1[:, m, :], ps[:, (2 + m % 4) * B:(2 + m % 4) * B + CAP], ACT.Relu, bias=b11[:, bass.ds(e * MT + m, 1)]).then_inc(S["f_hs"], 1)

        @block.vector
        def _(v):
            ch = Chain(v, S["dve_chain"], S["idle_v"])

            def do(ins):
                ch.link(ins)
                ch.join()

            def held(sem, val):
                v.wait_ge(S[sem], val)
                v.sem_inc(S["idle_v"], 1)

            def flat(t):
                return t[:].rearrange("p j f -> p (j f)")

            def rows(c, j=None):
                return X[:, bass.ds(c * CT, CT), :].rearrange("p j f -> p (j f)") if j is None else X[:, bass.ds(c * CT + j, 1), :].rearrange("p a f -> p (a f)")

            def stats(k):
                for t in range(NT):
                    ch.link(v.bn_stats(st[:, t, :], X[:, t, :]))
                ch.join()
                for t in range(NT):
                    i = v.bn_aggr(mv[:, t, :], st[:, t, :])
                    if t < NT - 1:
                        ch.link(i)
                i.then_inc(S["stat"], 1)
                v.wait_ge(S["stat_sd"], k)
                do(v.reciprocal(rs[:], sd[:]))
                do(v.scalar_tensor_tensor(nm[:], mv[:, :, 0], -1.0, rs[:], ALU.mult, ALU.mult))

            def normed(c, sem):
                for j in range(CT):
                    i = v.tensor_scalar(XN[:, j, :], rows(c, j), mv[:, bass.ds(c * CT + j, 1), 0], rs[:, bass.ds(c * CT + j, 1)], ALU.subtract, ALU.mult)
                i.then_inc(S[sem], 1)

            v.wait_ge(S["consts"], 9)
            v.wait_ge(S["made"], 3)
            v.wait_ge(S["loaded"], 16 * len(loads))
            lo, hi, ln, cnt, delta, bi = (sm[:, i:i + 1] for i in range(6))
            do(v.tensor_copy(dst[:], oh[:].rearrange("p j n -> p (j n)")[:, 0:ET].bitcast(I32)))
            ch.link(v.tensor_reduce(smi[:, 0:1], dg, AX.X, ALU.min))
            ch.link(v.tensor_reduce(smi[:, 1:2], dg, AX.X, ALU.max))
            do(v.tensor_reduce(smi[:, 2:3], dn, AX.X, ALU.min))
            do(v.tensor_scalar(smi[:], smi[:], 7, None, ALU.arith_shift_right))
            do(v.tensor_copy(sm[:, 0:3], smi[:]))
            ch.link(v.tensor_copy(lo0[:], sm[0:1, 0:1]))
            ch.link(v.scalar_tensor_tensor(cnt, hi, 1.0, lo, ALU.add, ALU.subtract))
            do(v.scalar_tensor_tensor(delta, ln, -1.0, hi, ALU.add, ALU.subtract))
            v.sem_inc(S["prepped"], 1)
            v.wait_ge(S["ranked"], 1)
            do(v.tensor_copy(bi, ps[0:NG, 0:1]))
            do(v.tensor_copy(bi_row[:], ps[0:1, 4:4 + NG]))
            ch.link(v.memset(seg_row[:, 0:1], 0))
            for c in range(1, NC + 1):
                g = min(c * SEG, NG) - 1
                ch.link(v.tensor_copy(seg_row[:, c:c + 1], bi_row[:, g:g + 1]))
            ch.link(v.memset(w_row[:, 0:1], NT))
            do(v.tensor_scalar(step, iota[0:NG, 0:MAXN], bi, None, ALU.is_ge))
            v.sem_inc(S["prepped"], 1)
            for k, q in enumerate(range(0, MAXN, 512)):
                m = min(512, MAXN - q)
                v.wait_ge(S["ranked"], 2 + k)
                ch.link(v.tensor_scalar(g_row[0:1, q:q + m], ps[0:1, 0:m], float(NG - 1), None, ALU.min))
                do(v.scalar_tensor_tensor(w_row[0:1, 1 + q:1 + q + m], ps[0:1, B:B + m], lo0[0:1, 0:1], iota[0:1, q:q + m], ALU.add, ALU.add))
                v.sem_inc(S["listed"], 1)
            ch.link(v.memset(KV[:], 0.0))
            do(v.memset(ps[:, 6 * B:8 * B], 0.0))
            v.sem_inc(S["listed"], 1)
            v.wait_ge(S["xload"], 16 * (NC + 1))

            def segment(L, c, n0):
                s0 = v.value_load(seg_row[0:1, bass.ds(c, 1)], min_val=0, max_val=MAXN)
                s1 = v.value_load(seg_row[0:1, bass.ds(c + 1, 1)], min_val=1, max_val=MAXN)
                with v.Fori(s0, s1) as n:
                    g = v.value_load(g_row[0:1, bass.ds(n, 1)], min_val=0, max_val=NG - 1)
                    w = v.value_load(w_row[0:1, bass.ds(n + 1, 1)], min_val=0, max_val=NT)
                    wp = v.value_load(w_row[0:1, bass.ds(n, 1)], min_val=0, max_val=NT)
                    for h in range(2):
                        v.wait_ge(S["half_used"], (n + n0) * 2 + (h + 1))
                        v.tensor_tensor(oh[:, 2 * h:2 * h + 2, :], iota[:, bass.ds(w * P, P)].unsqueeze(1).to_broadcast([P, 2, P]),
                                        dst[:, bass.ds(g * GT + 2 * h, 2)].unsqueeze(2).to_broadcast([P, 2, P]), ALU.is_equal).then_inc(S["oh_half"], 1)
                    v.wait_ge(S["added"], n + n0 + (1 + L))
                    r = acc[:, bass.ds(wp * AP_, AP_)]
                    v.tensor_tensor(r, r, ps[:, bass.ds(((n + n0 + 1) % 2) * B + 6 * B, AP_)], ALU.add).then_inc(S["added"], 1)

            for L in range(2):
                nE, nF = (E0, E1)[L], 0
                stats(2 * L + 1)
                if L == 1:
                    v.wait_ge(S["deg_sd"], 1)
                    do(v.reciprocal(dinv[:], dinv[:]))
                    do(v.memset(KV[:], 0.0))
                with v.Fori(0, NC) as c:
                    ch.loop(c, 12 if L == 0 else 7)
                    held("a_done", v5(L, c))
                    normed(c, "a_xn")
                    if L == 0:
                        held("a_hs", c + 1)
                        for r in range(4):
                            for j in range(CT):
                                i = v.max(m8[:, j, :], (Hs if r == 0 else Wk)[:, j, :])
                            do(i)
                            for j in range(CT):
                                i = v.match_replace(Wk[:, j, :], m8[:, j, :], (Hs if r == 0 else Wk)[:, j, :], SENT)
                            do(i)
                        do(v.tensor_tensor(flat(Wk), flat(Wk), flat(Hs), ALU.not_equal))
                        v.tensor_tensor(flat(Hs), flat(Wk), flat(Hs), ALU.mult).then_inc(S["a_sp"], 1)
                    else:
                        held("a_tab", (c + NC + 1) * 16)
                        held("a_xn", v5(L, c))
                        for j in range(CT):
                            ch.link(v.tensor_scalar(Wk[:, j, :], XN[:, j, :], dinv[:, bass.ds(c * CT + j, 1)], None, ALU.mult))
                        ch.join()
                        v.tensor_copy(a3[:, bass.ds(c * CT, CT), 0:D], Wk[:]).then_inc(S["a_sp"], 1)
                    for q in range(2):
                        ch.link(v.tensor_copy(Vb[:, :, q, P], valid[:, bass.ds(c * CT, CT)]))
                        if L == 0 and q == 0:
                            pass
                    held("a_v", v5(L, c))
                    k_ps = ps[:, 0:CT * B].rearrange("p (j f) -> p j f", f=B)[:, :, 0:D]
                    v.scalar_tensor_tensor(Kb[:], k_ps, 0.0, ex[:], ALU.max, ALU.add).then_inc(S["a_k"], 1)
                    held("a_kv", v5(L, c))
                    kv_ps = ps[:, 0:2 * B].rearrange("p (a f) -> p a f", a=2)[:, :, 0:P + 1]
                    do(v.tensor_tensor(KV[:], KV[:], kv_ps, ALU.add)) if L == 0 else v.tensor_tensor(KV[:], KV[:], kv_ps, ALU.add).then_inc(S["a_kvacc"], 1)
                    if L == 0:
                        v.sem_inc(S["a_kvacc"], 1)
                    else:
                        v.wait_ge(S["a_kvacc"], v5(L, c) + 1)
                        v.sem_inc(S["idle_v"], 1)
                ch.end(NC)
                do(v.memset(KVb[:], 0.0))
                do(v.memset(KS[:], 0.0))
                for q in range(2):
                    for h in range(HH):
                        r = slice(HD * h, HD * (h + 1))
                        ch.link(v.tensor_copy(KVb[r, q, HD * h:HD * (h + 1)], KV[r, q, HD * h:HD * (h + 1)]))
                        ch.link(v.tensor_copy(KVb[r, q, P + h:P + h + 1], KV[r, q, P:P + 1]))
                        ch.link(v.tensor_copy(KS[r, q, HD * h:HD * (h + 1)], KV[r, q, P:P + 1].to_broadcast([HD, HD])))
                ch.join()
                v.sem_inc(S["kv_ready"], 1)
                n0 = 0
                if L == 1:
                    n0 = v.snap(v.value_load(bi_row[0:1, NG - 1:NG], min_val=NG, max_val=MAXN))
                    v.memset(ps[:, 6 * B:8 * B], 0.0).then_inc(S["listed"], 1)
                else:
                    v.wait_ge(S["zeroed"], 16 * 11)
                with v.Fori(0, NC) as c:
                    q_ps = ps[:, 0:4 * B].rearrange("p (q n) -> p q n", n=B)[:, :, 0:HN]
                    q4 = QT.rearrange("p (q n) -> p q n", q=4)
                    e4 = flat(ex).rearrange("p (q n) -> p q n", q=4)
                    held("b_e", v5(L, c))
                    v.scalar_tensor_tensor(q4, q_ps, 0.0, e4, ALU.max, ALU.add).then_inc(S["b_qt"], 1)
                    if L == 0:
                        ch.loop(c, 14)
                        held("b_t", c + 1)
                        t_ps = ps[:, 0:CT * B].rearrange("p (j f) -> p j f", f=B)[:, :, 0:2 * (P + HH)].rearrange("p j (a f) -> p j a f", a=2)
                        do(v.tensor_scalar(den[:], t_ps[:, :, :, P:P + HH], 1e-6, None, ALU.add))
                        do(v.reciprocal(den[:], den[:]))
                        for j in range(CT):
                            i = v.tensor_tensor(Hs[:, j, :].rearrange("p (a h f) -> p a h f", a=2, h=HH),
                                                t_ps[:, j, :, 0:P].rearrange("p a (h f) -> p a h f", h=HH),
                                                den[:, j].unsqueeze(3).to_broadcast([P, 2, HH, HD]), ALU.mult)
                        do(i)
                        held("b_u", c + 1)
                        do(v.tensor_tensor(flat(Z), flat(Hs), flat(XN), ALU.add))

                        def norm(z, w, r, n, gi, last):
                            for j in range(CT):
                                i = v.bn_stats(st[:, j, :], Z[:, j, :])
                            do(i)
                            for j in range(CT):
                                i = v.bn_aggr(rt[:, 0, 2 * j:2 * j + 2], st[:, j, :])
                            i.then_inc(S[z], 1)
                            held(w, c + 1)
                            do(v.reciprocal(rt[:, 2, 0:CT], rt[:, 1, 0:CT]))
                            v.scalar_tensor_tensor(rt[:, 3, 0:CT], rt[:, 0, 0:2 * CT].rearrange("p (j s) -> p j s", s=2)[:, :, 0], -1.0,
                                                   rt[:, 2, 0:CT], ALU.mult, ALU.mult).then_inc(S[r], 1)
                            held(n, c + 1)
                            do(v.tensor_tensor(tmp[:], tmp[:], lng[:, gi, :].unsqueeze(1).to_broadcast([P, CT, D]), ALU.mult))
                            return v.tensor_tensor(last, tmp[:], lng[:, gi + 1, :].unsqueeze(1).to_broadcast([P, CT, D]), ALU.add)

                        norm("b_z", "b_sd1", "b_rs1", "b_n1", 0, X1[:]).then_inc(S["b_x1"], 1)
                        held("b_y", c + 1)
                        do(v.tensor_tensor(flat(Z), flat(X1), ps[:, 0:CT * D], ALU.add))
                        do(norm("b_z2", "b_sd2", "b_rs2", "b_n2", 2, tmp[:]))
                        do(v.tensor_tensor(rows(c), rows(c), flat(tmp), ALU.add))
                        do(v.tensor_tensor(rows(c), rows(c), ps[:, 3 * B:3 * B + CT * D], ALU.add))
                        v.sem_inc(S["b_done"], 1)
                        segment(L, c, 0)
                    else:
                        ch.loop(c, 2)
                        held("b_den", c + 1)
                        do(v.tensor_scalar(e4, q_ps, 1e-6, None, ALU.max))
                        do(v.reciprocal(flat(ex), flat(ex)))
                        v.tensor_tensor(QT, QT, flat(ex), ALU.mult).then_inc(S["b_qs"], 1)
                        held("b_y", c + (NC + 1))
                        v.tensor_tensor(rows(c), rows(c), ps[:, 0:CT * D], ALU.add).then_inc(S["b_done"], 1)
                        segment(L, c, n0)
                ch.end(NC)
                nl = v.value_load(bi_row[0:1, NG - 1:NG], min_val=NG, max_val=MAXN)
                w = v.value_load(w_row[0:1, bass.ds(nl, 1)], min_val=0, max_val=NT)
                v.wait_ge(S["half_used"], (nl + n0) * 2 + 2)
                v.sem_inc(S["idle_v"], 1)
                v.wait_ge(S["added"], nl + n0 + (1 + L))
                r = acc[:, bass.ds(w * AP_, AP_)]
                v.tensor_tensor(r, r, ps[:, bass.ds(((nl + n0 + 1) % 2) * B + 6 * B, AP_)], ALU.add).then_inc(S["added"], 1)
                v.wait_ge(S["added"], nl + n0 + (2 + L))
                v.sem_inc(S["agg_done"], 1)
                if L == 0:
                    do(v.tensor_copy(deg[:], a3[:, 0:NT, D]))
                    v.sem_inc(S["deg_ready"], 1)
                    do(v.tensor_scalar(rdeg[:], deg[:], 1.0, None, ALU.max))
                    do(v.reciprocal(rdeg[:], rdeg[:]))
                    with v.Fori(0, NC) as c:
                        for j in range(CT):
                            i = v.scalar_tensor_tensor(rows(c, j), acc[:, bass.ds((c * CT + j) * AP_, D)], rdeg[:, bass.ds(c * CT + j, 1)], rows(c, j), ALU.mult, ALU.add)
                        ch.loop(c, 1)
                        ch.link(i)
                    ch.end(NC)
                    ch.join()
                    v.sem_inc(S["layer_done"], 1)
                else:
                    with v.Fori(0, NC) as c:
                        held("c_y", c + 1)
                        v.tensor_tensor(rows(c), rows(c), ps[:, 4 * B:4 * B + CT * D], ALU.add).then_inc(S["c_done"], 1)
                    v.wait_ge(S["c_done"], NC + 1)
                stats(2 * L + 2)
                with v.Fori(0, NC) as c:
                    held("r_done", v5(L, c))
                    held("r_xall", v5(L, c))
                    normed(c, "r_xn")
                    held("r_lg", v5(L, c))
                    v.tensor_copy(LG[:, bass.ds(c * (CT * nE), CT * nE)], ps[:, 4 * B:4 * B + CT * nE]).then_inc(S["r_lgs"], 1)
                v.wait_ge(S["r_lgs"], NC * (L + 1))
                lg = LG[:, 0:NT * nE].rearrange("p (t e) -> p t e", e=nE)
                ohv = OH[:, 0:NT * nE].rearrange("p (t e) -> p t e", e=nE)
                if L == 1:
                    do(v.tensor_reduce(t25, lg, AX.X, ALU.max))
                    do(v.tensor_tensor(lg, lg, t25.unsqueeze(2).to_broadcast([P, NT, nE]), ALU.subtract))
                    v.sem_inc(S["negm"], 1)
                    v.wait_ge(S["expd"], 1)
                    do(v.tensor_reduce(se, lg, AX.X, ALU.add))
                    do(v.reciprocal(se, se))
                    do(v.tensor_tensor(lg, lg, se.unsqueeze(2).to_broadcast([P, NT, nE]), ALU.mult))
                for t in range(NT):
                    ch.link(v.max(mx[:, 8 * t:8 * t + 8], lg[:, t, :]))
                ch.join()
                for t in range(NT):
                    ch.link(v.max_index(mi[:, 8 * t:8 * t + 8], mx[:, 8 * t:8 * t + 8], lg[:, t, :]))
                ch.join()
                do(v.tensor_copy(mif, mi.rearrange("p (t s) -> p t s", s=8)[:, :, 0]))
                do(v.tensor_tensor(ohv, iota[:, 0:nE].unsqueeze(1).to_broadcast([P, NT, nE]), mif.unsqueeze(2).to_broadcast([P, NT, nE]), ALU.is_equal))
                do(v.tensor_tensor(ohv, ohv, valid[:].unsqueeze(2).to_broadcast([P, NT, nE]), ALU.mult))
                v.sem_inc(S["oh_ready"], 1)
                W = NT * nE
                half = W // 2
                tot = ps[:, 2 * B:2 * B + 2 * B]
                ttv = TT[:, 0:W].rearrange("p (e t) -> p e t", t=NT)
                inv_ = IN[:, 0:W].rearrange("p (e t) -> p e t", t=NT)
                mkv = MSK[:, 0:W].rearrange("p (e t) -> p e t", t=NT)
                prv = PR[:, 0:W].rearrange("p (t e) -> p t e", e=nE)
                do(v.memset(MSK[:, 0:W], 1.0))
                do(v.memset(mkv[:, :, 0:1], 0.0))
                v.wait_ge(S["mass"], L + 1)
                nh = 2 if L == 0 else 1
                wt = NT * nE // nh
                do(v.tensor_copy(PR[:, 0:wt], ps[:, 0:wt]))
                do(v.tensor_copy(IN[:, 0:wt], ps[:, 2 * B:2 * B + wt]))
                if nh == 2:
                    do(v.tensor_copy(PR[:, wt:2 * wt], ps[:, B:B + wt]))
                    do(v.tensor_copy(IN[:, wt:2 * wt], ps[:, 3 * B:3 * B + wt]))
                do(v.tensor_copy(ttv, IN[:, 0:W].rearrange("p (t e) -> p e t", e=nE)))
                do(v.tensor_tensor_scan(IN[:, 0:W], MSK[:, 0:W], TT[:, 0:W], 0.0, ALU.mult, ALU.add))
                do(v.tensor_copy(cntE[:, 0:nE], inv_[:, :, NT - 1]))
                do(v.tensor_tensor(IN[:, 0:W], IN[:, 0:W], TT[:, 0:W], ALU.subtract))
                do(v.tensor_tensor(prv, prv, IN[:, 0:W].rearrange("p (e t) -> p t e", t=NT), ALU.add))
                do(v.tensor_tensor(prv, prv, ohv, ALU.mult))
                do(v.tensor_reduce(rank, prv, AX.X, ALU.add))
                if L == 0:
                    do(v.tensor_scalar(nbE, cntE, float(P - 1), None, ALU.add))
                    do(v.tensor_copy(nbEi, nbE))
                    do(v.tensor_scalar(nbEi, nbEi, 7, None, ALU.arith_shift_right))
                    do(v.tensor_copy(nbE, nbEi))
                    do(v.tensor_tensor_scan(CE, ones[:, 0:E0], nbE, 0.0, ALU.mult, ALU.add))
                    do(v.tensor_tensor(baseE, CE, nbE, ALU.subtract))
                    do(v.tensor_scalar(baseE, baseE, float(P), None, ALU.mult))
                    eb3 = ebc[0:1, :].rearrange("p (b e) -> p b e", e=E0)
                    do(v.tensor_tensor(eb3, iota[0:1, 0:NB0].unsqueeze(2).to_broadcast([1, NB0, E0]), CE[0:1, :].unsqueeze(1).to_broadcast([1, NB0, E0]), ALU.is_ge))
                    do(v.tensor_reduce(ebf[0:1, :], eb3, AX.X, ALU.add))
                    do(v.tensor_scalar(ebi[:], ebf[0:1, :], float(E0 - 1), None, ALU.min))
                else:
                    do(v.tensor_scalar(baseE[:, 0:nE], iota[:, 0:nE], float(CAP), None, ALU.mult))
                do(v.tensor_tensor(prv, ohv, baseE[:, 0:nE].unsqueeze(1).to_broadcast([P, NT, nE]), ALU.mult))
                do(v.tensor_reduce(pos, prv, AX.X, ALU.add))
                if L == 0:
                    do(v.tensor_copy(kept, valid[:]))
                    do(v.tensor_tensor(t25, pos, rank, ALU.add))
                    do(v.tensor_copy(gidx[:], t25))
                else:
                    do(v.tensor_scalar(kept, rank, float(CAP), None, ALU.is_lt))
                    do(v.tensor_copy(rt[:, 4, :], se))
                    do(v.tensor_tensor(rt[:, 4, :], rt[:, 4, :], kept, ALU.mult))
                    do(v.tensor_tensor(kept, kept, valid[:], ALU.mult))
                    do(v.tensor_tensor(t25, pos, rank, ALU.add))
                    do(v.tensor_scalar(rank, rank, float(CAP - 1), None, ALU.min))
                    do(v.tensor_tensor(pos, pos, rank, ALU.add))
                    do(v.tensor_copy(gidx[:], pos))
                do(v.tensor_scalar(kept, kept, -FAR, FAR, ALU.mult, ALU.add))
                do(v.tensor_tensor(t25, t25, kept, ALU.add))
                do(v.tensor_copy(sidx[:], t25))
                if L == 0:
                    do(v.memset(h0[F0:F0 + 1], 1.0))
                v.sem_inc(S["routed"], 1)
                if L == 0:
                    with v.Fori(0, NB0 // Q0) as i4:
                        held("e_out", (i4 + 1) * 16)
                        held("e_y", i4 + 1)
                        v.tensor_scalar(y0.rearrange("p s f -> p (s f)"), ps[:, 3 * B:3 * B + Q0 * D], 0.0, None, ALU.max).then_inc(S["e_ys"], 1)
                    v.wait_ge(S["gathered"], 16 * NT)
                    with v.Fori(0, NC) as c:
                        ch.loop(c, 1)
                        ch.link(v.tensor_tensor(rows(c), rows(c), acc[:, bass.ds(c * (CT * D), CT * D)], ALU.add))
                    ch.end(NC)
                    ch.join()
                    do(v.memset(ring4[:, :, :, D:AP_], 1.0))
                    do(v.memset(acc[:, 0:1], 0.0))
                    do(v.memset(acc[:, NT * D:], 0.0))
                    do(v.memset(acc[:], 0.0))
                    v.sem_inc(S["layer_done"], 1)
                else:
                    with v.Fori(0, E1 // 2) as i2:
                        for s in range(2):
                            e = i2 * 2 + s
                            held("f_out", (e * 2 + 1) * 16)
                            held("f_y", e + 1)
                            v.tensor_copy(y1.rearrange("p s f -> p (s f)")[:, 0:(ST - 1) * D], ps[:, 6 * B:6 * B + (ST - 1) * D])
                            v.tensor_copy(y1[0:STAIL, ST - 1, :], ps[0:STAIL, 6 * B + (ST - 1) * D:8 * B]).then_inc(S["f_ys"], 1)
                    v.wait_ge(S["gathered"], 32 * NT)
                    bad = Hs[:].bitcast(I32)
                    for c in range(NC):
                        y = XALL[:, c * CT:(c + 1) * CT, :]
                        do(v.tensor_tensor(y, y, rt[:, 4, c * CT:(c + 1) * CT].unsqueeze(2).to_broadcast([P, CT, D]), ALU.mult))
                        for op, lim, fill in ((ALU.is_gt, FMAX, 10000.0), (ALU.is_lt, -FMAX, -10000.0), (None, None, 0.0)):
                            if op is None:
                                ch.link(v.tensor_tensor(bad, y, y, ALU.not_equal))
                            else:
                                ch.link(v.tensor_scalar(bad, y, lim, None, op))
                            do(v.memset(Kb[:], fill))
                            do(v.copy_predicated(y, bad, Kb[:]))
                        do(v.tensor_tensor(X[:, c * CT:(c + 1) * CT, :], X[:, c * CT:(c + 1) * CT, :], y, ALU.add))
                        v.sem_inc(S["layer_done"], 1)

        @block.tensor
        def _(pe):
            mm = nc.tensor.matmul
            tp = nc.tensor.transpose

            def held(sem, val):
                pe.wait_ge(S[sem], val)
                pe.sem_inc(S["idle_t"], 1)

            pe.wait_ge(S["made"], 3)
            pe.wait_ge(S["loaded"], 16 * len(loads))
            pe.wait_ge(S["prepped"], 1)
            cnt, delta = sm[:, 3:4], sm[:, 4:5]
            mm(ps[0:NG, 0:1], tri[0:NG, 0:NG], cnt, start=True, stop=True)
            mm(ps[0:1, 4:4 + NG], cnt, tri[0:NG, 0:NG], start=True, stop=True).then_inc(S["ranked"], 1)
            pe.wait_ge(S["prepped"], 2)
            for k, q in enumerate(range(0, MAXN, 512)):
                m = min(512, MAXN - q)
                if k:
                    pe.wait_ge(S["listed"], k)
                mm(ps[0:1, 0:m], ones[0:NG, 0:1], step[:, q:q + m], start=True, stop=True)
                mm(ps[0:1, B:B + m], delta, step[:, q:q + m], start=True, stop=True).then_inc(S["ranked"], 1)
            pe.wait_ge(S["listed"], -(-MAXN // 512) + 1)

            def transposes(srcb, sem, done=None):
                for j in range(CT):
                    for k in range(KD):
                        i = tp(ps[:, k * 1024 + j * P:k * 1024 + (j + 1) * P], srcb[:, j, k * P:(k + 1) * P], ident[:])
                i.then_inc(S[sem], 1)
                return i

            def segment(L, c, n0):
                s0 = pe.value_load(seg_row[0:1, bass.ds(c, 1)], min_val=0, max_val=MAXN)
                s1 = pe.value_load(seg_row[0:1, bass.ds(c + 1, 1)], min_val=1, max_val=MAXN)
                with pe.Fori(s0, s1) as n:
                    g = pe.value_load(g_row[0:1, bass.ds(n, 1)], min_val=0, max_val=NG - 1)
                    pe.wait_ge(S["landed"], g + (NG * L + 1))
                    pe.sem_inc(S["idle_t"], 1)
                    w = AP_ if L == 0 else AP_
                    for h in range(2):
                        pe.wait_ge(S["oh_half"], (n + n0) * 2 + (h + 1))
                        for j in (2 * h, 2 * h + 1):
                            i = mm(ps[:, bass.ds(((n + n0) % 2) * B + 6 * B, w)], oh[:, j, :],
                                   ring[:, bass.ds((g % R) * (GT * AP_) + j * AP_, w)], start=j == 0, stop=j == GT - 1)
                        i.then_inc(S["half_used"], 1)

            for L in range(2):
                if L == 1:
                    pe.wait_ge(S["wload"], 48)
                with pe.Fori(0, NC) as c:
                    held("a_kvacc", v5(L, c))
                    held("a_xn", v5(L, c))
                    transposes(XN, "a_tr")
                    held("a_xT", v5(L, c))
                    if L == 0:
                        for j in range(CT):
                            for k in range(KD):
                                i = mm(ps[:, 5 * B + j * D:5 * B + (j + 1) * D], xT[:, k, j * P:(j + 1) * P], wn[:, k, :], start=k == 0, stop=k == KD - 1)
                        i.then_inc(S["a_nb"], 1)
                    for j in range(CT):
                        for k in range(KD):
                            i = mm(ps[:, j * B:(j + 1) * B], xT[:, k, j * P:(j + 1) * P], wqkv[:, k, D:3 * D], start=k == 0, stop=k == KD - 1)
                    i.then_inc(S["a_kvp"], 1)
                    held("a_k", v5(L, c))
                    for q in range(2):
                        for j in range(CT):
                            i = mm(ps[:, q * B:q * B + P + 1], Kb[:, j, q * P:(q + 1) * P], Vb[:, j, q, :], start=j == 0, stop=j == CT - 1)
                    i.then_inc(S["a_kv"], 1)
                    pe.sem_inc(S["a_done"], 1)
                pe.wait_ge(S["kv_ready"], L + 1)
                n0 = 0
                if L == 1:
                    for q in range(2):
                        i = tp(ps[:, q * P:(q + 1) * P], KVb[:, q, 0:P], ident[:])
                    i.then_inc(S["ct_ps"], 1)
                    pe.wait_ge(S["ct_sb"], 1)
                    for q in range(2):
                        i = mm(ps[:, B + q * D:B + (q + 1) * D], CTx[:, q, :], wm1[:, q, :], start=True, stop=True)
                    i.then_inc(S["m_ps"], 1)
                    pe.wait_ge(S["m_ready"], 1)
                    n0 = pe.snap(pe.value_load(bi_row[0:1, NG - 1:NG], min_val=NG, max_val=MAXN))
                    pe.wait_ge(S["listed"], -(-MAXN // 512) + 2)
                with pe.Fori(0, NC) as c:
                    held("b_done", v5(L, c))
                    held("b_xs", v5(L, c) * 16)
                    for m in range(KD):
                        for n in range(2):
                            for k in range(KD):
                                i = mm(ps[:, (2 * m + n) * B:(2 * m + n) * B + HN], wqkv[:, k, m * P:(m + 1) * P], xT[:, k, n * HN:(n + 1) * HN], start=k == 0, stop=k == KD - 1)
                    i.then_inc(S["b_q"], 1)
                    held("b_qt", v5(L, c))
                    if L == 0:
                        for j in range(CT):
                            for q in range(2):
                                i = mm(ps[:, j * B + q * (P + HH):j * B + (q + 1) * (P + HH)], QT[:, q * CN + j * P:q * CN + (j + 1) * P], KVb[:, q, :], start=True, stop=True)
                        i.then_inc(S["b_t"], 1)
                        held("b_x1", c + 1)
                        transposes(X1, "b_x1t")
                        held("b_x1T", c + 1)
                        for m in range(KD):
                            for n in range(2):
                                for k in range(KD):
                                    i = mm(ps[:, (2 * m + n) * B:(2 * m + n) * B + HN], wm1[:, k, m * P:(m + 1) * P], QT[:, k * CN + n * HN:k * CN + (n + 1) * HN], start=k == 0, stop=k == KD - 1)
                        i.then_inc(S["b_h"], 1)
                        held("b_g", c + 1)
                        for j in range(CT):
                            o_ = ps[:, j * D:(j + 1) * D]
                            mm(o_, ones[0:1, :], brow[0:1, 0, :], start=True, stop=False)
                            for k in range(KD):
                                mm(o_, HT[:, k, j * P:(j + 1) * P], wm2[:, k, :], start=False, stop=k == KD - 1)
                        for j in range(CT):
                            for k in range(KD):
                                i = mm(ps[:, 3 * B + j * D:3 * B + (j + 1) * D], xT[:, k, j * P:(j + 1) * P], ws[:, k, :], start=k == 0, stop=k == KD - 1)
                        i.then_inc(S["b_y"], 1)
                    else:
                        for m in range(2):
                            for n in range(2):
                                i = mm(ps[:, (2 * m + n) * B:(2 * m + n) * B + HN], KS[:, m, :], QT[:, m * CN + n * HN:m * CN + (n + 1) * HN], start=True, stop=True)
                        i.then_inc(S["b_den"], 1)
                        held("b_qs", c + 1)
                        for j in range(CT):
                            o_ = ps[:, j * D:(j + 1) * D]
                            mm(o_, ones[0:1, :], brow[0:1, 1, :], start=True, stop=False)
                            for q in range(2):
                                i = mm(o_, QT[:, q * CN + j * P:q * CN + (j + 1) * P], Mx[:, q, :], start=False, stop=q == 1)
                        i.then_inc(S["b_y"], 1)
                    segment(L, c, n0)
                if L == 1:
                    with pe.Fori(0, NC) as c:
                        held("c_ag", c + 1)
                        transposes(AG, "c_tr")
                        held("c_aT", c + 1)
                        for j in range(CT):
                            o_ = ps[:, 4 * B + j * D:4 * B + (j + 1) * D]
                            mm(o_, ones[0:1, :], brow[0:1, 2, :], start=True, stop=False)
                            for k in range(KD):
                                i = mm(o_, xT[:, k, j * P:(j + 1) * P], wn[:, k, :], start=False, stop=k == KD - 1)
                        i.then_inc(S["c_y"], 1)
                nE = (E0, E1)[L]
                rwl = (rw, gw)[L]
                r0 = (0, E0)[L]
                with pe.Fori(0, NC) as c:
                    held("r_xn", v5(L, c))
                    transposes(XN, "r_tr")
                    held("r_xT", v5(L, c))
                    for j in range(CT):
                        o_ = ps[:, 4 * B + j * nE:4 * B + (j + 1) * nE]
                        mm(o_, ones[0:1, :], rrow[0:1, r0:r0 + nE], start=True, stop=False)
                        for k in range(KD):
                            i = mm(o_, xT[:, k, j * P:(j + 1) * P], rwl[:, k, :], start=False, stop=k == KD - 1)
                    i.then_inc(S["r_lg"], 1)
                    pe.sem_inc(S["r_done"], 1)
                pe.wait_ge(S["oh_ready"], L + 1)
                nh = 2 if L == 0 else 1
                wt = NT * nE // nh
                for q in range(nh):
                    mm(ps[:, q * B:q * B + wt], tris[:], OH[:, q * wt:(q + 1) * wt], start=True, stop=True)
                    i = mm(ps[:, (2 + q) * B:(2 + q) * B + wt], ones[:], OH[:, q * wt:(q + 1) * wt], start=True, stop=True)
                i.then_inc(S["mass"], 1)
                if L == 0:
                    with pe.Fori(0, NB0 // Q0) as i4:
                        held("e_x", (i4 + 1) * (16 * 4 * Q0))
                        for s in range(Q0):
                            for k in range(KD):
                                i = tp(ps[:, s * D + k * P:s * D + (k + 1) * P], xb0[:, s, k * P:(k + 1) * P], ident[:])
                        i.then_inc(S["e_tr"], 1)
                        held("e_xT", i4 + 1)
                        for s in range(Q0):
                            for k in range(KD):
                                i = mm(ps[0:F0, 2 * B + s * P:2 * B + (s + 1) * P], w10[:, s, k, :], xbT0[:, s, k, :], start=k == 0, stop=k == KD - 1)
                        i.then_inc(S["e_h"], 1)
                        held("e_hs", i4 + 1)
                        for s in range(Q0):
                            i = mm(ps[:, 3 * B + s * D:3 * B + (s + 1) * D], h0[0:F0 + 1, s, :], w20[0:F0 + 1, s, :], start=True, stop=True)
                        i.then_inc(S["e_y"], 1)
                        held("e_ys", i4 + 1)
                        pe.sem_inc(S["e_done"], 1)
                else:
                    with pe.Fori(0, E1 // 2) as i2:
                        for s in range(2):
                            e = i2 * 2 + s
                            held("f_x", (e + 1) * (16 * 5))
                            for t in range(ST):
                                rws = P if t < ST - 1 else STAIL
                                for k in range(KD):
                                    i = tp(ps[:, k * B + t * P:k * B + t * P + rws], xb1[0:rws, t, k * P:(k + 1) * P], ident[0:rws, 0:rws])
                            i.then_inc(S["f_tr"], 1)
                            held("f_xT", e + 1)
                            for m in range(MT):
                                held("f_hs", e * MT + (m + 1))
                                for k in range(KD):
                                    i = mm(ps[:, (2 + m % 4) * B:(2 + m % 4) * B + CAP], w11[:, s, k, m * P:(m + 1) * P], xb1T[:, k, 0:CAP], start=k == 0, stop=k == KD - 1)
                                i.then_inc(S["f_h"], 1)
                            held("f_hs", e * MT + (MT + 4))
                            for t in range(ST):
                                rws = P if t < ST - 1 else STAIL
                                o_ = ps[0:rws, 6 * B + t * D:6 * B + (t + 1) * D]
                                mm(o_, ones[0:1, 0:rws], b21[0:1, s, :], start=True, stop=False)
                                for m in range(MT):
                                    i = mm(o_, h1[:, m, t * P:t * P + rws], w21[:, s, m, :], start=False, stop=m == MT - 1)
                            i.then_inc(S["f_y"], 1)


def kernel(**inputs):
    import numpy as _np
    import concourse.bacc as _bacc
    from concourse import mybir as _mybir
    from concourse.bass_utils import run_bass_kernel_spmd as _run

    nc = _bacc.Bacc("TRN2", target_bir_lowering=False, num_devices=1)
    g = {k: _np.asarray(v) for k, v in inputs.items()}
    ep = NG * GE - E

    def halves(w):
        return w.reshape(KD, P, -1).transpose(1, 0, 2)

    dgrp = _np.pad(g["dst"], (0, ep), mode="edge").reshape(NG, GE)
    a = {
        "x": g["x"],
        "srcT": _np.pad(g["src"], (0, ep)).reshape(ET, P).T,
        "dstT": _np.pad(g["dst"], (0, ep), constant_values=-1).reshape(ET, P).T,
        "dgrp": dgrp,
        "dnext": _np.concatenate([dgrp[1:], _np.full((1, GE), NT * P, dgrp.dtype)]),
        "wn": halves(g["L0_gnn_W_neigh"]),
        "ws": halves(g["L0_gnn_W_self"]),
        "wqkv0": halves(g["L0_mix_Wqkv"].T),
        "wm1": halves(g["L0_mix_W1"].T),
        "wm2": halves(g["L0_mix_W2"].T),
        "lng": _np.broadcast_to(_np.stack([g["L0_mix_ln1_g"], g["L0_mix_ln1_b"], g["L0_mix_ln2_g"], g["L0_mix_ln2_b"]]), (P, 4, D)),
        "b1c": g["L0_mix_b1"].reshape(KD, P).T,
        "mb2": g["L0_mix_b2"][None],
        "b1rows": _np.stack([g["L1_mix_bproj"], g["L1_gnn_b"]])[None],
        "rw": halves(g["L0_ffn_router_w"].T),
        "gw": halves(g["L1_ffn_gate_w"]),
        "rrow": _np.concatenate([g["L0_ffn_router_b"], g["L1_ffn_gate_b"]])[None],
        "valid": (_np.arange(NT * P) < N).astype(_np.float32).reshape(NT, P).T,
        "wg1": halves(g["L1_gnn_W"].T),
        "wqkv1": _np.concatenate([halves(g["L1_mix_Wq"].T), halves(g["L1_mix_Wkv"].T)], axis=2),
        "wproj": halves(g["L1_mix_Wproj"].T),
        "e1": g["L0_ffn_W1"],
        "eb1": g["L0_ffn_b1"],
        "e2": _np.concatenate([g["L0_ffn_W2"], g["L0_ffn_b2"][:, None, :]], axis=1),
        "w1": g["L1_ffn_w1"],
        "w2": g["L1_ffn_w2"],
        "b11": g["L1_ffn_b1"].reshape(E1 * MT, P).T,
        "b2": g["L1_ffn_b2"],
    }
    arrays, args = {}, {}
    for name, arr in a.items():
        arr = _np.ascontiguousarray(arr)
        arrays[name + "_dram"] = arr
        args[name] = nc.dram_tensor(name + "_dram", arr.shape, _mybir.dt.from_np(arr.dtype), kind="ExternalInput").ap()
    out = nc.dram_tensor("out_dram", (N, D), F32, kind="ExternalOutput").ap()
    build(nc, args, out)
    r = _run(nc, [arrays], core_ids=[0])
    return r.results[0]["out_dram"]
```

```python
import numpy as np
import concourse.bass as bass
from concourse import mybir
from contextlib import ExitStack

F32 = mybir.dt.float32
I32 = mybir.dt.int32
U32 = mybir.dt.uint32
ALU = mybir.AluOpType
ACT = mybir.ActivationFunctionType
AX = mybir.AxisListType

P = 128
N = 3125
D = 256
KD = D // P
NT = -(-N // P)
TAIL = N - (NT - 1) * P
CT = 5
NC = NT // CT
CN = CT * P
HN = CN // 2
NP = NT * P
E = 50000
GT = 8
GH = GT // 2
GE = GT * P
NG = -(-E // GE)
ET = NG * GT
R = 7
LAG = 1
PARTS = 8
MAXN = NG * NT + 2
H = 8
HD = D // H
HH = P // HD
E0, F0 = 32, 64
NB0 = N // P + E0
E1, F1 = 8, 1024
EW = KD * F0 + D + 1
Q0 = 4
TURN0 = 2 * Q0
CAP = -(-5 * N // (4 * E1))
ST = -(-CAP // P)
STAIL = CAP - (ST - 1) * P
MT = F1 // P
XB1 = 4096
FAR = 1.0e6
IW = 33 * P
DW = GT * P + GT
SENT = -3.0e38
FMAX = 3.4028234e38
AP_ = D + 1


class Chain:

    def __init__(self, eng, sem, idle):
        self.eng, self.sem, self.idle = eng, sem, idle
        self.base, self.k, self.i, self.per = 0, 0, None, 0

    def loop(self, i, per):
        self.base += self.k
        self.i, self.per, self.k = i, per, 0

    def end(self, trips):
        assert self.k == self.per, (self.k, self.per)
        self.base += self.per * trips
        self.i, self.k = None, 0

    def link(self, ins):
        ins.then_inc(self.sem, 1)
        self.k += 1

    def join(self):
        if self.i is None:
            self.eng.wait_ge(self.sem, self.base + self.k)
        else:
            self.eng.wait_ge(self.sem, self.i * self.per + (self.base + self.k))
            self.eng.sem_inc(self.idle, 1)


def build(nc, a, out):
    ctx = ExitStack()
    with ctx:
        def sb(n, s, d=F32):
            return ctx.enter_context(nc.sbuf_tensor(n, s, d))

        def dr(n, s, d=F32):
            return nc.dram_tensor(n, s, d, kind="Internal").ap()

        xnT_d = dr("xnT_d", [P, KD, NP])
        table = [dr("table0", [NP, D]), dr("table1", [NP, D])]
        slots = [dr("slots0", [NB0 * P, D]), dr("slots1", [XB1, D])]
        yslots = [dr("yslots0", [NB0 * P, D]), dr("yslots1", [E1 * CAP, D])]

        X = sb("X", [P, NT, D])
        acc = sb("acc", [P, (NT + 1) * AP_])
        ring = sb("ring", [P, R * GT * AP_])
        iota = sb("iota", [P, IW], mybir.dt.int16)
        TE = sb("TE", [P, 2 * CT * D])
        step = TE[0:NG, 0:MAXN]
        src = sb("src", [P, ET], I32)
        dst = sb("dst", [P, DW])
        stage = sb("stage", [P, R, GT], I32)
        pair_row = sb("pair_row", [1, MAXN], I32)
        g_row = ring[0:1, 0:MAXN]
        w_row = ring[0:1, MAXN:2 * MAXN + 1]
        bi_row = sb("bi_row", [1, NG], I32)
        seg_row = sb("seg_row", [1, NC * PARTS + 1], I32)
        dg = TE[0:NG, 0:GE].bitcast(I32)
        dn = TE[0:NG, GE:2 * GE].bitcast(I32)
        tri = sb("tri", [P, P])
        tris = sb("tris", [P, P])
        ident = sb("ident", [P, P])
        ones = sb("ones", [P, P])
        valid = sb("valid", [P, NT])
        eps = sb("eps", [P, 1])
        sm = sb("sm", [NG, 12])
        smi = sb("smi", [NG, 3], I32)
        lo0 = sb("lo0", [1, 1])
        oh = sb("oh", [P, GT, P])
        st = sb("st", [P, NT, 6])
        mv = sb("mv", [P, NT, 2])
        rs = sb("rs", [P, NT])
        nm = sb("nm", [P, NT])
        sd = sb("sd", [P, NT])
        deg = sb("deg", [P, NT])
        rdeg = sb("rdeg", [P, NT])
        dinv = sb("dinv", [P, NT])
        wn = sb("wn", [P, KD, D])
        ws = sb("ws", [P, KD, D])
        wqkv = sb("wqkv", [P, KD, 3 * D])
        wm1 = sb("wm1", [P, KD, D])
        wm2 = sb("wm2", [P, KD, D])
        lng = sb("lng", [P, 4, D])
        b1c = sb("b1c", [P, KD])
        brow = sb("brow", [1, 3, D])
        XN = sb("XN", [P, CT, D])
        xT = sb("xT", [P, KD, CN])
        Kb = sb("Kb", [P, CT, D])
        Vb = sb("Vb", [P, CT, 2, P + 1])
        tmp = TE[:, 0:CT * D].rearrange("p (j f) -> p j f", f=D)
        ex = TE[:, CT * D:].rearrange("p (j f) -> p j f", f=D)
        Hs = sb("Hs", [P, CT, D])
        Wk = sb("Wk", [P, CT, D])
        m8 = sb("m8", [P, CT, 8])
        KV = sb("KV", [P, 2, P + 1])
        KVb = sb("KVb", [P, 2, P + HH])
        KS = sb("KS", [P, 2, P])
        Mx = sb("Mx", [P, 2, D])
        den = sb("den", [P, CT, 2, HH])
        rw = sb("rw", [P, KD, E0])
        gw = sb("gw", [P, KD, E1])
        rrow = sb("rrow", [1, E0 + E1])
        ps = ctx.enter_context(nc.psum_tensor("ps", [P, 8 * 512], F32))
        B = 512

        def bank(i, w=512, n=1):
            return ps[:, i * B:i * B + w * n]

        QT = Kb[:].rearrange("p j f -> p (j f)")
        X1 = Hs
        CTx = Vb[:, 0, :, 0:P]
        Z = Wk
        HT = Vb[:].rearrange("p j a f -> p (j a f)")[:, 0:KD * CN].rearrange("p (k n) -> p k n", k=KD)
        AG = XN
        XALL = acc[:, 0:NT * D].rearrange("p (t f) -> p t f", f=D)
        a3 = acc[:].rearrange("p (w f) -> p w f", f=AP_)
        ring4 = ring[:].rearrange("p (r j f) -> p r j f", r=R, f=AP_)
        o = [0]

        def take(n, v=None):
            r = ring[:, o[0]:o[0] + n]
            o[0] += n
            return r
        LG = take(NT * E0)
        OH = take(NT * E0)
        TT = take(NT * E0)
        IN = take(NT * E0)
        MSK = take(NT * E0)
        PR = take(NT * E0)
        mx = take(NT * 8)
        mi = take(NT * 8).bitcast(U32)
        mif = take(NT)
        rank = take(NT)
        pos = take(NT)
        kept = take(NT)
        wgt = take(NT)
        t25 = take(NT)
        se = take(NT)
        cntE = take(E0)
        nbE = take(E0)
        nbEi = take(E0).bitcast(I32)
        CE = take(E0)
        baseE = take(E0)
        ebc = take(NB0 * E0)
        ebf = take(NB0)
        sidx = sb("sidx", [P, NT], I32)
        gidx = sb("gidx", [P, NT], I32)
        ebi = sb("ebi", [1, NB0], I32)
        half_set = Q0 * (D + EW)
        home = [ring, acc]

        def xb0(p, h):
            return home[p][:, h * half_set:h * half_set + Q0 * D].rearrange("p (s f) -> p s f", s=Q0)

        def wb0(p, h):
            return home[p][:, h * half_set + Q0 * D:(h + 1) * half_set].rearrange("p (s f) -> p s f", s=Q0)

        def flat3(t):
            return t[:].rearrange("p j f -> p (j f)")
        xbT0 = [flat3(XN)[:, 0:Q0 * D], flat3(Kb)[:, 0:Q0 * D]]
        h0 = flat3(Hs)[:, 0:2 * Q0 * P].rearrange("p (h n) -> p h n", h=2)
        y0 = [flat3(Wk)[:, 0:Q0 * D], flat3(tmp)[:, 0:Q0 * D]]
        w11 = ring[:, 0:2 * KD * F1].rearrange("p (s k f) -> p s k f", s=2, k=KD)
        w21 = ring[:, 2 * KD * F1:4 * KD * F1].rearrange("p (s m f) -> p s m f", s=2, m=MT)
        h1 = acc[:, 0:MT * CAP].rearrange("p (m n) -> p m n", m=MT)
        xb1 = [XN[:, 0:ST, :], Kb[:, 0:ST, :]]
        xb1T = xT[:, :, 0:ST * P]
        y1 = Wk[:, 0:ST, :]
        b11 = sb("b11", [P, E1 * MT])
        b21 = sb("b21", [1, 2, D])
        rt = sb("rt", [P, 8, NT])

        S = {}
        names = """lists_in tail loaded xload consts made prepped ranked listed bounds idle_p idle_a idle_v idle_t idle_s
            dve_chain act_chain pool_chain landed oh_half half_used added agg_done stat stat_sd stat_done
            a_xn a_tr a_xT a_nb a_kvp a_hs a_e a_v a_k a_kv a_kvacc a_sp a_xnT a_tab kv_ready ct_ps ct_sb m_ps m_ready
            b_xs b_q b_e b_u b_qt b_t b_z b_sd1 b_rs1 b_n1 b_x1 b_x1t b_x1T b_h b_g b_y b_z2 b_sd2 b_rs2 b_n2 b_done b_den b_qs b_free
            layer_done c_ag c_tr c_aT c_y c_done deg_ready deg_sd
            r_xn r_tr r_xT r_lg r_lgs r_done r_xall oh_ready mass mass_used routed expd negm zeroed scattered gathered
            e_x e_w e_tr e_xT e_h e_hs e_y e_ys e_out e_done
            f_x f_w1 f_w2 f_b2 f_tr f_xT f_h f_hs f_y f_ys f_out f_hfree outp wload stagep""".split()
        for n in names:
            S[n] = ctx.enter_context(nc.semaphore(n))
        e_in = [[ctx.enter_context(nc.semaphore(f"e_in{p}{h}")) for h in range(2)] for p in range(2)]
        e_put = [ctx.enter_context(nc.semaphore(f"e_put{h}")) for h in range(2)]
        f_in = [ctx.enter_context(nc.semaphore(f"f_in{s}")) for s in range(2)]
        back = [ctx.enter_context(nc.semaphore(f"back{c}")) for c in range(NC)]
        slot_in = [ctx.enter_context(nc.semaphore(f"slot_in{i}")) for i in range(R)]
        NLOAD = 0

        block = ctx.enter_context(nc.Block())

        def v5(L, c):
            return c + (NC * L + 1)

        first = [(oh[:].rearrange("p j n -> p (j n)")[:, 0:ET].bitcast(I32), a["dstT"]), (dg, a["dgrp"]), (dn, a["dnext"])]
        loads = [(wn[:], a["wn"]), (valid[:], a["valid"]), (wqkv[:], a["wqkv0"]), (brow[:, 0, :], a["mb2"]), (brow[:, 1:3, :], a["b1rows"]), (src[:], a["srcT"]),
                 (ws[:], a["ws"]), (wm1[:], a["wm1"]), (wm2[:], a["wm2"]), (lng[:], a["lng"]), (b1c[:], a["b1c"]), (rw[:], a["rw"]), (gw[:], a["gw"]),
                 (rrow[:], a["rrow"]), (b11[:], a["b11"])]

        @block.sync
        def _(sp):
            def held(sem, val):
                sp.wait_ge(S[sem], val)
                sp.sem_inc(S["idle_s"], 1)

            for d, s in first:
                sp.dma_start(d, s).then_inc(S["lists_in"], 16)
            sp.wait_ge(S["tail"], 1)
            for c in range(NC):
                last = c == NC - 1
                n = CT - 1 if last else CT
                sp.dma_start(X[:, c * CT:c * CT + n, :], a["x"][c * CN:c * CN + n * P, :].rearrange("(j p) f -> p j f", p=P)).then_inc(S["xload"], 16)
            sp.dma_start(X[0:TAIL, NT - 1, :], a["x"][(NT - 1) * P:N, :]).then_inc(S["xload"], 16)
            for d, s in loads:
                sp.dma_start(d, s).then_inc(S["loaded"], 16)

            for L in range(2):
                def put(c, clear):
                    held("a_xT", v5(L, c))
                    sp.dma_start(xnT_d[:, :, bass.ds(c * CN, CN)], xT[:]).then_inc(S["a_xnT"], 16)
                    if clear:
                        for z in slots:
                            z = z.rearrange("(p r) f -> p (r f)", p=P)
                            w = z.shape[1] // (NC - 1)
                            sp.dma_start(z[:, bass.ds(c * w, w)], acc[:, 0:w]).then_inc(S["zeroed"], 16)
                    held("a_sp", v5(L, c))
                    sp.dma_start(table[L][bass.ds(c * CN, CN), :].rearrange("(j p) f -> p j f", p=P), Hs[:]).then_inc(S["a_tab"], 16)

                with sp.Fori(0, NC - 1) as c:
                    put(c, L == 0)
                put(NC - 1, False)
                sp.wait_ge(S["a_xnT"], 16 * NC * (L + 1) + 16)
                sp.wait_ge(S["kv_ready"], L + 1)
                with sp.Fori(0, NC) as c:
                    held("b_y", v5(L, c))
                    sp.dma_start(xT[:], xnT_d[:, :, bass.ds(c * CN, CN)]).then_inc(S["b_xs"], 16)
                if L == 0:
                    sp.wait_ge(S["layer_done"], 1)
                    sp.dma_start(wn[:], a["wg1"]).then_inc(S["wload"], 16)
                    sp.dma_start(wqkv[:], a["wqkv1"]).then_inc(S["wload"], 16)
                    sp.dma_start(wm1[:], a["wproj"]).then_inc(S["wload"], 16)
                    sp.wait_ge(S["scattered"], 16 * NT)

                    def load(q, p):
                        for h in range(2):
                            sp.dma_start(xb0(p, h), slots[0][bass.ds(q * (TURN0 * P) + h * (Q0 * P), Q0 * P), :].rearrange("(s p) f -> p s f", p=P)).then_inc(e_in[p][h], 16)
                            for s in range(Q0):
                                e = sp.value_load(ebi[0:1, bass.ds(q * TURN0 + (h * Q0 + s), 1)], min_val=0, max_val=E0 - 1)
                                sp.dma_start(wb0(p, h)[:, s, :], a["ew"][bass.ds(e, 1), :, :].rearrange("e p f -> p (e f)")).then_inc(e_in[p][h], 16)

                    def store(q):
                        for h in range(2):
                            held("e_ys", q * 2 + (h + 2))
                            sp.dma_start(yslots[0][bass.ds(q * (TURN0 * P) + h * (Q0 * P), Q0 * P), :].rearrange("(s p) f -> p s f", p=P),
                                         y0[h].rearrange("p (s f) -> p s f", s=Q0)).then_inc(e_put[h], 16)

                    load(0, 0)
                    with sp.Fori(0, NB0 // TURN0 // 2) as i:
                        for p in range(2):
                            q = i * 2 + p
                            held("e_y", q * 2 + 1)
                            load(q + 1, 1 - p)
                            store(q)
                    store(NB0 // TURN0 - 1)
                else:
                    def load_w(e, s):
                        sp.dma_start(w11[:, s], a["w1"][bass.ds(e, 1), :, :].rearrange("e (k p) f -> p (e k) f", p=P)).then_inc(f_in[s], 16)
                        sp.dma_start(w21[:, s], a["w2"][bass.ds(e, 1), :, :].rearrange("e (m p) f -> p (e m) f", p=P)).then_inc(f_in[s], 16)
                        sp.dma_start(b21[:, s, :], a["b2"][bass.ds(e, 1), :]).then_inc(f_in[s], 16)

                    def load_x(e, s):
                        sp.dma_start(xb1[s][:, 0:ST - 1, :], slots[1][bass.ds(e * CAP, (ST - 1) * P), :].rearrange("(t p) f -> p t f", p=P)).then_inc(f_in[s], 16)
                        sp.dma_start(xb1[s][0:STAIL, ST - 1, :], slots[1][bass.ds(e * CAP + (ST - 1) * P, STAIL), :]).then_inc(f_in[s], 16)

                    def store(e):
                        held("f_ys", e + 2)
                        sp.dma_start(yslots[1][bass.ds(e * CAP, (ST - 1) * P), :].rearrange("(t p) f -> p t f", p=P), y1[:, 0:ST - 1, :]).then_inc(S["f_out"], 16)
                        sp.dma_start(yslots[1][bass.ds(e * CAP + (ST - 1) * P, STAIL), :], y1[0:STAIL, ST - 1, :]).then_inc(S["f_out"], 16)

                    sp.wait_ge(S["routed"], 2)
                    load_w(0, 0)
                    sp.wait_ge(S["scattered"], 32 * NT)
                    load_x(0, 0)
                    with sp.Fori(0, E1 // 2 - 1) as i:
                        for s in range(2):
                            e = i * 2 + s
                            held("f_ys", e + 1)
                            load_w(e + 1, 1 - s)
                            load_x(e + 1, 1 - s)
                            store(e)
                    sp.wait_ge(S["f_ys"], E1 - 2 + 1)
                    load_w(E1 - 1, 1)
                    load_x(E1 - 1, 1)
                    store(E1 - 2)
                    store(E1 - 1)
            for c in range(NC):
                n = CT - 1 if c == NC - 1 else CT
                sp.wait_ge(S["layer_done"], 3 + c)
                sp.dma_start(out[c * CN:c * CN + n * P, :].rearrange("(j p) f -> p j f", p=P), X[:, c * CT:c * CT + n, :]).then_inc(S["outp"], 16)
            sp.dma_start(out[(NT - 1) * P:N, :], X[0:TAIL, NT - 1, :]).then_inc(S["outp"], 16)
            sp.wait_ge(S["outp"], 16 * (NC + 1))

        @block.gpsimd
        def _(gp):
            gp.memset(X[:, NT - 1, :], 0.0).then_inc(S["tail"], 1)
            gp.iota(iota[:], pattern=[[1, IW]], base=0, channel_multiplier=0, allow_small_or_imprecise_dtypes=True).then_inc(S["consts"], 1)
            gp.memset(tri[:], 1.0).then_inc(S["consts"], 1)
            gp.memset(tris[:], 1.0).then_inc(S["consts"], 1)
            gp.memset(ident[:], 0.0).then_inc(S["consts"], 1)
            gp.memset(ones[:], 1.0).then_inc(S["consts"], 1)
            gp.memset(eps[:], 1e-5).then_inc(S["consts"], 1)
            gp.memset(acc[:], 0.0).then_inc(S["consts"], 1)
            gp.wait_ge(S["consts"], 7)
            gp.affine_select(out=tri[:], in_=tri[:], compare_op=ALU.is_ge, fill=0.0, base=0, pattern=[[1, P]], channel_multiplier=-1).then_inc(S["made"], 1)
            gp.affine_select(out=tris[:], in_=tris[:], compare_op=ALU.is_gt, fill=0.0, base=0, pattern=[[1, P]], channel_multiplier=-1).then_inc(S["made"], 1)
            gp.affine_select(out=ident[:], in_=ident[:], compare_op=ALU.not_equal, fill=1.0, base=0, pattern=[[-1, P]], channel_multiplier=1).then_inc(S["made"], 1)
            gp.wait_ge(S["loaded"], 16 * len(loads))
            gp.wait_ge(S["listed"], -(-MAXN // 512) + 1)

            for L in range(2):
                gp.wait_ge(S["a_tab"], 16 * NC * (L + 1) + 16)

                def fetch(g, b):
                    gp.tensor_copy(stage[:, b, :], src[:, bass.ds(g * GT, GT)]).then_inc(S["stagep"], 1)
                    gp.wait_ge(S["stagep"], g + (1 + NG * L))
                    gp.sem_inc(S["idle_p"], 1)
                    for j in range(GT):
                        gp.indirect_dma_start(ring4[:, b, j, 0:D], None, table[L], bass.IndirectOffsetOnAxis(ap=stage[:, b, j:j + 1], axis=0)).then_inc(slot_in[b], 16)

                def arrived(b, turn):
                    before = L * (NG // R + (1 if b < NG % R else 0))
                    gp.wait_ge(slot_in[b], (turn + (before + 1)) * (16 * GT))
                    gp.sem_inc(S["landed"], 1)

                def freed(gprev, base):
                    n = gp.value_load(bi_row[0:1, gprev], min_val=1, max_val=MAXN)
                    gp.wait_ge(S["half_used"], n * 2 + base)
                    gp.sem_inc(S["idle_p"], 1)

                if L == 1:
                    ntot = gp.value_load(bi_row[0:1, NG - 1:NG], min_val=1, max_val=MAXN)
                    off = gp.snap(ntot * 2 + 2)
                else:
                    off = 2
                for g in range(R):
                    fetch(g, g)
                    if g >= LAG:
                        arrived(g - LAG, 0)
                with gp.Fori(1, NG // R) as r:
                    for b in range(R):
                        freed(bass.ds((r - 1) * R + b, 1), off)
                        fetch(r * R + b, b)
                        arrived((b - LAG) % R, r if b >= LAG else r - 1)
                for g in range(NG // R * R, NG):
                    freed(bass.ds(g - R, 1), off)
                    fetch(g, g % R)
                    arrived((g - LAG) % R, (g - LAG) // R)
                for g in range(NG - LAG, NG):
                    arrived(g % R, g // R)
                gp.wait_ge(S["routed"], L + 1)
                gp.wait_ge(S["r_xall"], 1 + NC * (L + 1))
                gp.wait_ge(S["zeroed"], 16 * 2 * (NC - 1))
                for t in range(NT):
                    gp.indirect_dma_start(slots[L], bass.IndirectOffsetOnAxis(ap=sidx[:, t:t + 1], axis=0), XALL[:, t, :], None,
                                          bounds_check=slots[L].shape[0] - 1, oob_is_err=False).then_inc(S["scattered"], 16)
                if L == 0:
                    for h in range(2):
                        gp.wait_ge(e_put[h], 16 * (NB0 // TURN0) + 16)
                else:
                    gp.wait_ge(S["f_out"], 32 * E1 + 16)
                for t in range(NT):
                    gp.indirect_dma_start(XALL[:, t, :], None, yslots[L], bass.IndirectOffsetOnAxis(ap=gidx[:, t:t + 1], axis=0)).then_inc(back[t // CT], 16)

        @block.scalar
        def _(ac):
            ch = Chain(ac, S["act_chain"], S["idle_a"])
            for n, k in (("a_kvacc", 1), ("b_done", 1), ("e_y", 1), ("e_ys", 1), ("f_ys", 1), ("r_done", 1), ("half_used", 2), ("b_y", 1), ("b_free", 1),
                         ("added", 1), ("a_xnT", 16), ("a_tab", 16), ("f_hs", 4), ("f_out", 16), ("c_done", 1), ("a_sp", 0), ("r_xall", 1)):
                if k:
                    ac.sem_inc(S[n], k)
            for h in range(2):
                ac.sem_inc(e_put[h], 16)
            ac.wait_ge(S["consts"], 7)
            ac.wait_ge(S["loaded"], 16 * len(loads))

            def held(sem, val):
                ac.wait_ge(S[sem], val)
                ac.sem_inc(S["idle_a"], 1)

            def landed(L):
                pass

            def root(k):
                ac.wait_ge(S["stat"], k)
                ac.activation(sd[:], mv[:, :, 1], ACT.Sqrt, bias=eps[:]).then_inc(S["stat_sd"], 1)

            def copyT(sem_in, sem_out, val, at=0):
                held(sem_in, val)
                for k in range(KD):
                    i = ac.activation(xT[:, k, :], ps[:, at + k * 1024:at + k * 1024 + CN], ACT.Copy)
                    if k == KD - 1:
                        i.then_inc(S[sem_out], 1)

            for L in range(2):
                if L == 1:
                    ac.wait_ge(S["deg_ready"], 1)
                    ac.activation(dinv[:], deg[:], ACT.Sqrt, bias=ones[:, 0:1]).then_inc(S["deg_sd"], 1)
                root(2 * L + 1)
                ac.wait_ge(S["made"], 3)
                with ac.Fori(0, NC) as c:
                    ch.loop(c, 1)
                    held("a_xnT", (c + NC * L + 1) * 16)
                    copyT("a_tr", "a_xT", v5(L, c), 2 * B)
                    held("a_tab", v5(L, c) * 16)
                    held("a_nb", v5(L, c))
                    if L == 0:
                        ac.activation(Hs[:].rearrange("p j f -> p (j f)"), ps[:, 5 * B:5 * B + CT * D], ACT.Copy).then_inc(S["a_hs"], 1)
                    else:
                        for j in range(CT):
                            i = ac.activation(Hs[:, j, :], ps[:, 5 * B + j * D:5 * B + (j + 1) * D], ACT.Copy, scale=dinv[:, bass.ds(c * CT + j, 1)])
                        i.then_inc(S["a_hs"], 1)
                    held("a_kvp", v5(L, c))
                    k_ps = ps[:, 0:CT * B].rearrange("p (j f) -> p j f", f=B)
                    ch.link(ac.activation(tmp[:], k_ps[:, :, 0:D], ACT.Relu, scale=-1.0))
                    ch.join()
                    ac.activation(ex[:], tmp[:], ACT.Exp, scale=-1.0).then_inc(S["a_e"], 1)
                    for j in range(CT):
                        i = ac.activation(Vb[:, j, :, 0:P], k_ps[:, j, D:2 * D].rearrange("p (a f) -> p a f", a=2), ACT.Copy, scale=valid[:, bass.ds(c * CT + j, 1)])
                    i.then_inc(S["a_v"], 1)
                ch.end(NC)
                if L == 1:
                    ac.wait_ge(S["ct_ps"], 1)
                    ac.activation(CTx, bank(0, D).rearrange("p (a f) -> p a f", a=2), ACT.Copy).then_inc(S["ct_sb"], 1)
                    ac.wait_ge(S["m_ps"], 1)
                    ac.activation(Mx[:].rearrange("p a f -> p (a f)"), bank(1, 512), ACT.Copy).then_inc(S["m_ready"], 1)
                with ac.Fori(0, NC) as c:
                    ch.loop(c, 1)
                    q_ps = ps[:, 0:4 * B].rearrange("p (q n) -> p q n", n=B)[:, :, 0:HN]
                    t4 = tmp[:].rearrange("p j f -> p (j f)").rearrange("p (q n) -> p q n", q=4)
                    e4 = ex[:].rearrange("p j f -> p (j f)").rearrange("p (q n) -> p q n", q=4)
                    held("b_done", v5(L, c))
                    held("b_q", v5(L, c))
                    ch.link(ac.activation(t4, q_ps, ACT.Relu, scale=-1.0))
                    ch.join()
                    ac.activation(e4, t4, ACT.Exp, scale=-1.0).then_inc(S["b_e"], 1)
                    if L == 0:
                        for j in range(CT):
                            i = ac.activation(XN[:, j, :], X[:, bass.ds(c * CT + j, 1), :].rearrange("p a f -> p (a f)"), ACT.Identity,
                                              scale=rs[:, bass.ds(c * CT + j, 1)], bias=nm[:, bass.ds(c * CT + j, 1)])
                        i.then_inc(S["b_u"], 1)

                        def norm(z, w, r):
                            held(z, c + 1)
                            ac.activation(rt[:, 1, 0:CT], rt[:, 0, 0:2 * CT].rearrange("p (j s) -> p j s", s=2)[:, :, 1], ACT.Sqrt, bias=eps[:]).then_inc(S[w], 1)
                            held(r, c + 1)

                        norm("b_z", "b_sd1", "b_rs1")
                        for j in range(CT):
                            i = ac.activation(tmp[:, j, :], Z[:, j, :], ACT.Identity, scale=rt[:, 2, j:j + 1], bias=rt[:, 3, j:j + 1])
                        i.then_inc(S["b_n1"], 1)
                        held("b_x1t", c + 1)
                        for k in range(KD):
                            i = ac.activation(QT[:, k * CN:(k + 1) * CN], ps[:, k * 1024:k * 1024 + CN], ACT.Copy)
                        i.then_inc(S["b_x1T"], 1)
                        held("b_h", c + 1)
                        for m in range(KD):
                            i = ac.activation(HT[:, m, :].rearrange("p (q n) -> p q n", q=2), q_ps[:, 2 * m:2 * m + 2, :], ACT.Gelu, bias=b1c[:, m:m + 1])
                        i.then_inc(S["b_g"], 1)
                        norm("b_z2", "b_sd2", "b_rs2")
                        for j in range(CT):
                            i = ac.activation(tmp[:, j, :], Z[:, j, :], ACT.Identity, scale=rt[:, 2, j:j + 1], bias=rt[:, 3, j:j + 1])
                        i.then_inc(S["b_n2"], 1)
                ch.end(NC)
                root(2 * L + 2)
                with ac.Fori(0, NC) as c:
                    held("r_xn", v5(L, c))
                    ac.activation(acc[:, bass.ds(c * CT * D, CT * D)], XN[:].rearrange("p j f -> p (j f)"), ACT.Copy).then_inc(S["r_xall"], 1)
                    copyT("r_tr", "r_xT", v5(L, c))
                if L == 1:
                    ac.wait_ge(S["negm"], 1)
                    ac.activation(LG[:, 0:NT * E1], LG[:, 0:NT * E1], ACT.Exp).then_inc(S["expd"], 1)
                if L == 0:
                    def turn(q, p):
                        for h in range(2):
                            held("e_tr", q * 2 + (h + 1))
                            ac.activation(xbT0[h], ps[:, 2 * h * B:2 * h * B + Q0 * D], ACT.Copy).then_inc(S["e_xT"], 1)
                        for h in range(2):
                            held("e_h", q * 2 + (h + 1))
                            for s in range(Q0):
                                i = ac.activation(h0[0:F0, h, s * P:(s + 1) * P], ps[0:F0, (4 + h) * B + s * P:(4 + h) * B + (s + 1) * P], ACT.Relu, bias=wb0(p, h)[0:F0, s, EW - 1:EW])
                            i.then_inc(S["e_hs"], 1)

                    with ac.Fori(0, NB0 // TURN0 // 2) as i2:
                        for p in range(2):
                            turn(i2 * 2 + p, p)
                    turn(NB0 // TURN0 - 1, 0)
                else:
                    with ac.Fori(0, E1 // 2) as i2:
                        for s in range(2):
                            e = i2 * 2 + s
                            held("f_tr", e + 1)
                            ac.activation(xb1T[:, :, 0:CAP], ps[:, 0:2 * B].rearrange("p (k n) -> p k n", k=2)[:, :, 0:CAP], ACT.Copy).then_inc(S["f_xT"], 1)
                            for m in range(MT):
                                held("f_h", e * MT + (m + 1))
                                ac.activation(h1[:, m, :], ps[:, (2 + m % 4) * B:(2 + m % 4) * B + CAP], ACT.Relu, bias=b11[:, bass.ds(e * MT + m, 1)]).then_inc(S["f_hs"], 1)

        @block.vector
        def _(v):
            ch = Chain(v, S["dve_chain"], S["idle_v"])

            def do(ins):
                ch.link(ins)
                ch.join()

            def held(sem, val):
                v.wait_ge(S[sem], val)
                v.sem_inc(S["idle_v"], 1)

            def flat(t):
                return t[:].rearrange("p j f -> p (j f)")

            def rows(c, j=None):
                return X[:, bass.ds(c * CT, CT), :].rearrange("p j f -> p (j f)") if j is None else X[:, bass.ds(c * CT + j, 1), :].rearrange("p a f -> p (a f)")

            def stats(k):
                for t in range(NT):
                    ch.link(v.bn_stats(st[:, t, :], X[:, t, :]))
                ch.join()
                for t in range(NT):
                    i = v.bn_aggr(mv[:, t, :], st[:, t, :])
                    if t < NT - 1:
                        ch.link(i)
                i.then_inc(S["stat"], 1)
                v.wait_ge(S["stat_sd"], k)
                do(v.reciprocal(rs[:], sd[:]))
                do(v.scalar_tensor_tensor(nm[:], mv[:, :, 0], -1.0, rs[:], ALU.mult, ALU.mult))

            def normed(c, sem):
                for j in range(CT):
                    i = v.tensor_scalar(XN[:, j, :], rows(c, j), mv[:, bass.ds(c * CT + j, 1), 0], rs[:, bass.ds(c * CT + j, 1)], ALU.subtract, ALU.mult)
                i.then_inc(S[sem], 1)

            v.wait_ge(S["consts"], 7)
            v.wait_ge(S["made"], 3)
            v.wait_ge(S["lists_in"], 16 * len(first))
            lo, hi, ln, cnt, delta, bi = (sm[:, i:i + 1] for i in range(6))
            do(v.memset(dst[:], -1.0))
            do(v.tensor_copy(dst[:, 0:ET], oh[:].rearrange("p j n -> p (j n)")[:, 0:ET].bitcast(I32)))
            ch.link(v.tensor_reduce(smi[:, 0:1], dg, AX.X, ALU.min))
            ch.link(v.tensor_reduce(smi[:, 1:2], dg, AX.X, ALU.max))
            do(v.tensor_reduce(smi[:, 2:3], dn, AX.X, ALU.min))
            do(v.tensor_scalar(smi[:], smi[:], 7, None, ALU.arith_shift_right))
            do(v.tensor_copy(sm[:, 0:3], smi[:]))
            ch.link(v.tensor_copy(lo0[:], sm[0:1, 0:1]))
            ch.link(v.scalar_tensor_tensor(cnt, hi, 1.0, lo, ALU.add, ALU.subtract))
            do(v.scalar_tensor_tensor(delta, ln, -1.0, hi, ALU.add, ALU.subtract))
            v.sem_inc(S["prepped"], 1)
            v.wait_ge(S["ranked"], 1)
            do(v.tensor_copy(bi, ps[0:NG, 0:1]))
            do(v.tensor_copy(bi_row[:], ps[0:1, 4:4 + NG]))
            ch.link(v.memset(seg_row[:, 0:1], 0))
            for k in range(1, NC * PARTS + 1):
                g = NG * k // (NC * PARTS) - 1
                ch.link(v.tensor_copy(seg_row[:, k:k + 1], bi_row[:, g:g + 1]))
            ch.link(v.memset(w_row[:, 0:1], NT))
            do(v.tensor_scalar(step, iota[0:NG, 0:MAXN], bi, None, ALU.is_ge))
            v.sem_inc(S["prepped"], 1)
            for k, q in enumerate(range(0, MAXN, 512)):
                m = min(512, MAXN - q)
                v.wait_ge(S["ranked"], 2 + k)
                ch.link(v.tensor_scalar(g_row[0:1, q:q + m], ps[0:1, 0:m], float(NG - 1), None, ALU.min))
                do(v.scalar_tensor_tensor(w_row[0:1, 1 + q:1 + q + m], ps[0:1, B:B + m], lo0[0:1, 0:1], iota[0:1, q:q + m], ALU.add, ALU.add))
                v.sem_inc(S["listed"], 1)
            ch.link(v.memset(KV[:], 0.0))
            do(v.scalar_tensor_tensor(g_row, g_row, float(1 << 5), w_row[:, 1:MAXN + 1], ALU.mult, ALU.add))
            do(v.tensor_scalar(g_row, g_row, float(1 << 7), None, ALU.mult))
            do(v.scalar_tensor_tensor(pair_row[:], w_row[:, 0:MAXN], float(1 << 19), g_row, ALU.mult, ALU.add))
            do(v.memset(ring4[:, :, :, D:AP_], 1.0))
            do(v.memset(ps[:, 6 * B:8 * B], 0.0))
            v.sem_inc(S["listed"], 1)
            v.wait_ge(S["loaded"], 16 * len(loads))
            do(v.tensor_tensor(brow[0:1, 1, :], brow[0:1, 1, :], brow[0:1, 2, :], ALU.add))
            v.wait_ge(S["xload"], 16 * (NC + 1))

            def segment(L, c, n0, k0, k1):
                s0 = v.value_load(seg_row[0:1, bass.ds(c * PARTS + k0, 1)], min_val=0, max_val=MAXN)
                s1 = v.value_load(seg_row[0:1, bass.ds(c * PARTS + k1, 1)], min_val=1, max_val=MAXN)
                with v.Fori(s0, s1) as n:
                    pr = v.value_load(pair_row[0:1, bass.ds(n, 1)], min_val=0, max_val=((NT + 1) << 19) - 1)
                    g4 = v.snap(pr // (1 << 12) % 128 * GT, min_val=0, max_val=(NG - 1) * GT)
                    w128 = v.snap(pr % 4096, min_val=0, max_val=NT * P)
                    wp = v.snap(pr // (1 << 19) * AP_, min_val=0, max_val=NT * AP_)
                    for h in range(2):
                        v.wait_ge(S["half_used"], (n + n0) * 2 + (h + 1))
                        v.tensor_tensor(oh[:, GH * h:GH * (h + 1), :], iota[:, bass.ds(w128, P)].unsqueeze(1).to_broadcast([P, GH, P]),
                                        dst[:, bass.ds(g4 + GH * h, GH)].unsqueeze(2).to_broadcast([P, GH, P]), ALU.is_equal).then_inc(S["oh_half"], 1)
                    v.wait_ge(S["added"], n + n0 + (1 + L))
                    r = acc[:, bass.ds(wp, AP_)]
                    v.tensor_tensor(r, r, ps[:, bass.ds(((n + n0 + 1) % 2) * B + 6 * B, AP_)], ALU.add).then_inc(S["added"], 1)

            for L in range(2):
                nE, nF = (E0, E1)[L], 0
                stats(2 * L + 1)
                if L == 1:
                    v.wait_ge(S["deg_sd"], 1)
                    do(v.reciprocal(dinv[:], dinv[:]))
                    do(v.memset(KV[:], 0.0))
                k_ps = ps[:, 0:CT * B].rearrange("p (j f) -> p j f", f=B)[:, :, 0:D]
                kv_ps = ps[:, 0:2 * B].rearrange("p (a f) -> p a f", a=2)[:, :, 0:P + 1]

                def messages(c, more):
                    held("a_hs", c + 1)
                    for q in range(2):
                        ch.link(v.tensor_copy(Vb[:, :, q, P], valid[:, bass.ds(c * CT, CT)]))
                    for r in range(4):
                        for j in range(CT):
                            i = v.max(m8[:, j, :], (Hs if r == 0 else Wk)[:, j, :])
                        do(i)
                        for j in range(CT):
                            i = v.match_replace(Wk[:, j, :], m8[:, j, :], (Hs if r == 0 else Wk)[:, j, :], SENT)
                        do(i)
                        if r == 0 and more:
                            normed(c + 1, "a_xn")
                        if r == 2:
                            held("a_v", c + 1)
                            v.scalar_tensor_tensor(Kb[:], k_ps, 0.0, ex[:], ALU.max, ALU.add).then_inc(S["a_k"], 1)
                    do(v.tensor_tensor(flat(Wk), flat(Wk), flat(Hs), ALU.not_equal))
                    v.tensor_tensor(flat(Hs), flat(Wk), flat(Hs), ALU.mult).then_inc(S["a_sp"], 1)

                def scaled(c, more):
                    for q in range(2):
                        ch.link(v.tensor_copy(Vb[:, :, q, P], valid[:, bass.ds(c * CT, CT)]))
                    held("a_hs", v5(L, c))
                    v.tensor_copy(a3[:, bass.ds(c * CT, CT), 0:D], Hs[:]).then_inc(S["a_sp"], 1)
                    held("a_v", v5(L, c))
                    v.scalar_tensor_tensor(Kb[:], k_ps, 0.0, ex[:], ALU.max, ALU.add).then_inc(S["a_k"], 1)
                    if more:
                        normed(c + 1, "a_xn")

                def keys_values(c):
                    held("a_kv", v5(L, c))
                    v.tensor_tensor(KV[:], KV[:], kv_ps, ALU.add).then_inc(S["a_kvacc"], 1)
                    v.wait_ge(S["a_kvacc"], v5(L, c) + 1)
                    v.sem_inc(S["idle_v"], 1)

                normed(0, "a_xn")
                with v.Fori(0, NC - 1) as c:
                    ch.loop(c, 11 if L == 0 else 2)
                    (messages, scaled)[L](c, True)
                    keys_values(c)
                ch.end(NC - 1)
                (messages, scaled)[L](NC - 1, False)
                keys_values(NC - 1)
                do(v.memset(KVb[:], 0.0))
                do(v.memset(KS[:], 0.0))
                for q in range(2):
                    for h in range(HH):
                        r = slice(HD * h, HD * (h + 1))
                        ch.link(v.tensor_copy(KVb[r, q, HD * h:HD * (h + 1)], KV[r, q, HD * h:HD * (h + 1)]))
                        ch.link(v.tensor_copy(KVb[r, q, P + h:P + h + 1], KV[r, q, P:P + 1]))
                        ch.link(v.tensor_copy(KS[r, q, HD * h:HD * (h + 1)], KV[r, q, P:P + 1].to_broadcast([HD, HD])))
                ch.join()
                v.sem_inc(S["kv_ready"], 1)
                n0 = 0
                if L == 1:
                    n0 = v.snap(v.value_load(bi_row[0:1, NG - 1:NG], min_val=NG, max_val=MAXN))
                    v.memset(ps[:, 6 * B:8 * B], 0.0).then_inc(S["listed"], 1)
                    v.wait_ge(S["listed"], -(-MAXN // 512) + 2)
                else:
                    v.wait_ge(S["zeroed"], 16 * 2 * (NC - 1))
                with v.Fori(0, NC) as c:
                    q_ps = ps[:, 0:4 * B].rearrange("p (q n) -> p q n", n=B)[:, :, 0:HN]
                    q4 = QT.rearrange("p (q n) -> p q n", q=4)
                    e4 = flat(ex).rearrange("p (q n) -> p q n", q=4)
                    segment(L, c, n0, 0, (1, 3)[L])
                    held("b_e", v5(L, c))
                    v.scalar_tensor_tensor(q4, q_ps, 0.0, e4, ALU.max, ALU.add).then_inc(S["b_qt"], 1)
                    if L == 0:
                        ch.loop(c, 14)
                        segment(L, c, n0, 1, 2)
                        held("b_t", c + 1)
                        t_ps = ps[:, 0:CT * B].rearrange("p (j f) -> p j f", f=B)[:, :, 0:2 * (P + HH)].rearrange("p j (a f) -> p j a f", a=2)
                        do(v.tensor_scalar(den[:], t_ps[:, :, :, P:P + HH], 1e-6, None, ALU.add))
                        do(v.reciprocal(den[:], den[:]))
                        for j in range(CT):
                            i = v.tensor_tensor(Hs[:, j, :].rearrange("p (a h f) -> p a h f", a=2, h=HH),
                                                t_ps[:, j, :, 0:P].rearrange("p a (h f) -> p a h f", h=HH),
                                                den[:, j].unsqueeze(3).to_broadcast([P, 2, HH, HD]), ALU.mult)
                        do(i)
                        held("b_u", c + 1)
                        do(v.tensor_tensor(flat(Z), flat(Hs), flat(XN), ALU.add))

                        def norm(z, w, r, n, gi, last, k):
                            for j in range(CT):
                                i = v.bn_stats(st[:, j, :], Z[:, j, :])
                            do(i)
                            for j in range(CT):
                                i = v.bn_aggr(rt[:, 0, 2 * j:2 * j + 2], st[:, j, :])
                            i.then_inc(S[z], 1)
                            segment(L, c, n0, k, k + 1)
                            held(w, c + 1)
                            do(v.reciprocal(rt[:, 2, 0:CT], rt[:, 1, 0:CT]))
                            v.scalar_tensor_tensor(rt[:, 3, 0:CT], rt[:, 0, 0:2 * CT].rearrange("p (j s) -> p j s", s=2)[:, :, 0], -1.0,
                                                   rt[:, 2, 0:CT], ALU.mult, ALU.mult).then_inc(S[r], 1)
                            segment(L, c, n0, k + 1, k + 2)
                            held(n, c + 1)
                            do(v.tensor_tensor(tmp[:], tmp[:], lng[:, gi, :].unsqueeze(1).to_broadcast([P, CT, D]), ALU.mult))
                            return v.tensor_tensor(last, tmp[:], lng[:, gi + 1, :].unsqueeze(1).to_broadcast([P, CT, D]), ALU.add)

                        norm("b_z", "b_sd1", "b_rs1", "b_n1", 0, X1[:], 2).then_inc(S["b_x1"], 1)
                        segment(L, c, n0, 4, 6)
                        held("b_y", c + 2)
                        do(v.tensor_tensor(flat(Z), flat(X1), ps[:, 0:CT * D], ALU.add))
                        do(v.tensor_tensor(rows(c), rows(c), ps[:, 3 * B:3 * B + CT * D], ALU.add))
                        v.sem_inc(S["b_free"], 1)
                        do(norm("b_z2", "b_sd2", "b_rs2", "b_n2", 2, tmp[:], 6))
                        do(v.tensor_tensor(rows(c), rows(c), flat(tmp), ALU.add))
                        v.sem_inc(S["b_done"], 1)
                    else:
                        ch.loop(c, 2)
                        segment(L, c, n0, 3, 5)
                        held("b_den", c + 1)
                        do(v.tensor_scalar(e4, q_ps, 1e-6, None, ALU.max))
                        do(v.reciprocal(flat(ex), flat(ex)))
                        v.tensor_tensor(QT, QT, flat(ex), ALU.mult).then_inc(S["b_qs"], 1)
                        segment(L, c, n0, 5, 7)
                        held("b_y", c + (NC + 2))
                        v.tensor_tensor(rows(c), rows(c), ps[:, 0:CT * D], ALU.add).then_inc(S["b_free"], 1)
                        v.sem_inc(S["b_done"], 1)
                        segment(L, c, n0, 7, 8)
                ch.end(NC)
                nl = v.value_load(bi_row[0:1, NG - 1:NG], min_val=NG, max_val=MAXN - 2)
                pr = v.value_load(pair_row[0:1, bass.ds(nl, 1)], min_val=0, max_val=((NT + 1) << 19) - 1)
                w = v.snap(pr // (1 << 19), min_val=0, max_val=NT)
                v.wait_ge(S["half_used"], (nl + n0) * 2 + 2)
                v.sem_inc(S["idle_v"], 1)
                v.wait_ge(S["added"], nl + n0 + (1 + L))
                r = acc[:, bass.ds(w * AP_, AP_)]
                v.tensor_tensor(r, r, ps[:, bass.ds(((nl + n0 + 1) % 2) * B + 6 * B, AP_)], ALU.add).then_inc(S["added"], 1)
                v.wait_ge(S["added"], nl + n0 + (2 + L))
                v.sem_inc(S["agg_done"], 1)
                if L == 0:
                    do(v.tensor_copy(deg[:], a3[:, 0:NT, D]))
                    v.sem_inc(S["deg_ready"], 1)
                    do(v.tensor_scalar(rdeg[:], deg[:], 1.0, None, ALU.max))
                    do(v.reciprocal(rdeg[:], rdeg[:]))
                    with v.Fori(0, NC) as c:
                        for j in range(CT):
                            i = v.scalar_tensor_tensor(rows(c, j), acc[:, bass.ds((c * CT + j) * AP_, D)], rdeg[:, bass.ds(c * CT + j, 1)], rows(c, j), ALU.mult, ALU.add)
                        ch.loop(c, 1)
                        ch.link(i)
                    ch.end(NC)
                    ch.join()
                    v.sem_inc(S["layer_done"], 1)
                else:
                    with v.Fori(0, NC) as c:
                        for j in range(CT):
                            i = v.scalar_tensor_tensor(rows(c, j), acc[:, bass.ds((c * CT + j) * AP_, D)], dinv[:, bass.ds(c * CT + j, 1)], rows(c, j), ALU.mult, ALU.add)
                        ch.loop(c, 1)
                        ch.link(i)
                    ch.end(NC)
                    ch.join()
                stats(2 * L + 2)
                with v.Fori(0, NC) as c:
                    held("r_done", v5(L, c))
                    held("r_xall", v5(L, c))
                    normed(c, "r_xn")
                    held("r_lg", v5(L, c))
                    v.tensor_copy(LG[:, bass.ds(c * (CT * nE), CT * nE)], ps[:, 4 * B:4 * B + CT * nE]).then_inc(S["r_lgs"], 1)
                v.wait_ge(S["r_lgs"], NC * (L + 1))
                lg = LG[:, 0:NT * nE].rearrange("p (t e) -> p t e", e=nE)
                ohv = OH[:, 0:NT * nE].rearrange("p (t e) -> p t e", e=nE)
                if L == 1:
                    do(v.tensor_reduce(t25, lg, AX.X, ALU.max))
                    do(v.tensor_tensor(lg, lg, t25.unsqueeze(2).to_broadcast([P, NT, nE]), ALU.subtract))
                    v.sem_inc(S["negm"], 1)
                    v.wait_ge(S["expd"], 1)
                    do(v.tensor_reduce(se, lg, AX.X, ALU.add))
                    do(v.reciprocal(se, se))
                    do(v.tensor_tensor(lg, lg, se.unsqueeze(2).to_broadcast([P, NT, nE]), ALU.mult))
                for t in range(NT):
                    ch.link(v.max(mx[:, 8 * t:8 * t + 8], lg[:, t, :]))
                ch.join()
                for t in range(NT):
                    ch.link(v.max_index(mi[:, 8 * t:8 * t + 8], mx[:, 8 * t:8 * t + 8], lg[:, t, :]))
                ch.join()
                do(v.tensor_copy(mif, mi.rearrange("p (t s) -> p t s", s=8)[:, :, 0]))
                do(v.tensor_tensor(ohv, iota[:, 0:nE].unsqueeze(1).to_broadcast([P, NT, nE]), mif.unsqueeze(2).to_broadcast([P, NT, nE]), ALU.is_equal))
                do(v.tensor_tensor(ohv, ohv, valid[:].unsqueeze(2).to_broadcast([P, NT, nE]), ALU.mult))
                v.sem_inc(S["oh_ready"], 1)
                W = NT * nE
                half = W // 2
                tot = ps[:, 2 * B:2 * B + 2 * B]
                ttv = TT[:, 0:W].rearrange("p (e t) -> p e t", t=NT)
                inv_ = IN[:, 0:W].rearrange("p (e t) -> p e t", t=NT)
                mkv = MSK[:, 0:W].rearrange("p (e t) -> p e t", t=NT)
                prv = PR[:, 0:W].rearrange("p (t e) -> p t e", e=nE)
                do(v.memset(MSK[:, 0:W], 1.0))
                do(v.memset(mkv[:, :, 0:1], 0.0))
                v.wait_ge(S["mass"], L + 1)
                nh = 2 if L == 0 else 1
                wt = NT * nE // nh
                do(v.tensor_copy(PR[:, 0:wt], ps[:, 0:wt]))
                do(v.tensor_copy(IN[:, 0:wt], ps[:, 2 * B:2 * B + wt]))
                if nh == 2:
                    do(v.tensor_copy(PR[:, wt:2 * wt], ps[:, B:B + wt]))
                    do(v.tensor_copy(IN[:, wt:2 * wt], ps[:, 3 * B:3 * B + wt]))
                do(v.tensor_copy(ttv, IN[:, 0:W].rearrange("p (t e) -> p e t", e=nE)))
                do(v.tensor_tensor_scan(IN[:, 0:W], MSK[:, 0:W], TT[:, 0:W], 0.0, ALU.mult, ALU.add))
                do(v.tensor_copy(cntE[:, 0:nE], inv_[:, :, NT - 1]))
                do(v.tensor_tensor(IN[:, 0:W], IN[:, 0:W], TT[:, 0:W], ALU.subtract))
                do(v.tensor_tensor(prv, prv, IN[:, 0:W].rearrange("p (e t) -> p t e", t=NT), ALU.add))
                do(v.tensor_tensor(prv, prv, ohv, ALU.mult))
                do(v.tensor_reduce(rank, prv, AX.X, ALU.add))
                if L == 0:
                    do(v.tensor_scalar(nbE, cntE, float(P - 1), None, ALU.add))
                    do(v.tensor_copy(nbEi, nbE))
                    do(v.tensor_scalar(nbEi, nbEi, 7, None, ALU.arith_shift_right))
                    do(v.tensor_copy(nbE, nbEi))
                    do(v.tensor_tensor_scan(CE, ones[:, 0:E0], nbE, 0.0, ALU.mult, ALU.add))
                    do(v.tensor_tensor(baseE, CE, nbE, ALU.subtract))
                    do(v.tensor_scalar(baseE, baseE, float(P), None, ALU.mult))
                    eb3 = ebc[0:1, :].rearrange("p (b e) -> p b e", e=E0)
                    do(v.tensor_tensor(eb3, iota[0:1, 0:NB0].unsqueeze(2).to_broadcast([1, NB0, E0]), CE[0:1, :].unsqueeze(1).to_broadcast([1, NB0, E0]), ALU.is_ge))
                    do(v.tensor_reduce(ebf[0:1, :], eb3, AX.X, ALU.add))
                    do(v.tensor_scalar(ebi[:], ebf[0:1, :], float(E0 - 1), None, ALU.min))
                else:
                    do(v.tensor_scalar(baseE[:, 0:nE], iota[:, 0:nE], float(CAP), None, ALU.mult))
                do(v.tensor_tensor(prv, ohv, baseE[:, 0:nE].unsqueeze(1).to_broadcast([P, NT, nE]), ALU.mult))
                do(v.tensor_reduce(pos, prv, AX.X, ALU.add))
                if L == 0:
                    do(v.tensor_copy(kept, valid[:]))
                    do(v.tensor_tensor(t25, pos, rank, ALU.add))
                    do(v.tensor_copy(gidx[:], t25))
                else:
                    do(v.tensor_scalar(kept, rank, float(CAP), None, ALU.is_lt))
                    do(v.tensor_copy(rt[:, 4, :], se))
                    do(v.tensor_tensor(rt[:, 4, :], rt[:, 4, :], kept, ALU.mult))
                    do(v.tensor_tensor(kept, kept, valid[:], ALU.mult))
                    do(v.tensor_tensor(t25, pos, rank, ALU.add))
                    do(v.tensor_scalar(rank, rank, float(CAP - 1), None, ALU.min))
                    do(v.tensor_tensor(pos, pos, rank, ALU.add))
                    do(v.tensor_copy(gidx[:], pos))
                do(v.tensor_scalar(kept, kept, -FAR, FAR, ALU.mult, ALU.add))
                do(v.tensor_tensor(t25, t25, kept, ALU.add))
                do(v.tensor_copy(sidx[:], t25))
                if L == 0:
                    do(v.memset(h0[F0:F0 + 1, :, :], 1.0))
                v.sem_inc(S["routed"], 1)
                if L == 0:
                    def turn(q):
                        for h in range(2):
                            v.wait_ge(e_put[h], (q + 1) * 16)
                            v.sem_inc(S["idle_v"], 1)
                            held("e_y", q * 2 + (h + 2))
                            v.tensor_scalar(y0[h], ps[:, (6, 0)[h] * B:(6, 0)[h] * B + Q0 * D], 0.0, None, ALU.max).then_inc(S["e_ys"], 1)

                    with v.Fori(0, NB0 // TURN0) as q:
                        turn(q)
                    for c in range(NC):
                        v.wait_ge(back[c], 16 * CT)
                    with v.Fori(0, NC) as c:
                        ch.loop(c, 1)
                        ch.link(v.tensor_tensor(rows(c), rows(c), acc[:, bass.ds(c * (CT * D), CT * D)], ALU.add))
                    ch.end(NC)
                    ch.join()
                    do(v.memset(ring4[:, :, :, D:AP_], 1.0))
                    do(v.memset(acc[:, 0:1], 0.0))
                    do(v.memset(acc[:, NT * D:], 0.0))
                    do(v.memset(acc[:], 0.0))
                    v.sem_inc(S["layer_done"], 1)
                else:
                    with v.Fori(0, E1 // 2) as i2:
                        for s in range(2):
                            e = i2 * 2 + s
                            held("f_out", (e * 2 + 1) * 16)
                            held("f_y", e + 1)
                            v.tensor_copy(y1.rearrange("p s f -> p (s f)")[:, 0:(ST - 1) * D], ps[:, 6 * B:6 * B + (ST - 1) * D])
                            v.tensor_copy(y1[0:STAIL, ST - 1, :], ps[0:STAIL, 6 * B + (ST - 1) * D:8 * B]).then_inc(S["f_ys"], 1)
                    bad = Hs[:].bitcast(I32)
                    do(v.memset(Kb[:], 0.0))
                    for c in range(NC):
                        v.wait_ge(back[c], 32 * CT)
                        y = XALL[:, c * CT:(c + 1) * CT, :]
                        do(v.tensor_tensor(y, y, rt[:, 4, c * CT:(c + 1) * CT].unsqueeze(2).to_broadcast([P, CT, D]), ALU.mult))
                        ch.link(v.tensor_scalar(Wk[:], y, 1.0e4, -1.0e4, ALU.min, ALU.max))
                        do(v.tensor_tensor(XN[:], y, y, ALU.subtract))
                        ch.link(v.tensor_scalar(bad, XN[:], 0.0, None, ALU.is_equal))
                        do(v.tensor_tensor(ex, y, y, ALU.not_equal))
                        do(v.copy_predicated(Wk[:], bad, y))
                        do(v.copy_predicated(Wk[:], ex.bitcast(I32), Kb[:]))
                        y = Wk[:]
                        do(v.tensor_tensor(X[:, c * CT:(c + 1) * CT, :], X[:, c * CT:(c + 1) * CT, :], y, ALU.add))
                        v.sem_inc(S["layer_done"], 1)

        @block.tensor
        def _(pe):
            mm = nc.tensor.matmul
            tp = nc.tensor.transpose

            def held(sem, val):
                pe.wait_ge(S[sem], val)
                pe.sem_inc(S["idle_t"], 1)

            pe.wait_ge(S["made"], 3)
            pe.wait_ge(S["prepped"], 1)
            cnt, delta = sm[:, 3:4], sm[:, 4:5]
            mm(ps[0:NG, 0:1], tri[0:NG, 0:NG], cnt, start=True, stop=True)
            mm(ps[0:1, 4:4 + NG], cnt, tri[0:NG, 0:NG], start=True, stop=True).then_inc(S["ranked"], 1)
            pe.wait_ge(S["prepped"], 2)
            for k, q in enumerate(range(0, MAXN, 512)):
                m = min(512, MAXN - q)
                if k:
                    pe.wait_ge(S["listed"], k)
                mm(ps[0:1, 0:m], ones[0:NG, 0:1], step[:, q:q + m], start=True, stop=True)
                mm(ps[0:1, B:B + m], delta, step[:, q:q + m], start=True, stop=True).then_inc(S["ranked"], 1)
            pe.wait_ge(S["listed"], -(-MAXN // 512) + 1)
            pe.wait_ge(S["loaded"], 16 * len(loads))

            def transposes(srcb, sem, at=0):
                for j in range(CT):
                    for k in range(KD):
                        i = tp(ps[:, at + k * 1024 + j * P:at + k * 1024 + (j + 1) * P], srcb[:, j, k * P:(k + 1) * P], ident[:])
                i.then_inc(S[sem], 1)

            def segment(L, c, n0, k0, k1):
                s0 = pe.value_load(seg_row[0:1, bass.ds(c * PARTS + k0, 1)], min_val=0, max_val=MAXN)
                s1 = pe.value_load(seg_row[0:1, bass.ds(c * PARTS + k1, 1)], min_val=1, max_val=MAXN)
                with pe.Fori(s0, s1) as n:
                    pr = pe.value_load(pair_row[0:1, bass.ds(n, 1)], min_val=0, max_val=((NT + 1) << 19) - 1)
                    g = pe.snap(pr // (1 << 12) % 128, min_val=0, max_val=NG - 1)
                    pe.wait_ge(S["landed"], g + (NG * L + 1))
                    pe.sem_inc(S["idle_t"], 1)
                    for h in range(2):
                        pe.wait_ge(S["oh_half"], (n + n0) * 2 + (h + 1))
                        for j in range(GH * h, GH * (h + 1)):
                            i = mm(ps[:, bass.ds(((n + n0) % 2) * B + 6 * B, AP_)], oh[:, j, :],
                                   ring[:, bass.ds((g % R) * (GT * AP_) + j * AP_, AP_)], start=j == 0, stop=j == GT - 1)
                        i.then_inc(S["half_used"], 1)

            for L in range(2):
                if L == 1:
                    pe.wait_ge(S["wload"], 48)
                def chunk(c, more):
                    held("a_xT", v5(L, c))
                    for j in range(CT):
                        for k in range(KD):
                            i = mm(ps[:, 5 * B + j * D:5 * B + (j + 1) * D], xT[:, k, j * P:(j + 1) * P], wn[:, k, :], start=k == 0, stop=k == KD - 1)
                    i.then_inc(S["a_nb"], 1)
                    held("a_kvacc", v5(L, c))
                    for j in range(CT):
                        for k in range(KD):
                            i = mm(ps[:, j * B:(j + 1) * B], xT[:, k, j * P:(j + 1) * P], wqkv[:, k, D:3 * D], start=k == 0, stop=k == KD - 1)
                    i.then_inc(S["a_kvp"], 1)
                    held("a_k", v5(L, c))
                    if more:
                        held("a_xn", v5(L, c) + 1)
                        transposes(XN, "a_tr", 2 * B)
                    for q in range(2):
                        for j in range(CT):
                            i = mm(ps[:, q * B:q * B + P + 1], Kb[:, j, q * P:(q + 1) * P], Vb[:, j, q, :], start=j == 0, stop=j == CT - 1)
                    i.then_inc(S["a_kv"], 1)

                pe.wait_ge(S["a_xn"], v5(L, 0))
                transposes(XN, "a_tr", 2 * B)
                with pe.Fori(0, NC - 1) as c:
                    chunk(c, True)
                chunk(NC - 1, False)
                pe.wait_ge(S["kv_ready"], L + 1)
                n0 = 0
                if L == 1:
                    for q in range(2):
                        i = tp(ps[:, q * P:(q + 1) * P], KVb[:, q, 0:P], ident[:])
                    i.then_inc(S["ct_ps"], 1)
                    pe.wait_ge(S["ct_sb"], 1)
                    for q in range(2):
                        i = mm(ps[:, B + q * D:B + (q + 1) * D], CTx[:, q, :], wm1[:, q, :], start=True, stop=True)
                    i.then_inc(S["m_ps"], 1)
                    pe.wait_ge(S["m_ready"], 1)
                    n0 = pe.snap(pe.value_load(bi_row[0:1, NG - 1:NG], min_val=NG, max_val=MAXN))
                    pe.wait_ge(S["listed"], -(-MAXN // 512) + 2)
                with pe.Fori(0, NC) as c:
                    held("b_free", v5(L, c))
                    held("b_xs", v5(L, c) * 16)
                    for m in range(KD):
                        for n in range(2):
                            for k in range(KD):
                                i = mm(ps[:, (2 * m + n) * B:(2 * m + n) * B + HN], wqkv[:, k, m * P:(m + 1) * P], xT[:, k, n * HN:(n + 1) * HN], start=k == 0, stop=k == KD - 1)
                    i.then_inc(S["b_q"], 1)
                    segment(L, c, n0, 0, (1, 3)[L])
                    held("b_qt", v5(L, c))
                    if L == 0:
                        for j in range(CT):
                            for q in range(2):
                                i = mm(ps[:, j * B + q * (P + HH):j * B + (q + 1) * (P + HH)], QT[:, q * CN + j * P:q * CN + (j + 1) * P], KVb[:, q, :], start=True, stop=True)
                        i.then_inc(S["b_t"], 1)
                        segment(L, c, n0, 1, 4)
                        held("b_x1", c + 1)
                        transposes(X1, "b_x1t")
                        segment(L, c, n0, 4, 5)
                        held("b_x1T", c + 1)
                        for m in range(KD):
                            for n in range(2):
                                for k in range(KD):
                                    i = mm(ps[:, (2 * m + n) * B:(2 * m + n) * B + HN], wm1[:, k, m * P:(m + 1) * P], QT[:, k * CN + n * HN:k * CN + (n + 1) * HN], start=k == 0, stop=k == KD - 1)
                        i.then_inc(S["b_h"], 1)
                        segment(L, c, n0, 5, 6)
                        held("b_g", c + 1)
                        for j in range(CT):
                            o_ = ps[:, j * D:(j + 1) * D]
                            mm(o_, ones[0:1, :], brow[0:1, 0, :], start=True, stop=False)
                            for k in range(KD):
                                mm(o_, HT[:, k, j * P:(j + 1) * P], wm2[:, k, :], start=False, stop=k == KD - 1)
                        for j in range(CT):
                            for k in range(KD):
                                i = mm(ps[:, 3 * B + j * D:3 * B + (j + 1) * D], xT[:, k, j * P:(j + 1) * P], ws[:, k, :], start=k == 0, stop=k == KD - 1)
                        i.then_inc(S["b_y"], 1)
                    else:
                        for m in range(2):
                            for n in range(2):
                                i = mm(ps[:, (2 * m + n) * B:(2 * m + n) * B + HN], KS[:, m, :], QT[:, m * CN + n * HN:m * CN + (n + 1) * HN], start=True, stop=True)
                        i.then_inc(S["b_den"], 1)
                        segment(L, c, n0, 3, 5)
                        held("b_qs", c + 1)
                        for j in range(CT):
                            o_ = ps[:, j * D:(j + 1) * D]
                            mm(o_, ones[0:1, :], brow[0:1, 1, :], start=True, stop=False)
                            for q in range(2):
                                i = mm(o_, QT[:, q * CN + j * P:q * CN + (j + 1) * P], Mx[:, q, :], start=False, stop=q == 1)
                        i.then_inc(S["b_y"], 1)
                    segment(L, c, n0, (6, 5)[L], 8)
                nE = (E0, E1)[L]
                rwl = (rw, gw)[L]
                r0 = (0, E0)[L]
                with pe.Fori(0, NC) as c:
                    held("r_xn", v5(L, c))
                    transposes(XN, "r_tr")
                    held("r_xT", v5(L, c))
                    for j in range(CT):
                        o_ = ps[:, 4 * B + j * nE:4 * B + (j + 1) * nE]
                        mm(o_, ones[0:1, :], rrow[0:1, r0:r0 + nE], start=True, stop=False)
                        for k in range(KD):
                            i = mm(o_, xT[:, k, j * P:(j + 1) * P], rwl[:, k, :], start=False, stop=k == KD - 1)
                    i.then_inc(S["r_lg"], 1)
                    pe.sem_inc(S["r_done"], 1)
                pe.wait_ge(S["oh_ready"], L + 1)
                nh = 2 if L == 0 else 1
                wt = NT * nE // nh
                for q in range(nh):
                    mm(ps[:, q * B:q * B + wt], tris[:], OH[:, q * wt:(q + 1) * wt], start=True, stop=True)
                    i = mm(ps[:, (2 + q) * B:(2 + q) * B + wt], ones[:], OH[:, q * wt:(q + 1) * wt], start=True, stop=True)
                i.then_inc(S["mass"], 1)
                if L == 0:
                    def turn(q, p, full):
                        for h in range(2):
                            if h == 0:
                                held("e_ys", q * 2 + 1)
                            pe.wait_ge(e_in[p][h], full)
                            pe.sem_inc(S["idle_t"], 1)
                            for s in range(Q0):
                                for k in range(KD):
                                    i = tp(ps[:, 2 * h * B + s * D + k * P:2 * h * B + s * D + (k + 1) * P], xb0(p, h)[:, s, k * P:(k + 1) * P], ident[:])
                            i.then_inc(S["e_tr"], 1)
                        for h in range(2):
                            held("e_xT", q * 2 + (h + 1))
                            for s in range(Q0):
                                for k in range(KD):
                                    i = mm(ps[0:F0, (4 + h) * B + s * P:(4 + h) * B + (s + 1) * P], wb0(p, h)[:, s, k * F0:(k + 1) * F0],
                                           xbT0[h][:, s * D + k * P:s * D + (k + 1) * P], start=k == 0, stop=k == KD - 1)
                            i.then_inc(S["e_h"], 1)
                        for h in range(2):
                            held("e_hs", q * 2 + (h + 1))
                            for s in range(Q0):
                                i = mm(ps[:, (6, 0)[h] * B + s * D:(6, 0)[h] * B + (s + 1) * D], h0[0:F0 + 1, h, s * P:(s + 1) * P],
                                       wb0(p, h)[0:F0 + 1, s, KD * F0:KD * F0 + D], start=True, stop=True)
                            i.then_inc(S["e_y"], 1)

                    per = 16 * (Q0 + 1)
                    with pe.Fori(0, NB0 // TURN0 // 2) as i2:
                        for p in range(2):
                            turn(i2 * 2 + p, p, (i2 + 1) * per)
                    turn(NB0 // TURN0 - 1, 0, (NB0 // TURN0 // 2 + 1) * per)
                else:
                    def turned(e, s, full):
                        pe.wait_ge(f_in[s], full)
                        pe.sem_inc(S["idle_t"], 1)
                        for t in range(ST):
                            rws = P if t < ST - 1 else STAIL
                            for k in range(KD):
                                i = tp(ps[:, k * B + t * P:k * B + t * P + rws], xb1[s][0:rws, t, k * P:(k + 1) * P], ident[0:rws, 0:rws])
                        i.then_inc(S["f_tr"], 1)

                    def expert(e, s, nxt):
                        held("f_xT", e + 1)
                        for m in range(MT):
                            held("f_hs", e * MT + (m + 1))
                            for k in range(KD):
                                i = mm(ps[:, (2 + m % 4) * B:(2 + m % 4) * B + CAP], w11[:, s, k, m * P:(m + 1) * P], xb1T[:, k, 0:CAP], start=k == 0, stop=k == KD - 1)
                            i.then_inc(S["f_h"], 1)
                        if nxt is not None:
                            turned(e + 1, 1 - s, nxt)
                        held("f_hs", e * MT + (MT + 4))
                        held("f_ys", e + 1)
                        for t in range(ST):
                            rws = P if t < ST - 1 else STAIL
                            o_ = ps[0:rws, 6 * B + t * D:6 * B + (t + 1) * D]
                            mm(o_, ones[0:1, 0:rws], b21[0:1, s, :], start=True, stop=False)
                            for m in range(MT):
                                i = mm(o_, h1[:, m, t * P:t * P + rws], w21[:, s, m, :], start=False, stop=m == MT - 1)
                        i.then_inc(S["f_y"], 1)

                    per = 16 * 5
                    turned(0, 0, per)
                    with pe.Fori(0, E1 // 2 - 1) as i2:
                        expert(i2 * 2, 0, (i2 + 1) * per)
                        expert(i2 * 2 + 1, 1, (i2 + 2) * per)
                    expert(E1 - 2, 0, E1 // 2 * per)
                    expert(E1 - 1, 1, None)


def kernel(**inputs):
    import numpy as _np
    import concourse.bacc as _bacc
    from concourse import mybir as _mybir
    from concourse.bass_utils import run_bass_kernel_spmd as _run

    nc = _bacc.Bacc("TRN2", target_bir_lowering=False, num_devices=1)
    g = {k: _np.asarray(v) for k, v in inputs.items()}
    ep = NG * GE - E

    def halves(w):
        return w.reshape(KD, P, -1).transpose(1, 0, 2)

    dgrp = _np.pad(g["dst"], (0, ep), mode="edge").reshape(NG, GE)
    ew = _np.zeros((E0, P, EW), _np.float32)
    ew[:, :, 0:KD * F0] = g["L0_ffn_W1"].reshape(E0, KD, P, F0).transpose(0, 2, 1, 3).reshape(E0, P, KD * F0)
    ew[:, 0:F0, KD * F0:KD * F0 + D] = g["L0_ffn_W2"]
    ew[:, F0, KD * F0:KD * F0 + D] = g["L0_ffn_b2"]
    ew[:, 0:F0, EW - 1] = g["L0_ffn_b1"]
    a = {
        "x": g["x"],
        "srcT": _np.pad(g["src"], (0, ep)).reshape(ET, P).T,
        "dstT": _np.pad(g["dst"], (0, ep), constant_values=-1).reshape(ET, P).T,
        "dgrp": dgrp,
        "dnext": _np.concatenate([dgrp[1:], _np.full((1, GE), NT * P, dgrp.dtype)]),
        "wn": halves(g["L0_gnn_W_neigh"]),
        "ws": halves(g["L0_gnn_W_self"]),
        "wqkv0": halves(g["L0_mix_Wqkv"].T),
        "wm1": halves(g["L0_mix_W1"].T),
        "wm2": halves(g["L0_mix_W2"].T),
        "lng": _np.broadcast_to(_np.stack([g["L0_mix_ln1_g"], g["L0_mix_ln1_b"], g["L0_mix_ln2_g"], g["L0_mix_ln2_b"]]), (P, 4, D)),
        "b1c": g["L0_mix_b1"].reshape(KD, P).T,
        "mb2": g["L0_mix_b2"][None],
        "b1rows": _np.stack([g["L1_mix_bproj"], g["L1_gnn_b"]])[None],
        "rw": halves(g["L0_ffn_router_w"].T),
        "gw": halves(g["L1_ffn_gate_w"]),
        "rrow": _np.concatenate([g["L0_ffn_router_b"], g["L1_ffn_gate_b"]])[None],
        "valid": (_np.arange(NT * P) < N).astype(_np.float32).reshape(NT, P).T,
        "wg1": halves(g["L1_gnn_W"].T),
        "wqkv1": _np.concatenate([halves(g["L1_mix_Wq"].T), halves(g["L1_mix_Wkv"].T)], axis=2),
        "wproj": halves(g["L1_mix_Wproj"].T),
        "ew": ew,
        "w1": g["L1_ffn_w1"],
        "w2": g["L1_ffn_w2"],
        "b11": g["L1_ffn_b1"].reshape(E1 * MT, P).T,
        "b2": g["L1_ffn_b2"],
    }
    arrays, args = {}, {}
    for name, arr in a.items():
        arr = _np.ascontiguousarray(arr)
        arrays[name + "_dram"] = arr
        args[name] = nc.dram_tensor(name + "_dram", arr.shape, _mybir.dt.from_np(arr.dtype), kind="ExternalInput").ap()
    out = nc.dram_tensor("out_dram", (N, D), F32, kind="ExternalOutput").ap()
    build(nc, args, out)
    r = _run(nc, [arrays], core_ids=[0])
    return r.results[0]["out_dram"]
```

```python
import numpy as np
import concourse.bass as bass
from concourse import mybir
from contextlib import ExitStack

F32 = mybir.dt.float32
I32 = mybir.dt.int32
U32 = mybir.dt.uint32
ALU = mybir.AluOpType
ACT = mybir.ActivationFunctionType
AX = mybir.AxisListType

P = 128
N = 3125
D = 256
KD = D // P
NT = -(-N // P)
TAIL = N - (NT - 1) * P
CT = 5
NC = NT // CT
CN = CT * P
NP = NT * P
E = 50000
GT = 8
GH = GT // 2
GE = GT * P
NG = -(-E // GE)
ET = NG * GT
R = 7
LAG = 1
PARTS = 7
MAXN = NG * NT + 2
H = 8
HD = D // H
HH = P // HD
E0, F0 = 32, 64
NB0 = N // P + E0
E1, F1 = 8, 1024
EW = KD * F0 + D + 1
Q0 = 4
TURN0 = 2 * Q0
CAP = -(-5 * N // (4 * E1))
ST = -(-CAP // P)
STAIL = CAP - (ST - 1) * P
MT = F1 // P
XB1 = 4096
FAR = 1.0e6
IW = 33 * P
DW = GT * P + GT
SENT = -3.0e38
FMAX = 3.4028234e38
AP_ = D + 1


class Chain:

    def __init__(self, eng, sem, idle):
        self.eng, self.sem, self.idle = eng, sem, idle
        self.base, self.k, self.i, self.per = 0, 0, None, 0

    def loop(self, i, per):
        self.base += self.k
        self.i, self.per, self.k = i, per, 0

    def end(self, trips):
        assert self.k == self.per, (self.k, self.per)
        self.base += self.per * trips
        self.i, self.k = None, 0

    def link(self, ins):
        ins.then_inc(self.sem, 1)
        self.k += 1

    def join(self):
        if self.i is None:
            self.eng.wait_ge(self.sem, self.base + self.k)
        else:
            self.eng.wait_ge(self.sem, self.i * self.per + (self.base + self.k))
            self.eng.sem_inc(self.idle, 1)


def build(nc, a, out):
    ctx = ExitStack()
    with ctx:
        def sb(n, s, d=F32):
            return ctx.enter_context(nc.sbuf_tensor(n, s, d))

        def dr(n, s, d=F32):
            return nc.dram_tensor(n, s, d, kind="Internal").ap()

        xnT_d = dr("xnT_d", [P, KD, NP])
        table = [dr("table0", [NP, D]), dr("table1", [NP, D])]
        slots = [dr("slots0", [NB0 * P, D]), dr("slots1", [XB1, D])]
        yslots = [dr("yslots0", [NB0 * P, D]), dr("yslots1", [E1 * CAP, D])]

        X = sb("X", [P, NT, D])
        acc = sb("acc", [P, (NT + 1) * AP_])
        ring = sb("ring", [P, R * GT * AP_])
        iota = sb("iota", [P, IW], mybir.dt.int16)
        TE = sb("TE", [P, 2 * CT * D])
        step = ring[0:NG, 2560:2560 + MAXN]
        src = sb("src", [P, ET], I32)
        dst = sb("dst", [P, DW])
        stage = sb("stage", [P, R, GT], I32)
        pair_row = sb("pair_row", [1, MAXN], I32)
        g_row = ring[0:1, 0:MAXN]
        w_row = ring[0:1, MAXN:2 * MAXN + 1]
        bi_row = sb("bi_row", [1, NG], I32)
        seg_row = sb("seg_row", [1, NC * PARTS + 1], I32)
        dg = ring[0:NG, 4096:4096 + GE].bitcast(I32)
        dn = ring[0:NG, 5120:5120 + GE].bitcast(I32)
        tri = sb("tri", [P, P])
        tris = sb("tris", [P, P])
        ident = sb("ident", [P, P])
        ones = sb("ones", [P, P])
        valid = sb("valid", [P, NT])
        eps = sb("eps", [P, 1])
        sm = sb("sm", [NG, 12])
        smi = sb("smi", [NG, 3], I32)
        lo0 = sb("lo0", [1, 1])
        oh = sb("oh", [P, GT, P])
        st = sb("st", [P, CT, 6])
        mv = sb("mv", [P, CT, 2])
        rs = sb("rs", [P, NT])
        nm = sb("nm", [P, NT])
        sd = sb("sd", [P, CT])
        deg = sb("deg", [P, NT])
        rdeg = sb("rdeg", [P, NT])
        dinv = sb("dinv", [P, NT])
        wn = sb("wn", [P, KD, D])
        ws = sb("ws", [P, KD, D])
        wqkv = sb("wqkv", [P, KD, 3 * D])
        wm1 = sb("wm1", [P, KD, D])
        wm2 = sb("wm2", [P, KD, D])
        lng = sb("lng", [P, 5, D])
        lnc = sb("lnc", [P, KD, 2])
        b1c = sb("b1c", [P, KD])
        brow = sb("brow", [1, 2, D])
        XN = sb("XN", [P, CT, D])
        xT = sb("xT", [P, KD, CN])
        Kb = sb("Kb", [P, CT, D])
        Vb = sb("Vb", [P, CT, 2, P + 1])
        tmp = TE[:, 0:CT * D].rearrange("p (j f) -> p j f", f=D)
        ex = TE[:, CT * D:].rearrange("p (j f) -> p j f", f=D)
        Hs = sb("Hs", [P, CT, D])
        Wk = sb("Wk", [P, CT, D])
        m8 = sb("m8", [P, CT, 8])
        KV = sb("KV", [P, 2, P + 1])
        KVb = sb("KVb", [P, 2, P + HH])
        KS = ws[:, :, 0:P]
        Mx = wm2
        den = sb("den", [P, CT * H])[:]
        rw = sb("rw", [P, KD, E0])
        gw = sb("gw", [P, KD, E1])
        rrow = sb("rrow", [P, E0 + E1])
        ps = ctx.enter_context(nc.psum_tensor("ps", [P, 8 * 512], F32))
        B = 512

        def bank(i, w=512, n=1):
            return ps[:, i * B:i * B + w * n]

        QT = Kb[:].rearrange("p j f -> p (j f)")
        X1 = Hs
        N2 = Vb[:].rearrange("p j a f -> p (j a f)")[:, 0:CT * D].rearrange("p (j f) -> p j f", f=D)
        CTx = Vb[:, 0, :, 0:P]
        Z = Wk
        HT = Vb[:].rearrange("p j a f -> p (j a f)")[:, 0:KD * CN].rearrange("p (k n) -> p k n", k=KD)
        XALL = acc[:, 0:NT * D].rearrange("p (t f) -> p t f", f=D)
        a3 = acc[:].rearrange("p (w f) -> p w f", f=AP_)
        ring4 = ring[:].rearrange("p (r j f) -> p r j f", r=R, f=AP_)
        unfit = [XN[:], Kb[:]]
        o = [0]

        def take(n):
            r = ring[:, o[0]:o[0] + n]
            o[0] += n
            return r

        LG = take(NT * E0)
        OH = take(NT * E0)
        TT = take((NT + 1) * E0)
        IN = take((NT + 1) * E0)
        MSK = take((NT + 1) * E0)
        PR = take(NT * E0)
        mx = take(NT * 8)
        mi = take(NT * 8).bitcast(U32)
        mif = take(NT)
        rank = take(NT)
        pos = take(NT)
        kept = take(NT)
        t25 = take(NT)
        se = take(NT)
        cntE = take(E0)
        nbE = take(E0)
        nbEi = take(E0).bitcast(I32)
        CE = take(E0)
        baseE = take(E0)
        ebc = take(NB0 * E0)
        ebf = take(NB0)
        sidx = sb("sidx", [P, NT], I32)
        gidx = sb("gidx", [P, NT], I32)
        ebi = sb("ebi", [1, NB0], I32)
        half_set = Q0 * (D + EW)
        home = [ring, acc]

        def xb0(p, h):
            return home[p][:, h * half_set:h * half_set + Q0 * D].rearrange("p (s f) -> p s f", s=Q0)

        def wb0(p, h):
            return home[p][:, h * half_set + Q0 * D:(h + 1) * half_set].rearrange("p (s f) -> p s f", s=Q0)

        def flat3(t):
            return t[:].rearrange("p j f -> p (j f)")
        xbT0 = [flat3(XN)[:, 0:Q0 * D], flat3(Kb)[:, 0:Q0 * D]]
        h0 = flat3(Hs)[:, 0:2 * Q0 * P].rearrange("p (h n) -> p h n", h=2)
        y0 = [flat3(Wk)[:, 0:Q0 * D], flat3(tmp)[:, 0:Q0 * D]]
        w11 = ring[:, 0:2 * KD * F1].rearrange("p (s k f) -> p s k f", s=2, k=KD)
        w21 = ring[:, 2 * KD * F1:4 * KD * F1].rearrange("p (s m f) -> p s m f", s=2, m=MT)
        h1 = acc[:, 0:MT * CAP].rearrange("p (m n) -> p m n", m=MT)
        xb1 = [XN[:, 0:ST, :], Kb[:, 0:ST, :]]
        xb1T = xT[:, :, 0:ST * P]
        y1 = Wk[:, 0:ST, :]
        warm = sb("warm", [P, 4])
        b11 = sb("b11", [P, E1 * MT])
        b21 = lng[0:1, 0:2, :]
        rt = sb("rt", [P, 8, NT])

        S = {}
        names = """early_in lists_in b_self_in_psum start_set loaded consts made pairs_prepared pairs_summed
            pairs_listed idle_p idle_a idle_v idle_t idle_s dve_chain act_chain landed oh_half half_used added
            agg_done stat stat_sd stat_rs a_rows_normed a_rows_transposed a_xT_written a_messages_in_psum
            a_kv_in_psum a_messages_in_sbuf a_exp_done a_values_written a_keys_written a_ktv_in_psum a_ktv_added
            a_messages_final a_xT_stored a_table_stored kv_ready context_in_psum context_in_sbuf mproj_in_psum
            mproj_written b_xT_loaded b_q_in_psum b_exp_done b_rows_normed b_q_written b_attn_in_psum
            b_sum1_stats b_std1 b_scale1 b_normed1 b_x1_transposed b_x1T_written b_hidden_in_psum b_gelu_done
            b_y_in_psum b_sum2_stats b_std2 b_scale2 b_normed2 b_den_in_psum b_q_scaled b_y_read x_out y_scaled
            deg_ready deg_sd r_rows_normed r_rows_transposed r_xT_written r_logits_in_psum r_logits_read
            r_rows_copied oh_ready ranks_in_psum blocks_named routed logits_exp_done logits_shifted zeroed
            scattered e_rows_transposed e_xT_written e_hidden_in_psum e_hidden_written e_y_in_psum e_y_written
            f_rows_transposed f_xT_written f_hidden_in_psum f_hidden_written f_y_in_psum f_y_written f_y_stored
            out_stored weights1_loaded senders_staged""".split()
        for n in names:
            S[n] = ctx.enter_context(nc.semaphore(n))
        e_in = [[ctx.enter_context(nc.semaphore(f"e_in{p}{h}")) for h in range(2)] for p in range(2)]
        e_put = [ctx.enter_context(nc.semaphore(f"e_put{h}")) for h in range(2)]
        f_in = [ctx.enter_context(nc.semaphore(f"f_in{s}")) for s in range(2)]
        x_in = [ctx.enter_context(nc.semaphore(f"x_in{c}")) for c in range(NC)]
        back = [ctx.enter_context(nc.semaphore(f"back{c}")) for c in range(NC)]
        slot_in = [ctx.enter_context(nc.semaphore(f"slot_in{i}")) for i in range(R)]

        block = ctx.enter_context(nc.Block())

        def v5(L, c):
            return c + (NC * L + 1)

        first = [(oh[:].rearrange("p j n -> p (j n)")[:, 0:ET].bitcast(I32), a["dstT"]), (dg, a["dgrp"]), (dn, a["dnext"])]
        early = [(wqkv[:], a["wqkv0"])]
        loads = [(wn[:], a["wn"]), (valid[:], a["valid"]), (brow[:], a["b1rows"]), (lnc[:], a["lnc"]), (src[:], a["srcT"]),
                 (ws[:], a["ws"]), (wm1[:], a["wm1"]), (wm2[:], a["wm2"]), (lng[:], a["lng"]), (b1c[:], a["b1c"]), (rw[:], a["rw"]), (gw[:], a["gw"]),
                 (rrow[:], a["rrow"]), (b11[:], a["b11"])]

        @block.sync
        def _(sp):
            def held(sem, val):
                sp.wait_ge(S[sem], val)
                sp.sem_inc(S["idle_s"], 1)

            for d, s in first:
                sp.dma_start(d, s).then_inc(S["lists_in"], 16)
            sp.wait_ge(S["start_set"], 1)
            for c in range(NC):
                last = c == NC - 1
                n = CT - 1 if last else CT
                if c == 1:
                    for d, s in early:
                        sp.dma_start(d, s).then_inc(S["early_in"], 16)
                sp.dma_start(X[:, c * CT:c * CT + n, :], a["x"][c * CN:c * CN + n * P, :].rearrange("(j p) f -> p j f", p=P)).then_inc(x_in[c], 16)
            sp.dma_start(X[0:TAIL, NT - 1, :], a["x"][(NT - 1) * P:N, :]).then_inc(x_in[NC - 1], 16)
            for d, s in loads:
                sp.dma_start(d, s).then_inc(S["loaded"], 16)
            sp.wait_ge(S["consts"], 6)

            for L in range(2):
                def put(c, clear, last):
                    held("a_xT_written", v5(L, c))
                    sp.dma_start(xnT_d[:, :, bass.ds(c * CN, CN)], xT[:]).then_inc(S["a_xT_stored"], 16)
                    if clear:
                        for z in slots:
                            z = z.rearrange("(p r) f -> p (r f)", p=P)
                            w = z.shape[1] // (NC - 1)
                            sp.dma_start(z[:, bass.ds(c * w, w)], acc[:, 0:w]).then_inc(S["zeroed"], 16)
                    if last:
                        sp.wait_ge(S["a_xT_stored"], 16 * NC * (L + 1) + 16)
                        sp.wait_ge(S["a_messages_in_psum"], NC * (L + 1))
                        sp.dma_start(xT[:], xnT_d[:, :, 0:CN]).then_inc(S["b_xT_loaded"], 16)
                    held("a_messages_final", v5(L, c))
                    sp.dma_start(table[L][bass.ds(c * CN, CN), :].rearrange("(j p) f -> p j f", p=P), Hs[:]).then_inc(S["a_table_stored"], 16)

                with sp.Fori(0, NC - 1) as c:
                    put(c, L == 0, False)
                put(NC - 1, False, True)
                with sp.Fori(1, NC) as c:
                    held(*(("b_self_in_psum", c + 1), ("b_q_in_psum", c + NC))[L])
                    sp.dma_start(xT[:], xnT_d[:, :, bass.ds(c * CN, CN)]).then_inc(S["b_xT_loaded"], 16)
                if L == 0:
                    sp.wait_ge(S["b_y_in_psum"], NC)
                    sp.dma_start(wn[:], a["wg1"]).then_inc(S["weights1_loaded"], 16)
                    sp.dma_start(wqkv[:], a["wqkv1"]).then_inc(S["weights1_loaded"], 16)
                    sp.dma_start(wm1[:], a["wproj"]).then_inc(S["weights1_loaded"], 16)
                    sp.wait_ge(S["scattered"], 16 * NT)
                    sp.wait_ge(S["blocks_named"], 1)

                    def load(q, p):
                        for h in range(2):
                            sp.dma_start(xb0(p, h), slots[0][bass.ds(q * (TURN0 * P) + h * (Q0 * P), Q0 * P), :].rearrange("(s p) f -> p s f", p=P)).then_inc(e_in[p][h], 16)
                            for s in range(Q0):
                                e = sp.value_load(ebi[0:1, bass.ds(q * TURN0 + (h * Q0 + s), 1)], min_val=0, max_val=E0 - 1)
                                sp.dma_start(wb0(p, h)[:, s, :], a["ew"][bass.ds(e, 1), :, :].rearrange("e p f -> p (e f)")).then_inc(e_in[p][h], 16)

                    def store(q):
                        for h in range(2):
                            held("e_y_written", q * 2 + (h + 2))
                            sp.dma_start(yslots[0][bass.ds(q * (TURN0 * P) + h * (Q0 * P), Q0 * P), :].rearrange("(s p) f -> p s f", p=P),
                                         y0[h].rearrange("p (s f) -> p s f", s=Q0)).then_inc(e_put[h], 16)

                    load(0, 0)
                    with sp.Fori(0, NB0 // TURN0 // 2) as i:
                        for p in range(2):
                            q = i * 2 + p
                            held("e_y_in_psum", q * 2 + 1)
                            load(q + 1, 1 - p)
                            store(q)
                    store(NB0 // TURN0 - 1)
                else:
                    def load_w(e, s):
                        sp.dma_start(w11[:, s], a["w1"][bass.ds(e, 1), :, :].rearrange("e (k p) f -> p (e k) f", p=P)).then_inc(f_in[s], 16)
                        sp.dma_start(w21[:, s], a["w2"][bass.ds(e, 1), :, :].rearrange("e (m p) f -> p (e m) f", p=P)).then_inc(f_in[s], 16)
                        sp.dma_start(b21[:, s, :], a["b2"][bass.ds(e, 1), :]).then_inc(f_in[s], 16)

                    def load_x(e, s):
                        sp.dma_start(xb1[s][:, 0:ST - 1, :], slots[1][bass.ds(e * CAP, (ST - 1) * P), :].rearrange("(t p) f -> p t f", p=P)).then_inc(f_in[s], 16)
                        sp.dma_start(xb1[s][0:STAIL, ST - 1, :], slots[1][bass.ds(e * CAP + (ST - 1) * P, STAIL), :]).then_inc(f_in[s], 16)

                    def store(e):
                        held("f_y_written", e + 2)
                        sp.dma_start(yslots[1][bass.ds(e * CAP, (ST - 1) * P), :].rearrange("(t p) f -> p t f", p=P), y1[:, 0:ST - 1, :]).then_inc(S["f_y_stored"], 16)
                        sp.dma_start(yslots[1][bass.ds(e * CAP + (ST - 1) * P, STAIL), :], y1[0:STAIL, ST - 1, :]).then_inc(S["f_y_stored"], 16)

                    sp.wait_ge(S["routed"], 2)
                    load_w(0, 0)
                    sp.wait_ge(S["scattered"], 32 * NT)
                    load_x(0, 0)
                    with sp.Fori(0, E1 // 2 - 1) as i:
                        for s in range(2):
                            e = i * 2 + s
                            held("f_y_written", e + 1)
                            load_w(e + 1, 1 - s)
                            load_x(e + 1, 1 - s)
                            store(e)
                    sp.wait_ge(S["f_y_written"], E1 - 2 + 1)
                    load_w(E1 - 1, 1)
                    load_x(E1 - 1, 1)
                    store(E1 - 2)
                    store(E1 - 1)
            for c in range(NC):
                n = CT - 1 if c == NC - 1 else CT
                sp.wait_ge(S["x_out"], c + 1)
                sp.dma_start(out[c * CN:c * CN + n * P, :].rearrange("(j p) f -> p j f", p=P), X[:, c * CT:c * CT + n, :]).then_inc(S["out_stored"], 16)
            sp.dma_start(out[(NT - 1) * P:N, :], X[0:TAIL, NT - 1, :]).then_inc(S["out_stored"], 16)
            sp.wait_ge(S["out_stored"], 16 * (NC + 1))

        @block.gpsimd
        def _(gp):
            gp.memset(X[:, NT - 1, :], 0.0).then_inc(S["start_set"], 1)
            gp.memset(eps[:], 1e-5).then_inc(S["start_set"], 1)
            gp.memset(dst[:], -1.0).then_inc(S["start_set"], 1)
            gp.memset(tri[:], 1.0).then_inc(S["consts"], 1)
            gp.memset(tris[:], 1.0).then_inc(S["consts"], 1)
            gp.memset(ident[:], 0.0).then_inc(S["consts"], 1)
            gp.memset(ones[:], 1.0).then_inc(S["consts"], 1)
            gp.wait_ge(S["consts"], 4)
            gp.affine_select(out=tri[:], in_=tri[:], compare_op=ALU.is_ge, fill=0.0, base=0, pattern=[[1, P]], channel_multiplier=-1).then_inc(S["made"], 1)
            gp.affine_select(out=tris[:], in_=tris[:], compare_op=ALU.is_gt, fill=0.0, base=0, pattern=[[1, P]], channel_multiplier=-1).then_inc(S["made"], 1)
            gp.affine_select(out=ident[:], in_=ident[:], compare_op=ALU.not_equal, fill=1.0, base=0, pattern=[[-1, P]], channel_multiplier=1).then_inc(S["made"], 1)
            gp.iota(iota[:], pattern=[[1, IW]], base=0, channel_multiplier=0, allow_small_or_imprecise_dtypes=True).then_inc(S["consts"], 1)
            gp.memset(acc[:], 0.0).then_inc(S["consts"], 1)
            gp.wait_ge(S["loaded"], 16 * len(loads))
            gp.wait_ge(S["pairs_listed"], -(-MAXN // 512) + 1)

            for L in range(2):
                gp.wait_ge(S["a_table_stored"], 16 * NC * (L + 1) + 16)

                def fetch(g, b):
                    gp.tensor_copy(stage[:, b, :], src[:, bass.ds(g * GT, GT)]).then_inc(S["senders_staged"], 1)
                    gp.wait_ge(S["senders_staged"], g + (1 + NG * L))
                    gp.sem_inc(S["idle_p"], 1)
                    for j in range(GT):
                        gp.indirect_dma_start(ring4[:, b, j, 0:D], None, table[L], bass.IndirectOffsetOnAxis(ap=stage[:, b, j:j + 1], axis=0)).then_inc(slot_in[b], 16)

                def arrived(b, turn):
                    before = L * (NG // R + (1 if b < NG % R else 0))
                    gp.wait_ge(slot_in[b], (turn + (before + 1)) * (16 * GT))
                    gp.sem_inc(S["landed"], 1)

                def freed(gprev, base):
                    n = gp.value_load(bi_row[0:1, gprev], min_val=1, max_val=MAXN)
                    gp.wait_ge(S["half_used"], n * 2 + base)
                    gp.sem_inc(S["idle_p"], 1)

                if L == 1:
                    ntot = gp.value_load(bi_row[0:1, NG - 1:NG], min_val=1, max_val=MAXN)
                    off = gp.snap(ntot * 2 + 2)
                else:
                    off = 2
                for g in range(R):
                    fetch(g, g)
                    if g >= LAG:
                        arrived(g - LAG, 0)
                with gp.Fori(1, NG // R) as r:
                    for b in range(R):
                        freed(bass.ds((r - 1) * R + b, 1), off)
                        fetch(r * R + b, b)
                        arrived((b - LAG) % R, r if b >= LAG else r - 1)
                for g in range(NG // R * R, NG):
                    freed(bass.ds(g - R, 1), off)
                    fetch(g, g % R)
                    arrived((g - LAG) % R, (g - LAG) // R)
                for g in range(NG - LAG, NG):
                    arrived(g % R, g // R)
                gp.wait_ge(S["routed"], L + 1)
                gp.wait_ge(S["r_rows_copied"], NC * (L + 1))
                gp.wait_ge(S["zeroed"], 16 * 2 * (NC - 1))
                for t in range(NT):
                    gp.indirect_dma_start(slots[L], bass.IndirectOffsetOnAxis(ap=sidx[:, t:t + 1], axis=0), XALL[:, t, :], None,
                                          bounds_check=slots[L].shape[0] - 1, oob_is_err=False).then_inc(S["scattered"], 16)
                if L == 0:
                    for h in range(2):
                        gp.wait_ge(e_put[h], 16 * (NB0 // TURN0) + 16)
                else:
                    gp.wait_ge(S["f_y_stored"], 32 * E1 + 16)
                for t in range(NT):
                    gp.indirect_dma_start(XALL[:, t, :], None, yslots[L], bass.IndirectOffsetOnAxis(ap=gidx[:, t:t + 1], axis=0)).then_inc(back[t // CT], 16)

        @block.scalar
        def _(ac):
            ch = Chain(ac, S["act_chain"], S["idle_a"])
            for n, k in (("a_ktv_added", 1), ("e_y_in_psum", 1), ("e_y_written", 1), ("f_y_written", 1), ("half_used", 2), ("b_self_in_psum", 1), ("b_q_scaled", 1), ("b_y_read", 1),
                         ("added", 1), ("a_xT_stored", 16), ("a_table_stored", 16), ("f_hidden_written", 4), ("f_y_stored", 16), ("r_logits_in_psum", 1), ("r_logits_read", 1)):
                if k:
                    ac.sem_inc(S[n], k)
            for h in range(2):
                ac.sem_inc(e_put[h], 16)
            ac.wait_ge(S["start_set"], 2)

            def held(sem, val):
                ac.wait_ge(S[sem], val)
                ac.sem_inc(S["idle_a"], 1)

            def root(k, c):
                held("stat", c + (k * NC + 1))
                ac.activation(sd[:], mv[:, :, 1], ACT.Sqrt, bias=eps[:]).then_inc(S["stat_sd"], 1)

            def copyT(sem_in, sem_out, val, at=0):
                held(sem_in, val)
                ac.activation(xT[:].rearrange("p k n -> p (k n)"), ps[:, at:at + KD * CN], ACT.Copy).then_inc(S[sem_out], 1)

            for L in range(2):
                if L == 1:
                    ac.wait_ge(S["deg_ready"], 1)
                    ac.activation(dinv[:], deg[:], ACT.Sqrt, bias=ones[:, 0:1]).then_inc(S["deg_sd"], 1)
                def rows_in(c):
                    held("a_xT_stored", (c + NC * L + 1) * 16)
                    copyT("a_rows_transposed", "a_xT_written", v5(L, c), 2 * B)

                for c in range(NC):
                    root(2 * L, c)
                    if c == 1:
                        rows_in(0)
                if L == 0:
                    ac.wait_ge(S["consts"], 6)
                    ac.wait_ge(S["loaded"], 16 * len(loads))
                ac.wait_ge(S["made"], 3)
                def products_out(c):
                    held("a_kv_in_psum", v5(L, c))
                    k_ps = ps[:, 0:CT * B].rearrange("p (j f) -> p j f", f=B)
                    ch.link(ac.activation(tmp[:], k_ps[:, :, 0:D], ACT.Relu, scale=-1.0))
                    ch.join()
                    ac.activation(ex[:], tmp[:], ACT.Exp, scale=-1.0).then_inc(S["a_exp_done"], 1)
                    for j in range(CT):
                        i = ac.activation(Vb[:, j, :, 0:P], k_ps[:, j, D:2 * D].rearrange("p (a f) -> p a f", a=2), ACT.Copy, scale=valid[:, bass.ds(c * CT + j, 1)])
                    i.then_inc(S["a_values_written"], 1)
                    held("a_table_stored", v5(L, c) * 16)
                    held("a_messages_in_psum", v5(L, c))
                    if L == 0:
                        ac.activation(Hs[:].rearrange("p j f -> p (j f)"), ps[:, 5 * B:5 * B + CT * D], ACT.Copy).then_inc(S["a_messages_in_sbuf"], 1)
                    else:
                        for j in range(CT):
                            i = ac.activation(Hs[:, j, :], ps[:, 5 * B + j * D:5 * B + (j + 1) * D], ACT.Copy, scale=dinv[:, bass.ds(c * CT + j, 1)])
                        i.then_inc(S["a_messages_in_sbuf"], 1)

                ac.activation(warm[:, 2 * L:2 * L + 1], eps[:], ACT.Exp)
                with ac.Fori(0, NC - 1) as c:
                    ch.loop(c, 1)
                    products_out(c)
                    rows_in(c + 1)
                ch.end(NC - 1)
                products_out(NC - 1)
                if L == 1:
                    ac.wait_ge(S["context_in_psum"], 1)
                    ac.activation(CTx, bank(0, D).rearrange("p (a f) -> p a f", a=2), ACT.Copy).then_inc(S["context_in_sbuf"], 1)
                    ac.wait_ge(S["mproj_in_psum"], 1)
                    ac.activation(Mx[:].rearrange("p a f -> p (a f)"), bank(1, 512), ACT.Copy).then_inc(S["mproj_written"], 1)
                with ac.Fori(0, NC) as c:
                    ch.loop(c, 1)
                    if L == 1:
                        held("b_q_scaled", c + 1)
                    held("b_q_in_psum", v5(L, c))
                    ch.link(ac.activation(tmp[:].rearrange("p j f -> p (j f)"), ps[:, 0:KD * CN], ACT.Relu, scale=-1.0))
                    ch.join()
                    ac.activation(ex[:], tmp[:], ACT.Exp, scale=-1.0).then_inc(S["b_exp_done"], 1)
                    if L == 0:
                        for j in range(CT):
                            i = ac.activation(XN[:, j, :], X[:, bass.ds(c * CT + j, 1), :].rearrange("p a f -> p (a f)"), ACT.Identity,
                                              scale=rs[:, bass.ds(c * CT + j, 1)], bias=nm[:, bass.ds(c * CT + j, 1)])
                        i.then_inc(S["b_rows_normed"], 1)

                        def norm(z, w, r):
                            held(z, c + 1)
                            ac.activation(rt[:, 1, 0:CT], rt[:, 0, 0:2 * CT].rearrange("p (j s) -> p j s", s=2)[:, :, 1], ACT.Sqrt, bias=eps[:]).then_inc(S[w], 1)
                            held(r, c + 1)

                        norm("b_sum1_stats", "b_std1", "b_scale1")
                        for j in range(CT):
                            i = ac.activation(tmp[:, j, :], Z[:, j, :], ACT.Identity, scale=rt[:, 2, j:j + 1], bias=rt[:, 3, j:j + 1])
                        i.then_inc(S["b_normed1"], 1)
                        held("b_x1_transposed", c + 1)
                        for k in range(KD):
                            i = ac.activation(QT[:, k * CN:(k + 1) * CN], ps[:, k * CN:(k + 1) * CN], ACT.Identity, scale=lnc[:, k, 0:1], bias=lnc[:, k, 1:2])
                        i.then_inc(S["b_x1T_written"], 1)
                        held("b_hidden_in_psum", c + 1)
                        for m in range(KD):
                            i = ac.activation(HT[:, m, :], ps[:, m * CN:(m + 1) * CN], ACT.Gelu, bias=b1c[:, m:m + 1])
                        i.then_inc(S["b_gelu_done"], 1)
                        norm("b_sum2_stats", "b_std2", "b_scale2")
                        for j in range(CT):
                            i = ac.activation(N2[:, j, :], Z[:, j, :], ACT.Identity, scale=rt[:, 2, j:j + 1], bias=rt[:, 3, j:j + 1])
                        i.then_inc(S["b_normed2"], 1)
                ch.end(NC)
                ac.activation(warm[:, 2 * L + 1:2 * L + 2], eps[:], ACT.Sqrt)

                def routed_rows(c, more):
                    held("stat_rs", v5(L, c))
                    for j in range(CT):
                        i = ac.activation(XN[:, j, :], X[:, bass.ds(c * CT + j, 1), :].rearrange("p a f -> p (a f)"), ACT.Identity,
                                          scale=rs[:, bass.ds(c * CT + j, 1)], bias=nm[:, bass.ds(c * CT + j, 1)])
                    i.then_inc(S["r_rows_normed"], 1)
                    held("r_rows_normed", v5(L, c))
                    ac.activation(acc[:, bass.ds(c * CT * D, CT * D)], XN[:].rearrange("p j f -> p (j f)"), ACT.Copy).then_inc(S["r_rows_copied"], 1)
                    if more:
                        root(2 * L + 1, c + 1)
                    held("r_logits_in_psum", v5(L, c))
                    copyT("r_rows_transposed", "r_xT_written", v5(L, c))
                root(2 * L + 1, 0)
                with ac.Fori(0, NC - 1) as c:
                    routed_rows(c, True)
                routed_rows(NC - 1, False)
                if L == 1:
                    ac.wait_ge(S["logits_shifted"], 1)
                    ac.activation(LG[:, 0:NT * E1], LG[:, 0:NT * E1], ACT.Exp).then_inc(S["logits_exp_done"], 1)
                if L == 0:
                    def turn(q, p):
                        for h in range(2):
                            held("e_rows_transposed", q * 2 + (h + 1))
                            ac.activation(xbT0[h], ps[:, 2 * h * B:2 * h * B + Q0 * D], ACT.Copy).then_inc(S["e_xT_written"], 1)
                        for h in range(2):
                            held("e_hidden_in_psum", q * 2 + (h + 1))
                            for s in range(Q0):
                                i = ac.activation(h0[0:F0, h, s * P:(s + 1) * P], ps[0:F0, (4 + h) * B + s * P:(4 + h) * B + (s + 1) * P], ACT.Relu, bias=wb0(p, h)[0:F0, s, EW - 1:EW])
                            i.then_inc(S["e_hidden_written"], 1)

                    with ac.Fori(0, NB0 // TURN0 // 2) as i2:
                        for p in range(2):
                            turn(i2 * 2 + p, p)
                    turn(NB0 // TURN0 - 1, 0)
                else:
                    with ac.Fori(0, E1 // 2) as i2:
                        for s in range(2):
                            e = i2 * 2 + s
                            held("f_rows_transposed", e + 1)
                            ac.activation(xb1T[:, :, 0:CAP], ps[:, 0:2 * B].rearrange("p (k n) -> p k n", k=2)[:, :, 0:CAP], ACT.Copy).then_inc(S["f_xT_written"], 1)
                            for m in range(MT):
                                held("f_hidden_in_psum", e * MT + (m + 1))
                                ac.activation(h1[:, m, :], ps[:, (2 + m % 4) * B:(2 + m % 4) * B + CAP], ACT.Relu, bias=b11[:, bass.ds(e * MT + m, 1)]).then_inc(S["f_hidden_written"], 1)
                    for c in range(NC):
                        ac.wait_ge(back[c], 32 * CT)
                        for t in range(c * CT, (c + 1) * CT):
                            ch.link(ac.activation(XALL[:, t, :], XALL[:, t, :], ACT.Copy, scale=rt[:, 4, t:t + 1]))
                        ch.join()
                        if c >= 2:
                            ac.wait_ge(S["x_out"], c - 1)
                        y = XALL[:, c * CT:(c + 1) * CT, :]
                        ac.activation(unfit[c % 2], y, ACT.Abs, scale=0.0).then_inc(S["y_scaled"], 1)

        @block.vector
        def _(v):
            ch = Chain(v, S["dve_chain"], S["idle_v"])

            def do(ins):
                ch.link(ins)
                ch.join()

            def held(sem, val):
                v.wait_ge(S[sem], val)
                v.sem_inc(S["idle_v"], 1)

            def flat(t):
                return t[:].rearrange("p j f -> p (j f)")

            def rows(c, j=None):
                return X[:, bass.ds(c * CT, CT), :].rearrange("p j f -> p (j f)") if j is None else X[:, bass.ds(c * CT + j, 1), :].rearrange("p a f -> p (a f)")

            def spread(c):
                for j in range(CT):
                    i = v.bn_stats(st[:, j, :], rows(c, j))
                do(i)
                for j in range(CT):
                    i = v.bn_aggr(mv[:, j, :], st[:, j, :])
                i.then_inc(S["stat"], 1)

            def scales(k, c):
                held("stat_sd", c + (k * NC + 1))
                r = rs[:, bass.ds(c * CT, CT)]
                do(v.reciprocal(r, sd[:]))
                return v.scalar_tensor_tensor(nm[:, bass.ds(c * CT, CT)], mv[:, :, 0], -1.0, r, ALU.mult, ALU.mult)

            def normed(c, sem):
                for j in range(CT):
                    i = v.tensor_scalar(XN[:, j, :], rows(c, j), rs[:, bass.ds(c * CT + j, 1)], nm[:, bass.ds(c * CT + j, 1)], ALU.mult, ALU.add)
                i.then_inc(S[sem], 1)

            def whole_rows(L):
                for c in range(NC):
                    if L == 0:
                        v.wait_ge(x_in[c], 32 if c == NC - 1 else 16)
                    else:
                        v.wait_ge(back[c], 16 * CT)
                        do(v.tensor_tensor(rows(c), rows(c), acc[:, c * CT * D:(c + 1) * CT * D], ALU.add))
                    spread(c)
                    do(scales(2 * L, c))
                    if c == 0:
                        normed(0, "a_rows_normed")

            v.wait_ge(S["start_set"], 3)
            v.wait_ge(S["lists_in"], 16 * len(first))
            lo, hi, ln, cnt, delta, bi = (sm[:, i:i + 1] for i in range(6))
            do(v.tensor_copy(dst[:, 0:ET], oh[:].rearrange("p j n -> p (j n)")[:, 0:ET].bitcast(I32)))
            ch.link(v.tensor_reduce(smi[:, 0:1], dg, AX.X, ALU.min))
            ch.link(v.tensor_reduce(smi[:, 1:2], dg, AX.X, ALU.max))
            do(v.tensor_reduce(smi[:, 2:3], dn, AX.X, ALU.min))
            do(v.tensor_scalar(smi[:], smi[:], 7, None, ALU.arith_shift_right))
            do(v.tensor_copy(sm[:, 0:3], smi[:]))
            ch.link(v.tensor_copy(lo0[:], sm[0:1, 0:1]))
            ch.link(v.scalar_tensor_tensor(cnt, hi, 1.0, lo, ALU.add, ALU.subtract))
            do(v.scalar_tensor_tensor(delta, ln, -1.0, hi, ALU.add, ALU.subtract))
            v.sem_inc(S["pairs_prepared"], 1)
            whole_rows(0)
            v.wait_ge(S["consts"], 6)
            v.wait_ge(S["pairs_summed"], 1)
            do(v.tensor_copy(bi, ps[0:NG, 6 * B:6 * B + 1]))
            do(v.tensor_copy(bi_row[:], ps[0:1, 6 * B + 4:6 * B + 4 + NG]))
            ch.link(v.memset(seg_row[:, 0:1], 0))
            parts = NC * PARTS
            ch.link(v.tensor_copy(seg_row[:, 1:parts], bi_row[:, 0:parts - 1]))
            ch.link(v.tensor_copy(seg_row[:, parts:parts + 1], bi_row[:, NG - 1:NG]))
            ch.link(v.memset(w_row[:, 0:1], NT))
            do(v.tensor_scalar(step, iota[0:NG, 0:MAXN], bi, None, ALU.is_ge))
            v.sem_inc(S["pairs_prepared"], 1)
            for k, q in enumerate(range(0, MAXN, 512)):
                m = min(512, MAXN - q)
                v.wait_ge(S["pairs_summed"], 2 + k)
                ch.link(v.tensor_scalar(g_row[0:1, q:q + m], ps[0:1, 6 * B:6 * B + m], float(NG - 1), None, ALU.min))
                do(v.scalar_tensor_tensor(w_row[0:1, 1 + q:1 + q + m], ps[0:1, 7 * B:7 * B + m], lo0[0:1, 0:1], iota[0:1, q:q + m], ALU.add, ALU.add))
                v.sem_inc(S["pairs_listed"], 1)
            ch.link(v.memset(KV[:], 0.0))
            do(v.scalar_tensor_tensor(g_row, g_row, float(1 << 5), w_row[:, 1:MAXN + 1], ALU.mult, ALU.add))
            do(v.tensor_scalar(g_row, g_row, float(1 << 7), None, ALU.mult))
            do(v.scalar_tensor_tensor(pair_row[:], w_row[:, 0:MAXN], float(1 << 19), g_row, ALU.mult, ALU.add))
            do(v.memset(ring4[:, :, :, D:AP_], 1.0))
            v.sem_inc(S["pairs_listed"], 1)
            v.wait_ge(S["loaded"], 16 * len(loads))
            ch.link(v.tensor_tensor(brow[0:1, 0, :], brow[0:1, 0, :], brow[0:1, 1, :], ALU.add))
            do(v.tensor_tensor(lng[:, 1, :], lng[:, 1, :], lng[:, 4, :], ALU.add))

            reached = [None]

            def segment(L, c, n0, k0, k1):
                s0 = v.value_load(seg_row[0:1, bass.ds(c * PARTS, 1)], min_val=0, max_val=MAXN) if k0 == 0 else reached[0]
                s1 = v.value_load(seg_row[0:1, bass.ds(c * PARTS + k1, 1)], min_val=1, max_val=MAXN)
                reached[0] = s1
                with v.Fori(s0, s1) as n:
                    pr = v.value_load(pair_row[0:1, bass.ds(n, 1)], min_val=0, max_val=((NT + 1) << 19) - 1)
                    g4 = v.snap(pr // (1 << 12) % 128 * GT, min_val=0, max_val=(NG - 1) * GT)
                    w128 = v.snap(pr % 4096, min_val=0, max_val=NT * P)
                    wp = v.snap(pr // (1 << 19) * AP_, min_val=0, max_val=NT * AP_)
                    for h in range(2):
                        v.wait_ge(S["half_used"], (n + n0) * 2 + (h + 1))
                        v.tensor_tensor(oh[:, GH * h:GH * (h + 1), :], iota[:, bass.ds(w128, P)].unsqueeze(1).to_broadcast([P, GH, P]),
                                        dst[:, bass.ds(g4 + GH * h, GH)].unsqueeze(2).to_broadcast([P, GH, P]), ALU.is_equal).then_inc(S["oh_half"], 1)
                    v.wait_ge(S["added"], n + n0 + (1 + L))
                    r = acc[:, bass.ds(wp, AP_)]
                    v.tensor_tensor(r, r, ps[:, bass.ds(((n + n0 + 1) % 2) * B + 6 * B, AP_)], ALU.add).then_inc(S["added"], 1)

            for L in range(2):
                nE = (E0, E1)[L]
                if L == 1:
                    v.wait_ge(S["deg_sd"], 1)
                    ch.link(v.reciprocal(dinv[:], dinv[:]))
                    do(v.memset(KV[:], 0.0))
                    whole_rows(1)
                k_ps = ps[:, 0:CT * B].rearrange("p (j f) -> p j f", f=B)[:, :, 0:D]
                kv_ps = ps[:, 0:2 * B].rearrange("p (a f) -> p a f", a=2)[:, :, 0:P + 1]

                def heads():
                    ch.link(v.memset(KVb[:], 0.0))
                    if L == 1:
                        ch.link(v.memset(KS[:], 0.0))
                    ch.join()
                    for q in range(2):
                        for h in range(HH):
                            r = slice(HD * h, HD * (h + 1))
                            ch.link(v.tensor_copy(KVb[r, q, HD * h:HD * (h + 1)], KV[r, q, HD * h:HD * (h + 1)]))
                            if L == 0:
                                ch.link(v.tensor_copy(KVb[r, q, P + h:P + h + 1], KV[r, q, P:P + 1]))
                            else:
                                ch.link(v.tensor_copy(KS[r, q, HD * h:HD * (h + 1)], KV[r, q, P:P + 1].to_broadcast([HD, HD])))
                    ch.join()
                    v.sem_inc(S["kv_ready"], 1)

                def features(c, more):
                    for q in range(2):
                        ch.link(v.tensor_copy(Vb[:, :, q, P], valid[:, bass.ds(c * CT, CT)]))
                    held("a_values_written", v5(L, c))
                    v.scalar_tensor_tensor(Kb[:], k_ps, 0.0, ex[:], ALU.max, ALU.add).then_inc(S["a_keys_written"], 1)
                    if more:
                        normed(c + 1, "a_rows_normed")

                def messages(c, more):
                    features(c, more)
                    held("a_messages_in_sbuf", c + 1)
                    for r in range(4):
                        for j in range(CT):
                            i = v.max(m8[:, j, :], (Hs if r == 0 else Wk)[:, j, :])
                        do(i)
                        for j in range(CT):
                            i = v.match_replace(Wk[:, j, :], m8[:, j, :], (Hs if r == 0 else Wk)[:, j, :], SENT)
                        do(i)
                        if r == 0:
                            keys_values(c)
                    do(v.tensor_tensor(flat(Wk), flat(Wk), flat(Hs), ALU.not_equal))
                    v.tensor_tensor(flat(Hs), flat(Wk), flat(Hs), ALU.mult).then_inc(S["a_messages_final"], 1)
                    if not more:
                        heads()

                def scaled(c, more):
                    features(c, more)
                    held("a_messages_in_sbuf", v5(L, c))
                    v.tensor_copy(a3[:, bass.ds(c * CT, CT), 0:D], Hs[:]).then_inc(S["a_messages_final"], 1)
                    keys_values(c)
                    if not more:
                        heads()

                def keys_values(c):
                    held("a_ktv_in_psum", v5(L, c))
                    v.tensor_tensor(KV[:], KV[:], kv_ps, ALU.add).then_inc(S["a_ktv_added"], 1)
                    v.wait_ge(S["a_ktv_added"], v5(L, c) + 1)
                    v.sem_inc(S["idle_v"], 1)

                with v.Fori(0, NC - 1) as c:
                    ch.loop(c, 11 if L == 0 else 2)
                    (messages, scaled)[L](c, True)
                ch.end(NC - 1)
                (messages, scaled)[L](NC - 1, False)
                n0 = 0
                if L == 1:
                    n0 = v.snap(v.value_load(bi_row[0:1, NG - 1:NG], min_val=NG, max_val=MAXN))
                else:
                    v.wait_ge(S["zeroed"], 16 * 2 * (NC - 1))
                v.memset(ps[:, 6 * B:8 * B], 0.0).then_inc(S["pairs_listed"], 1)
                v.wait_ge(S["pairs_listed"], -(-MAXN // 512) + 2 + L)
                with v.Fori(0, NC) as c:
                    segment(L, c, n0, 0, (1, 2)[L])
                    held("b_exp_done", v5(L, c))
                    v.scalar_tensor_tensor(QT, ps[:, 0:KD * CN], 0.0, flat(ex), ALU.max, ALU.add).then_inc(S["b_q_written"], 1)
                    if L == 0:
                        ch.loop(c, 15)
                        held("b_rows_normed", c + 1)
                        held("b_self_in_psum", c + 2)
                        do(v.tensor_tensor(rows(c), rows(c), ps[:, 3 * B:3 * B + CT * D], ALU.add))
                        segment(L, c, n0, 1, 2)
                        held("b_attn_in_psum", c + 1)
                        do(v.tensor_scalar(den, ps[:, CT * D:CT * D + CT * H], 1e-6, None, ALU.add))
                        do(v.reciprocal(den, den))
                        do(v.tensor_tensor(flat(Hs).rearrange("p (h f) -> p h f", f=HD), ps[:, 0:CT * D].rearrange("p (h f) -> p h f", f=HD),
                                           den.unsqueeze(2).to_broadcast([P, CT * H, HD]), ALU.mult))
                        do(v.tensor_tensor(flat(Z), flat(Hs), flat(XN), ALU.add))

                        def norm(z, w, r, n, nb, gi, last, k):
                            for j in range(CT):
                                i = v.bn_stats(st[:, j, :], Z[:, j, :])
                            do(i)
                            for j in range(CT):
                                i = v.bn_aggr(rt[:, 0, 2 * j:2 * j + 2], st[:, j, :])
                            i.then_inc(S[z], 1)
                            segment(L, c, n0, k, k + 1)
                            held(w, c + 1)
                            do(v.reciprocal(rt[:, 2, 0:CT], rt[:, 1, 0:CT]))
                            v.scalar_tensor_tensor(rt[:, 3, 0:CT], rt[:, 0, 0:2 * CT].rearrange("p (j s) -> p j s", s=2)[:, :, 0], -1.0,
                                                   rt[:, 2, 0:CT], ALU.mult, ALU.mult).then_inc(S[r], 1)
                            if nb is tmp:
                                segment(L, c, n0, k + 1, k + 2)
                            held(n, c + 1)
                            do(v.tensor_tensor(last, nb, lng[:, gi, :].unsqueeze(1).to_broadcast([P, CT, D]), ALU.mult))
                            return v.tensor_tensor(last, last, lng[:, gi + 1, :].unsqueeze(1).to_broadcast([P, CT, D]), ALU.add)

                        do(norm("b_sum1_stats", "b_std1", "b_scale1", "b_normed1", tmp, 0, X1[:], 2))
                        segment(L, c, n0, 4, 6)
                        held("b_y_in_psum", c + 1)
                        do(v.tensor_tensor(flat(Z), flat(X1), ps[:, 3 * B:3 * B + CT * D], ALU.add))
                        v.sem_inc(S["b_y_read"], 1)
                        do(norm("b_sum2_stats", "b_std2", "b_scale2", "b_normed2", N2, 2, N2, 6))
                        do(v.tensor_tensor(rows(c), rows(c), N2.rearrange("p j f -> p (j f)"), ALU.add))
                    else:
                        ch.loop(c, 2)
                        segment(L, c, n0, 2, 4)
                        held("b_den_in_psum", c + 1)
                        do(v.tensor_scalar(flat(ex), ps[:, 0:KD * CN], 1e-6, None, ALU.max))
                        do(v.reciprocal(flat(ex), flat(ex)))
                        v.tensor_tensor(QT, QT, flat(ex), ALU.mult).then_inc(S["b_q_scaled"], 1)
                        segment(L, c, n0, 4, 6)
                        held("b_y_in_psum", c + (NC + 1))
                        v.tensor_tensor(rows(c), rows(c), ps[:, 3 * B:3 * B + CT * D], ALU.add).then_inc(S["b_y_read"], 1)
                        segment(L, c, n0, 6, 7)
                ch.end(NC)
                nl = v.value_load(bi_row[0:1, NG - 1:NG], min_val=NG, max_val=MAXN - 2)
                pr = v.value_load(pair_row[0:1, bass.ds(nl, 1)], min_val=0, max_val=((NT + 1) << 19) - 1)
                w = v.snap(pr // (1 << 19), min_val=0, max_val=NT)
                v.wait_ge(S["half_used"], (nl + n0) * 2 + 2)
                v.sem_inc(S["idle_v"], 1)
                v.wait_ge(S["added"], nl + n0 + (1 + L))
                r = acc[:, bass.ds(w * AP_, AP_)]
                v.tensor_tensor(r, r, ps[:, bass.ds(((nl + n0 + 1) % 2) * B + 6 * B, AP_)], ALU.add).then_inc(S["added"], 1)
                v.wait_ge(S["added"], nl + n0 + (2 + L))
                v.sem_inc(S["agg_done"], 1)
                if L == 0:
                    do(v.tensor_copy(deg[:], a3[:, 0:NT, D]))
                    v.sem_inc(S["deg_ready"], 1)
                    do(v.tensor_scalar(rdeg[:], deg[:], 1.0, None, ALU.max))
                    do(v.reciprocal(rdeg[:], rdeg[:]))
                share = (rdeg, dinv)[L]

                def whole(c):
                    for j in range(CT):
                        i = v.scalar_tensor_tensor(rows(c, j), acc[:, bass.ds((c * CT + j) * AP_, D)], share[:, bass.ds(c * CT + j, 1)], rows(c, j), ALU.mult, ALU.add)
                    do(i)
                    spread(c)
                    scales(2 * L + 1, c).then_inc(S["stat_rs"], 1)

                ohv = OH[:, 0:NT * nE].rearrange("p (t e) -> p t e", e=nE)

                def choice(lg, n, t0):
                    for t in range(n):
                        i = v.max(mx[:, 8 * t:8 * t + 8], lg[:, t, :])
                    do(i)
                    for t in range(n):
                        i = v.max_index(mi[:, 8 * t:8 * t + 8], mx[:, 8 * t:8 * t + 8], lg[:, t, :])
                    do(i)
                    do(v.tensor_copy(mif[:, 0:n], mi[:, 0:8 * n].rearrange("p (t s) -> p t s", s=8)[:, :, 0]))
                    o_ = ohv[:, bass.ds(t0, n), :]
                    do(v.tensor_tensor(o_, iota[:, 0:nE].unsqueeze(1).to_broadcast([P, n, nE]), mif[:, 0:n].unsqueeze(2).to_broadcast([P, n, nE]), ALU.is_equal))
                    do(v.tensor_tensor(o_, o_, valid[:, bass.ds(t0, n)].unsqueeze(2).to_broadcast([P, n, nE]), ALU.mult))

                def logits(c):
                    held("r_logits_in_psum", v5(L, c) + 1)
                    r0 = (0, E0)[L]
                    l_ = LG[:, 0:CT * nE] if L == 0 else LG[:, bass.ds(c * (CT * nE), CT * nE)]
                    do(v.tensor_tensor(l_.rearrange("p (j e) -> p j e", e=nE), ps[:, 4 * B:4 * B + CT * nE].rearrange("p (j e) -> p j e", e=nE),
                                       rrow[:, r0:r0 + nE].unsqueeze(1).to_broadcast([P, CT, nE]), ALU.add))
                    v.sem_inc(S["r_logits_read"], 1)
                    if L == 0:
                        choice(l_.rearrange("p (j e) -> p j e", e=nE), CT, c * CT)

                whole(0)
                whole(1)
                with v.Fori(0, NC - 2) as c:
                    ch.loop(c, (9, 4)[L])
                    whole(c + 2)
                    logits(c)
                ch.end(NC - 2)
                logits(NC - 2)
                logits(NC - 1)
                if L == 1:
                    lg = LG[:, 0:NT * nE].rearrange("p (t e) -> p t e", e=nE)
                    do(v.tensor_reduce(t25, lg, AX.X, ALU.max))
                    do(v.tensor_tensor(lg, lg, t25.unsqueeze(2).to_broadcast([P, NT, nE]), ALU.subtract))
                    v.sem_inc(S["logits_shifted"], 1)
                    v.wait_ge(S["logits_exp_done"], 1)
                    do(v.tensor_reduce(se, lg, AX.X, ALU.add))
                    do(v.reciprocal(se, se))
                    do(v.tensor_tensor(lg, lg, se.unsqueeze(2).to_broadcast([P, NT, nE]), ALU.mult))
                    choice(lg, NT, 0)
                v.sem_inc(S["oh_ready"], 1)
                W, W1 = NT * nE, (NT + 1) * nE
                TTv, INv, MKv = (t[:, 0:W1].rearrange("p (e t) -> p e t", t=NT + 1) for t in (TT, IN, MSK))
                prv = PR[:, 0:W].rearrange("p (t e) -> p t e", e=nE)
                do(v.memset(MSK[:, 0:W1], 1.0))
                ch.link(v.memset(MKv[:, :, 0:1], 0.0))
                do(v.memset(TTv[:, :, 0:1], 0.0))
                v.wait_ge(S["ranks_in_psum"], L + 1)
                do(v.tensor_copy(TTv[:, :, 1:NT + 1], ps[:, 2 * B:2 * B + W].rearrange("p (t e) -> p e t", e=nE)))
                if L == 0:
                    do(v.tensor_reduce(cntE, TTv, AX.X, ALU.add))
                    do(v.tensor_scalar(nbE, cntE, float(P - 1), None, ALU.add))
                    do(v.tensor_copy(nbEi, nbE))
                    do(v.tensor_scalar(nbEi, nbEi, 7, None, ALU.arith_shift_right))
                    do(v.tensor_copy(nbE, nbEi))
                    do(v.tensor_tensor_scan(CE, ones[:, 0:E0], nbE, 0.0, ALU.mult, ALU.add))
                    do(v.tensor_tensor(baseE, CE, nbE, ALU.subtract))
                    do(v.tensor_scalar(TTv[:, :, 0], baseE, float(P), None, ALU.mult))
                do(v.tensor_tensor_scan(IN[:, 0:W1], MSK[:, 0:W1], TT[:, 0:W1], 0.0, ALU.mult, ALU.add))
                do(v.tensor_tensor(prv, ps[:, 0:W].rearrange("p (t e) -> p t e", e=nE), INv[:, :, 0:NT].rearrange("p e t -> p t e"), ALU.add))
                do(v.tensor_tensor(prv, prv, ohv, ALU.mult))
                do(v.tensor_reduce(rank, prv, AX.X, ALU.add))
                if L == 0:
                    ch.link(v.tensor_copy(gidx[:], rank))
                    do(v.tensor_scalar(kept, valid[:], -FAR, FAR, ALU.mult, ALU.add))
                    do(v.tensor_tensor(t25, rank, kept, ALU.add))
                    do(v.tensor_copy(sidx[:], t25))
                    v.sem_inc(S["routed"], 1)
                    eb3 = ebc[0:1, :].rearrange("p (b e) -> p b e", e=E0)
                    ch.link(v.memset(h0[F0:F0 + 1, :, :], 1.0))
                    do(v.tensor_tensor(eb3, iota[0:1, 0:NB0].unsqueeze(2).to_broadcast([1, NB0, E0]), CE[0:1, :].unsqueeze(1).to_broadcast([1, NB0, E0]), ALU.is_ge))
                    do(v.tensor_reduce(ebf[0:1, :], eb3, AX.X, ALU.add))
                    do(v.tensor_scalar(ebi[:], ebf[0:1, :], float(E0 - 1), None, ALU.min))
                    v.sem_inc(S["blocks_named"], 1)
                else:
                    ch.link(v.tensor_scalar(pos, mif, float(CAP), None, ALU.mult))
                    do(v.tensor_scalar(kept, rank, float(CAP), None, ALU.is_lt))
                    ch.link(v.tensor_tensor(rt[:, 4, :], se, kept, ALU.mult))
                    ch.link(v.tensor_tensor(t25, pos, rank, ALU.add))
                    do(v.tensor_scalar(rank, rank, float(CAP - 1), None, ALU.min))
                    ch.link(v.tensor_tensor(kept, kept, valid[:], ALU.mult))
                    do(v.tensor_tensor(pos, pos, rank, ALU.add))
                    ch.link(v.tensor_copy(gidx[:], pos))
                    do(v.tensor_scalar(kept, kept, -FAR, FAR, ALU.mult, ALU.add))
                    do(v.tensor_tensor(t25, t25, kept, ALU.add))
                    do(v.tensor_copy(sidx[:], t25))
                    v.sem_inc(S["routed"], 1)
                if L == 0:
                    def turn(q):
                        for h in range(2):
                            v.wait_ge(e_put[h], (q + 1) * 16)
                            v.sem_inc(S["idle_v"], 1)
                            held("e_y_in_psum", q * 2 + (h + 2))
                            v.tensor_scalar(y0[h], ps[:, (6, 0)[h] * B:(6, 0)[h] * B + Q0 * D], 0.0, None, ALU.max).then_inc(S["e_y_written"], 1)

                    with v.Fori(0, NB0 // TURN0) as q:
                        turn(q)
                else:
                    with v.Fori(0, E1 // 2) as i2:
                        for s in range(2):
                            e = i2 * 2 + s
                            held("f_y_stored", (e * 2 + 1) * 16)
                            held("f_y_in_psum", e + 1)
                            v.tensor_copy(y1.rearrange("p s f -> p (s f)")[:, 0:(ST - 1) * D], ps[:, 6 * B:6 * B + (ST - 1) * D])
                            v.tensor_copy(y1[0:STAIL, ST - 1, :], ps[0:STAIL, 6 * B + (ST - 1) * D:8 * B]).then_inc(S["f_y_written"], 1)
                    for c in range(NC):
                        v.wait_ge(S["y_scaled"], c + 1)
                        y = XALL[:, c * CT:(c + 1) * CT, :]
                        ch.link(v.tensor_scalar(Wk[:], y, 0.0, 1.0e4, ALU.is_gt, ALU.mult))
                        do(v.tensor_scalar(Hs[:], y, 0.0, -1.0e4, ALU.is_lt, ALU.mult))
                        do(v.tensor_tensor(flat(Wk), flat(Wk), flat(Hs), ALU.add))
                        do(v.copy_predicated(y, unfit[c % 2].bitcast(I32), Wk[:]))
                        v.tensor_tensor(rows(c), rows(c), acc[:, c * CT * D:(c + 1) * CT * D], ALU.add).then_inc(S["x_out"], 1)

        @block.tensor
        def _(pe):
            mm = nc.tensor.matmul
            tp = nc.tensor.transpose

            def held(sem, val):
                pe.wait_ge(S[sem], val)
                pe.sem_inc(S["idle_t"], 1)

            def transposes(srcb, sem, at=0):
                for j in range(CT):
                    for k in range(KD):
                        i = tp(ps[:, at + k * CN + j * P:at + k * CN + (j + 1) * P], srcb[:, j, k * P:(k + 1) * P], ident[:])
                i.then_inc(S[sem], 1)

            def keys_and_values():
                for j in range(CT):
                    for k in range(KD):
                        i = mm(ps[:, j * B:(j + 1) * B], xT[:, k, j * P:(j + 1) * P], wqkv[:, k, D:3 * D], start=k == 0, stop=k == KD - 1)
                i.then_inc(S["a_kv_in_psum"], 1)

            pe.wait_ge(S["made"], 3)
            pe.wait_ge(S["pairs_prepared"], 1)
            cnt, delta = sm[:, 3:4], sm[:, 4:5]
            mm(ps[0:NG, 6 * B:6 * B + 1], tri[0:NG, 0:NG], cnt, start=True, stop=True)
            mm(ps[0:1, 6 * B + 4:6 * B + 4 + NG], cnt, tri[0:NG, 0:NG], start=True, stop=True).then_inc(S["pairs_summed"], 1)
            pe.wait_ge(S["a_rows_normed"], 1)
            transposes(XN, "a_rows_transposed", 2 * B)
            pe.wait_ge(S["early_in"], 16 * len(early))
            pe.wait_ge(S["a_xT_written"], 1)
            keys_and_values()
            pe.wait_ge(S["pairs_prepared"], 2)
            for k, q in enumerate(range(0, MAXN, 512)):
                m = min(512, MAXN - q)
                if k:
                    pe.wait_ge(S["pairs_listed"], k)
                mm(ps[0:1, 6 * B:6 * B + m], ones[0:NG, 0:1], step[:, q:q + m], start=True, stop=True)
                mm(ps[0:1, 7 * B:7 * B + m], delta, step[:, q:q + m], start=True, stop=True).then_inc(S["pairs_summed"], 1)
            pe.wait_ge(S["pairs_listed"], -(-MAXN // 512))
            pe.wait_ge(S["loaded"], 16 * len(loads))

            pieces = [(0, B), (B, CN)], [(0, 2 * B - CN), (2 * B - CN, CN)]

            def across(stationary, moving, k):
                for m in range(KD):
                    for a0, a1 in pieces[m]:
                        for q in k(m):
                            i = mm(ps[:, m * CN + a0:m * CN + a1], stationary(q, m), moving(q)[:, a0:a1], start=q == k(m)[0], stop=q == k(m)[-1])
                return i

            reached = [None]

            def segment(L, c, n0, k0, k1):
                s0 = pe.value_load(seg_row[0:1, bass.ds(c * PARTS, 1)], min_val=0, max_val=MAXN) if k0 == 0 else reached[0]
                s1 = pe.value_load(seg_row[0:1, bass.ds(c * PARTS + k1, 1)], min_val=1, max_val=MAXN)
                reached[0] = s1
                with pe.Fori(s0, s1) as n:
                    pr = pe.value_load(pair_row[0:1, bass.ds(n, 1)], min_val=0, max_val=((NT + 1) << 19) - 1)
                    g = pe.snap(pr // (1 << 12) % 128, min_val=0, max_val=NG - 1)
                    pe.wait_ge(S["landed"], g + (NG * L + 1))
                    pe.sem_inc(S["idle_t"], 1)
                    for h in range(2):
                        pe.wait_ge(S["oh_half"], (n + n0) * 2 + (h + 1))
                        for j in range(GH * h, GH * (h + 1)):
                            i = mm(ps[:, bass.ds(((n + n0) % 2) * B + 6 * B, AP_)], oh[:, j, :],
                                   ring[:, bass.ds((g % R) * (GT * AP_) + j * AP_, AP_)], start=j == 0, stop=j == GT - 1)
                        i.then_inc(S["half_used"], 1)

            for L in range(2):
                if L == 1:
                    pe.wait_ge(S["weights1_loaded"], 48)
                def chunk(c, more):
                    for j in range(CT):
                        for k in range(KD):
                            i = mm(ps[:, 5 * B + j * D:5 * B + (j + 1) * D], xT[:, k, j * P:(j + 1) * P], wn[:, k, :], start=k == 0, stop=k == KD - 1)
                    i.then_inc(S["a_messages_in_psum"], 1)
                    held("a_keys_written", v5(L, c))
                    for q in range(2):
                        for j in range(CT):
                            i = mm(ps[:, q * B:q * B + P + 1], Kb[:, j, q * P:(q + 1) * P], Vb[:, j, q, :], start=j == 0, stop=j == CT - 1)
                    i.then_inc(S["a_ktv_in_psum"], 1)
                    if more:
                        held("a_rows_normed", v5(L, c) + 1)
                        transposes(XN, "a_rows_transposed", 2 * B)
                        held("a_xT_written", v5(L, c) + 1)
                        held("a_ktv_added", v5(L, c) + 1)
                        keys_and_values()

                if L == 1:
                    pe.wait_ge(S["a_rows_normed"], v5(L, 0))
                    transposes(XN, "a_rows_transposed", 2 * B)
                    pe.wait_ge(S["a_xT_written"], v5(L, 0))
                    keys_and_values()
                with pe.Fori(0, NC - 1) as c:
                    chunk(c, True)
                chunk(NC - 1, False)
                pe.wait_ge(S["a_ktv_added"], NC * (L + 1) + 1)
                pe.wait_ge(S["a_messages_in_sbuf"], NC * (L + 1))
                n0 = 0
                if L == 1:
                    pe.wait_ge(S["kv_ready"], 2)
                    for q in range(2):
                        i = tp(ps[:, q * P:(q + 1) * P], KVb[:, q, 0:P], ident[:])
                    i.then_inc(S["context_in_psum"], 1)
                    pe.wait_ge(S["context_in_sbuf"], 1)
                    for q in range(2):
                        i = mm(ps[:, B + q * D:B + (q + 1) * D], CTx[:, q, :], wm1[:, q, :], start=True, stop=True)
                    i.then_inc(S["mproj_in_psum"], 1)
                    pe.wait_ge(S["mproj_written"], 1)
                    n0 = pe.snap(pe.value_load(bi_row[0:1, NG - 1:NG], min_val=NG, max_val=MAXN))
                with pe.Fori(0, NC) as c:
                    held("b_xT_loaded", v5(L, c) * 16)
                    both = lambda m: (0, 1)
                    across(lambda k, m: wqkv[:, k, m * P:(m + 1) * P], lambda k: xT[:, k, :], both).then_inc(S["b_q_in_psum"], 1)
                    if L == 0:
                        held("b_y_read", c + 1)
                        for j in range(CT):
                            for k in range(KD):
                                i = mm(ps[:, 3 * B + j * D:3 * B + (j + 1) * D], xT[:, k, j * P:(j + 1) * P], ws[:, k, :], start=k == 0, stop=k == KD - 1)
                        i.then_inc(S["b_self_in_psum"], 1)
                        pe.wait_ge(S["kv_ready"], 1)
                        segment(L, c, n0, 0, 1)
                        held("b_q_written", c + 1)
                        for j in range(CT):
                            for q in range(2):
                                x = QT[:, q * CN + j * P:q * CN + (j + 1) * P]
                                mm(ps[:, (j * 2 + q) * P:(j * 2 + q + 1) * P], x, KVb[:, q, 0:P], start=True, stop=True)
                                i = mm(ps[:, CT * D + (j * 2 + q) * HH:CT * D + (j * 2 + q + 1) * HH], x, KVb[:, q, P:P + HH], start=True, stop=True)
                        i.then_inc(S["b_attn_in_psum"], 1)
                        segment(L, c, n0, 1, 4)
                        held("b_normed1", c + 1)
                        transposes(tmp, "b_x1_transposed")
                        held("b_x1T_written", c + 1)
                        across(lambda k, m: wm1[:, k, m * P:(m + 1) * P], lambda k: QT[:, k * CN:(k + 1) * CN], both).then_inc(S["b_hidden_in_psum"], 1)
                        segment(L, c, n0, 4, 5)
                        held("b_gelu_done", c + 1)
                        for j in range(CT):
                            for k in range(KD):
                                i = mm(ps[:, 3 * B + j * D:3 * B + (j + 1) * D], HT[:, k, j * P:(j + 1) * P], wm2[:, k, :], start=k == 0, stop=k == KD - 1)
                        i.then_inc(S["b_y_in_psum"], 1)
                    else:
                        segment(L, c, n0, 0, 2)
                        held("b_q_written", v5(L, c))
                        across(lambda k, m: KS[:, m, :], lambda m: QT[:, m * CN:(m + 1) * CN], lambda m: (m,)).then_inc(S["b_den_in_psum"], 1)
                        segment(L, c, n0, 2, 4)
                        held("b_q_scaled", c + 2)
                        held("b_y_read", v5(L, c))
                        for j in range(CT):
                            o_ = ps[:, 3 * B + j * D:3 * B + (j + 1) * D]
                            mm(o_, ones[0:1, :], brow[0:1, 0, :], start=True, stop=False)
                            for q in range(2):
                                i = mm(o_, QT[:, q * CN + j * P:q * CN + (j + 1) * P], Mx[:, q, :], start=False, stop=q == 1)
                        i.then_inc(S["b_y_in_psum"], 1)
                    segment(L, c, n0, (5, 4)[L], 7)
                nE = (E0, E1)[L]
                rwl = (rw, gw)[L]
                with pe.Fori(0, NC) as c:
                    held("r_rows_normed", v5(L, c))
                    transposes(XN, "r_rows_transposed")
                    held("r_xT_written", v5(L, c))
                    held("r_logits_read", v5(L, c))
                    for j in range(CT):
                        o_ = ps[:, 4 * B + j * nE:4 * B + (j + 1) * nE]
                        for k in range(KD):
                            i = mm(o_, xT[:, k, j * P:(j + 1) * P], rwl[:, k, :], start=k == 0, stop=k == KD - 1)
                    i.then_inc(S["r_logits_in_psum"], 1)
                pe.wait_ge(S["oh_ready"], L + 1)
                W = NT * nE
                for a0 in range(0, W, B):
                    a1 = min(a0 + B, W)
                    mm(ps[:, a0:a1], tris[:], OH[:, a0:a1], start=True, stop=True)
                    i = mm(ps[:, 2 * B + a0:2 * B + a1], ones[:], OH[:, a0:a1], start=True, stop=True)
                i.then_inc(S["ranks_in_psum"], 1)
                if L == 0:
                    def turn(q, p, full):
                        for h in range(2):
                            if h == 0:
                                held("e_y_written", q * 2 + 1)
                            pe.wait_ge(e_in[p][h], full)
                            pe.sem_inc(S["idle_t"], 1)
                            for s in range(Q0):
                                for k in range(KD):
                                    i = tp(ps[:, 2 * h * B + s * D + k * P:2 * h * B + s * D + (k + 1) * P], xb0(p, h)[:, s, k * P:(k + 1) * P], ident[:])
                            i.then_inc(S["e_rows_transposed"], 1)
                        for h in range(2):
                            held("e_xT_written", q * 2 + (h + 1))
                            for s in range(Q0):
                                for k in range(KD):
                                    i = mm(ps[0:F0, (4 + h) * B + s * P:(4 + h) * B + (s + 1) * P], wb0(p, h)[:, s, k * F0:(k + 1) * F0],
                                           xbT0[h][:, s * D + k * P:s * D + (k + 1) * P], start=k == 0, stop=k == KD - 1)
                            i.then_inc(S["e_hidden_in_psum"], 1)
                        for h in range(2):
                            held("e_hidden_written", q * 2 + (h + 1))
                            for s in range(Q0):
                                i = mm(ps[:, (6, 0)[h] * B + s * D:(6, 0)[h] * B + (s + 1) * D], h0[0:F0 + 1, h, s * P:(s + 1) * P],
                                       wb0(p, h)[0:F0 + 1, s, KD * F0:KD * F0 + D], start=True, stop=True)
                            i.then_inc(S["e_y_in_psum"], 1)

                    per = 16 * (Q0 + 1)
                    with pe.Fori(0, NB0 // TURN0 // 2) as i2:
                        for p in range(2):
                            turn(i2 * 2 + p, p, (i2 + 1) * per)
                    turn(NB0 // TURN0 - 1, 0, (NB0 // TURN0 // 2 + 1) * per)
                else:
                    def turned(e, s, full):
                        pe.wait_ge(f_in[s], full)
                        pe.sem_inc(S["idle_t"], 1)
                        for t in range(ST):
                            rws = P if t < ST - 1 else STAIL
                            for k in range(KD):
                                i = tp(ps[:, k * B + t * P:k * B + t * P + rws], xb1[s][0:rws, t, k * P:(k + 1) * P], ident[0:rws, 0:rws])
                        i.then_inc(S["f_rows_transposed"], 1)

                    def expert(e, s, nxt):
                        held("f_xT_written", e + 1)
                        for m in range(MT):
                            held("f_hidden_written", e * MT + (m + 1))
                            for k in range(KD):
                                i = mm(ps[:, (2 + m % 4) * B:(2 + m % 4) * B + CAP], w11[:, s, k, m * P:(m + 1) * P], xb1T[:, k, 0:CAP], start=k == 0, stop=k == KD - 1)
                            i.then_inc(S["f_hidden_in_psum"], 1)
                        if nxt is not None:
                            turned(e + 1, 1 - s, nxt)
                        held("f_hidden_written", e * MT + (MT + 4))
                        held("f_y_written", e + 1)
                        for t in range(ST):
                            rws = P if t < ST - 1 else STAIL
                            o_ = ps[0:rws, 6 * B + t * D:6 * B + (t + 1) * D]
                            mm(o_, ones[0:1, 0:rws], b21[0:1, s, :], start=True, stop=False)
                            for m in range(MT):
                                i = mm(o_, h1[:, m, t * P:t * P + rws], w21[:, s, m, :], start=False, stop=m == MT - 1)
                        i.then_inc(S["f_y_in_psum"], 1)

                    per = 16 * 5
                    turned(0, 0, per)
                    with pe.Fori(0, E1 // 2 - 1) as i2:
                        expert(i2 * 2, 0, (i2 + 1) * per)
                        expert(i2 * 2 + 1, 1, (i2 + 2) * per)
                    expert(E1 - 2, 0, E1 // 2 * per)
                    expert(E1 - 1, 1, None)


def kernel(**inputs):
    import numpy as _np
    import concourse.bacc as _bacc
    from concourse import mybir as _mybir
    from concourse.bass_utils import run_bass_kernel_spmd as _run

    nc = _bacc.Bacc("TRN2", target_bir_lowering=False, num_devices=1)
    g = {k: _np.asarray(v) for k, v in inputs.items()}
    ep = NG * GE - E

    def halves(w):
        return w.reshape(KD, P, -1).transpose(1, 0, 2)

    dgrp = _np.pad(g["dst"], (0, ep), mode="edge").reshape(NG, GE)
    ew = _np.zeros((E0, P, EW), _np.float32)
    ew[:, :, 0:KD * F0] = g["L0_ffn_W1"].reshape(E0, KD, P, F0).transpose(0, 2, 1, 3).reshape(E0, P, KD * F0)
    ew[:, 0:F0, KD * F0:KD * F0 + D] = g["L0_ffn_W2"]
    ew[:, F0, KD * F0:KD * F0 + D] = g["L0_ffn_b2"]
    ew[:, 0:F0, EW - 1] = g["L0_ffn_b1"]
    a = {
        "x": g["x"],
        "srcT": _np.pad(g["src"], (0, ep)).reshape(ET, P).T,
        "dstT": _np.pad(g["dst"], (0, ep), constant_values=-1).reshape(ET, P).T,
        "dgrp": dgrp,
        "dnext": _np.concatenate([dgrp[1:], _np.full((1, GE), NT * P, dgrp.dtype)]),
        "wn": halves(g["L0_gnn_W_neigh"]),
        "ws": halves(g["L0_gnn_W_self"]),
        "wqkv0": halves(g["L0_mix_Wqkv"].T),
        "wm1": halves(g["L0_mix_W1"].T),
        "wm2": halves(g["L0_mix_W2"].T),
        "lng": _np.broadcast_to(_np.stack([g["L0_mix_ln1_g"], g["L0_mix_ln1_b"], g["L0_mix_ln2_g"], g["L0_mix_ln2_b"], g["L0_mix_b2"]]), (P, 5, D)),
        "lnc": _np.stack([g["L0_mix_ln1_g"], g["L0_mix_ln1_b"]], axis=1).reshape(KD, P, 2).transpose(1, 0, 2),
        "b1c": g["L0_mix_b1"].reshape(KD, P).T,
        "b1rows": _np.stack([g["L1_mix_bproj"], g["L1_gnn_b"]])[None],
        "rw": halves(g["L0_ffn_router_w"].T),
        "gw": halves(g["L1_ffn_gate_w"]),
        "rrow": _np.broadcast_to(_np.concatenate([g["L0_ffn_router_b"], g["L1_ffn_gate_b"]]), (P, E0 + E1)),
        "valid": (_np.arange(NT * P) < N).astype(_np.float32).reshape(NT, P).T,
        "wg1": halves(g["L1_gnn_W"].T),
        "wqkv1": _np.concatenate([halves(g["L1_mix_Wq"].T), halves(g["L1_mix_Wkv"].T)], axis=2),
        "wproj": halves(g["L1_mix_Wproj"].T),
        "ew": ew,
        "w1": g["L1_ffn_w1"],
        "w2": g["L1_ffn_w2"],
        "b11": g["L1_ffn_b1"].reshape(E1 * MT, P).T,
        "b2": g["L1_ffn_b2"],
    }
    arrays, args = {}, {}
    for name, arr in a.items():
        arr = _np.ascontiguousarray(arr)
        arrays[name + "_dram"] = arr
        args[name] = nc.dram_tensor(name + "_dram", arr.shape, _mybir.dt.from_np(arr.dtype), kind="ExternalInput").ap()
    out = nc.dram_tensor("out_dram", (N, D), F32, kind="ExternalOutput").ap()
    build(nc, args, out)
    r = _run(nc, [arrays], core_ids=[0])
    return r.results[0]["out_dram"]
```
